# Optimizing a Trainium2 kernel written in Bass

```python
import numpy as np
import jax
import jax.numpy as jnp

def _softmax(x, axis=-1):
    return jax.nn.softmax(x, axis=axis)

def _gelu(x):
    return jax.nn.gelu(x, approximate=True)

def _silu(x):
    return jax.nn.silu(x)

def _sigmoid(x):
    return jax.nn.sigmoid(x)

def _layernorm(x, axis=-1, eps=1e-05):
    m = jnp.mean(x, axis=axis, keepdims=True)
    v = jnp.var(x, axis=axis, keepdims=True)
    return (x - m) / jnp.sqrt(v + eps)

def _scatter_add(tgt, idx, src, axis=0):
    return tgt.at[idx].add(src)

def _segment_sum(src, seg, n):
    return jax.ops.segment_sum(src, seg, n)
kernel_name = 'mk_decoder_preln_d2_seqx_r4_1bd807'

def setup_inputs(seed: int=0):
    np.random.seed(seed)
    _w = jnp.asarray

    def _rec_inputs():
        import jax
        import jax.numpy as jnp
        _rk = jax.random.key(seed)
        x = -0.0002928 + 1 * jax.random.normal(jax.random.fold_in(_rk, 1), (8, 256, 256), jnp.float32)
        _lenS = 256 - jax.random.randint(jax.random.fold_in(_rk, 7), (8,), 0, max(1, 256 // 4) + 1, jnp.int32)
        _lenS2 = 77 - jax.random.randint(jax.random.fold_in(_rk, 8), (8,), 0, max(1, 77 // 4) + 1, jnp.int32)
        _ctx_1024P = jax.random.normal(jax.random.fold_in(_rk, 11), (8, 16, 256), jnp.float32)
        _ctx_1024c = jax.random.dirichlet(jax.random.fold_in(_rk, 511), 0.3 * jnp.ones((16,), jnp.float32), (8, 77))
        _ctx_1024t = jnp.einsum('bsk,bkd->bsd', _ctx_1024c, _ctx_1024P)
        _ctx_1024t = _ctx_1024t * jax.lax.rsqrt(jnp.mean(jnp.square(_ctx_1024t)) + 1e-12) * 0.953939
        ctx_1024 = -1.39393e-06 + 0.999914 * (_ctx_1024t + 0.3 * jax.random.normal(jax.random.fold_in(_rk, 611), (8, 77, 256), jnp.float32))
        _validS = jnp.arange(256)[None, :] < _lenS[:, None]
        _validS2 = jnp.arange(77)[None, :] < _lenS2[:, None]
        _causal = jnp.tril(jnp.ones((256, 256), dtype=bool))
        mask_1x1xSxS2_fk1 = jnp.where(jnp.broadcast_to(_validS2[0:1, None, None, :], (1, 1, 256, 77)), 1.0, 0.0).astype(jnp.float32)
        return (x, ctx_1024, mask_1x1xSxS2_fk1)
    x, ctx_1024, mask_1x1xSxS2_fk1 = _rec_inputs()

    def _L0_attn_setup():
        import jax, jax.numpy as jnp
        import numpy as np
        EPS = 1e-06
        NUM_HEADS = 16

        def rms_norm(x, w):
            var = jnp.mean(jnp.square(x), axis=-1, keepdims=True)
            return x * jax.lax.rsqrt(var + EPS) * w
        key = jax.random.key(seed)
        ks = jax.random.split(key, 6)
        B, N, C = (8, 256, 256)
        return {'x': jax.random.normal(ks[0], (B, N, C), dtype=jnp.float32), 'w_qkv': jax.random.normal(ks[1], (3 * C, C), dtype=jnp.float32) * (1.0 / np.sqrt(C)), 'b_qkv': jax.random.normal(ks[2], (3 * C,), dtype=jnp.float32) * 0.02, 'qn_w': jnp.ones((C // NUM_HEADS,), dtype=jnp.float32), 'kn_w': jnp.ones((C // NUM_HEADS,), dtype=jnp.float32), 'w_proj': jax.random.normal(ks[3], (C, C), dtype=jnp.float32) * (1.0 / np.sqrt(C)), 'b_proj': jax.random.normal(ks[4], (C,), dtype=jnp.float32) * 0.02}
    _L0_attn_all = _L0_attn_setup()
    _L0_attn_in = {k: v for k, v in _L0_attn_all.items() if k in ('w_qkv', 'b_qkv', 'qn_w', 'kn_w', 'w_proj', 'b_proj')}
    del _L0_attn_all

    def _L0_xattn_setup():
        import jax, jax.numpy as jnp
        import numpy as np
        DIM = 256
        NUM_HEADS = 16
        HEAD_DIM = DIM // NUM_HEADS
        SCALE = HEAD_DIM ** (-0.5)
        EPS = 1e-05

        def layernorm(x, gamma, beta):
            mu = jnp.mean(x, axis=-1, keepdims=True)
            var = jnp.mean(jnp.square(x - mu), axis=-1, keepdims=True)
            return (x - mu) * jax.lax.rsqrt(var + EPS) * gamma + beta
        key = jax.random.key(seed)
        ks = jax.random.split(key, 12)
        B, Lq, Lk = (2, 512, 512)
        s = 0.02
        return {'q': jax.random.normal(ks[0], (B, Lq, DIM), jnp.float32), 'k': jax.random.normal(ks[1], (B, Lk, DIM), jnp.float32), 'v': jax.random.normal(ks[2], (B, Lk, DIM), jnp.float32), 'Wq': jax.random.normal(ks[3], (DIM, DIM), jnp.float32) * s, 'Wk': jax.random.normal(ks[4], (DIM, DIM), jnp.float32) * s, 'Wv': jax.random.normal(ks[5], (DIM, DIM), jnp.float32) * s, 'gq': jnp.ones((HEAD_DIM,), jnp.float32), 'bq': jnp.zeros((HEAD_DIM,), jnp.float32), 'gk': jnp.ones((HEAD_DIM,), jnp.float32), 'bk': jnp.zeros((HEAD_DIM,), jnp.float32), 'Wo': jax.random.normal(ks[6], (DIM, DIM), jnp.float32) * s, 'bo': jnp.zeros((DIM,), jnp.float32)}
    _L0_xattn_all = _L0_xattn_setup()
    _L0_xattn_in = {k: v for k, v in _L0_xattn_all.items() if k in ('Wq', 'Wk', 'Wv', 'gq', 'bq', 'gk', 'bk', 'Wo', 'bo')}
    del _L0_xattn_all

    def _L0_ffn_setup():
        import jax, jax.numpy as jnp
        import numpy as np
        TOP_K = 2
        key = jax.random.key(seed)
        ks = jax.random.split(key, 8)
        B, S, D = (2, 512, 256)
        N_r, N_s = (16, 2)
        u = jax.random.normal(ks[0], (B, S, D), dtype=jnp.float32)
        centroids = jax.random.normal(ks[1], (N_r, D), dtype=jnp.float32)
        expert_biases = jnp.zeros((N_r,), dtype=jnp.float32)
        Wr = jax.random.normal(ks[2], (N_r, D, D), dtype=jnp.float32) * (1.0 / np.sqrt(D))
        br = jax.random.normal(ks[3], (N_r, D), dtype=jnp.float32) * 0.01
        Ws = jax.random.normal(ks[4], (N_s, D, D), dtype=jnp.float32) * (1.0 / np.sqrt(D))
        bs = jax.random.normal(ks[5], (N_s, D), dtype=jnp.float32) * 0.01
        return {'u': u, 'centroids': centroids, 'expert_biases': expert_biases, 'Wr': Wr, 'br': br, 'Ws': Ws, 'bs': bs}
    _L0_ffn_all = _L0_ffn_setup()
    _L0_ffn_in = {k: v for k, v in _L0_ffn_all.items() if k in ('centroids', 'expert_biases', 'Wr', 'br', 'Ws', 'bs')}
    del _L0_ffn_all

    def _L1_attn_setup():
        import jax, jax.numpy as jnp
        import numpy as np
        HIDDEN = 256
        HEADS = 16
        HEAD_DIM = HIDDEN // HEADS
        B, S = (4, 512)
        key = jax.random.key(seed)
        ks = jax.random.split(key, 10)
        scale = 1.0 / np.sqrt(HIDDEN)

        def lin(k):
            return jax.random.uniform(k, (HIDDEN, HIDDEN), jnp.float32, -scale, scale)
        return {'x': jax.random.normal(ks[0], (B, S, HIDDEN), jnp.float32), 'Wq': lin(ks[1]), 'bq': jnp.zeros((HIDDEN,), jnp.float32), 'Wk': lin(ks[2]), 'bk': jnp.zeros((HIDDEN,), jnp.float32), 'Wv': lin(ks[3]), 'bv': jnp.zeros((HIDDEN,), jnp.float32), 'Wo': lin(ks[4]), 'bo': jnp.zeros((HIDDEN,), jnp.float32), 'head_mask': jnp.ones((HEADS,), jnp.float32)}
    _L1_attn_all = _L1_attn_setup()
    _L1_attn_in = {k: v for k, v in _L1_attn_all.items() if k in ('Wq', 'bq', 'Wk', 'bk', 'Wv', 'bv', 'Wo', 'bo', 'head_mask')}
    del _L1_attn_all

    def _L1_xattn_setup():
        import jax, jax.numpy as jnp
        import numpy as np
        D_MODEL = 256
        NUM_HEADS = 16
        DEPTH = D_MODEL // NUM_HEADS
        B, S = (2, 512)

        def _split_heads(x):
            b, s, _ = x.shape
            return x.reshape(b, s, NUM_HEADS, DEPTH).transpose(0, 2, 1, 3)
        key = jax.random.key(seed)
        ks = jax.random.split(key, 12)
        s = 0.02
        inp = {'v': jax.random.normal(ks[0], (B, S, D_MODEL), jnp.float32), 'k': jax.random.normal(ks[1], (B, S, D_MODEL), jnp.float32), 'q': jax.random.normal(ks[2], (B, S, D_MODEL), jnp.float32), 'mask': jnp.triu(jnp.ones((S, S), jnp.float32), k=1)[None, None, :, :], 'wq_w': jax.random.normal(ks[3], (D_MODEL, D_MODEL), jnp.float32) * s, 'wq_b': jnp.zeros((D_MODEL,), jnp.float32), 'wk_w': jax.random.normal(ks[4], (D_MODEL, D_MODEL), jnp.float32) * s, 'wk_b': jnp.zeros((D_MODEL,), jnp.float32), 'wv_w': jax.random.normal(ks[5], (D_MODEL, D_MODEL), jnp.float32) * s, 'wv_b': jnp.zeros((D_MODEL,), jnp.float32), 'dense_w': jax.random.normal(ks[6], (D_MODEL, D_MODEL), jnp.float32) * s, 'dense_b': jnp.zeros((D_MODEL,), jnp.float32)}
        return inp
    _L1_xattn_all = _L1_xattn_setup()
    _L1_xattn_in = {k: v for k, v in _L1_xattn_all.items() if k in ('wq_w', 'wq_b', 'wk_w', 'wk_b', 'wv_w', 'wv_b', 'dense_w', 'dense_b')}
    del _L1_xattn_all

    def _L1_ffn_setup():
        import jax, jax.numpy as jnp
        import numpy as np
        B, T, C, D = (2, 1024, 256, 128)
        E = 8
        MIN_E = 2
        EPS = 1e-12
        NEG = -1000000000.0

        def _xavier(key, shape, fan_in, fan_out):
            bound = (6.0 / (fan_in + fan_out)) ** 0.5
            return jax.random.uniform(key, shape, jnp.float32, -bound, bound)

        def _forward(hidden_states, sim_matrix, gates, q_proj, k_proj, v_proj, o_proj):
            b, t, c = hidden_states.shape
            x = hidden_states.reshape(b * t, c)
            xn = x / jnp.maximum(jnp.linalg.norm(x, axis=-1, keepdims=True), EPS)
            sn = sim_matrix / jnp.maximum(jnp.linalg.norm(sim_matrix, axis=0, keepdims=True), EPS)
            logits = xn @ sn - jax.nn.sigmoid(gates)
            gated = jax.nn.relu(logits)
            mask = (gated > 0).astype(logits.dtype)
            inactive = jnp.sum(mask, axis=1) == 0
            top_idx = jax.lax.top_k(logits, MIN_E)[1]
            n = mask.shape[0]
            fb = jnp.zeros_like(mask).at[jnp.arange(n)[:, None], top_idx].set(1.0)
            mask = jnp.where(inactive[:, None] & (fb > 0), 1.0, mask)
            masked_logits = jnp.where(mask > 0, gated, NEG)
            routing_weights = jax.nn.softmax(masked_logits, axis=-1)
            m = jax.lax.stop_gradient(mask)
            q = jnp.einsum('tc,ecd,te->td', x, q_proj, m)
            k = jnp.einsum('tc,ecd,te->td', x, k_proj, m)
            v = jnp.einsum('tc,ecd,te->td', x, v_proj, m)
            qh = q.reshape(b, t, D)
            kh = k.reshape(b, t, D)
            vh = v.reshape(b, t, D)
            scores = jnp.einsum('bqd,bkd->bqk', qh, kh) / jnp.sqrt(jnp.asarray(D, qh.dtype))
            causal = jnp.tril(jnp.ones((t, t), bool))
            scores = jnp.where(causal, scores, jnp.finfo(scores.dtype).min)
            attn = jax.nn.softmax(scores, axis=-1)
            attn_out = jnp.einsum('bqk,bkd->bqd', attn, vh).reshape(b * t, D)
            final = jnp.einsum('td,edc,te->tc', attn_out, o_proj, m * routing_weights)
            return final.reshape(b, t, c)
        key = jax.random.key(seed)
        k = jax.random.split(key, 6)
        hidden_states = jax.random.normal(k[0], (B, T, C), jnp.float32)
        sim_matrix = jax.random.normal(k[1], (C, E), jnp.float32)
        gates = jnp.zeros((E,), jnp.float32)
        q_proj = _xavier(k[2], (E, C, D), C, D)
        k_proj = _xavier(k[3], (E, C, D), C, D)
        v_proj = _xavier(k[4], (E, C, D), C, D)
        o_proj = _xavier(k[5], (E, D, C), D, C)
        return dict(hidden_states=hidden_states, sim_matrix=sim_matrix, gates=gates, q_proj=q_proj, k_proj=k_proj, v_proj=v_proj, o_proj=o_proj)
    _L1_ffn_all = _L1_ffn_setup()
    _L1_ffn_in = {k: v for k, v in _L1_ffn_all.items() if k in ('sim_matrix', 'gates', 'q_proj', 'k_proj', 'v_proj', 'o_proj')}
    del _L1_ffn_all
    return {'x': x, 'ctx_1024': ctx_1024, 'mask_1x1xSxS2_fk1': mask_1x1xSxS2_fk1, 'L0_attn_w_qkv': _L0_attn_in['w_qkv'], 'L0_attn_b_qkv': _L0_attn_in['b_qkv'], 'L0_attn_qn_w': _L0_attn_in['qn_w'], 'L0_attn_kn_w': _L0_attn_in['kn_w'], 'L0_attn_w_proj': _L0_attn_in['w_proj'], 'L0_attn_b_proj': _L0_attn_in['b_proj'], 'L0_xattn_Wq': _L0_xattn_in['Wq'], 'L0_xattn_Wk': _L0_xattn_in['Wk'], 'L0_xattn_Wv': _L0_xattn_in['Wv'], 'L0_xattn_gq': _L0_xattn_in['gq'], 'L0_xattn_bq': _L0_xattn_in['bq'], 'L0_xattn_gk': _L0_xattn_in['gk'], 'L0_xattn_bk': _L0_xattn_in['bk'], 'L0_xattn_Wo': _L0_xattn_in['Wo'], 'L0_xattn_bo': _L0_xattn_in['bo'], 'L0_ffn_centroids': _L0_ffn_in['centroids'], 'L0_ffn_expert_biases': _L0_ffn_in['expert_biases'], 'L0_ffn_Wr': _L0_ffn_in['Wr'], 'L0_ffn_br': _L0_ffn_in['br'], 'L0_ffn_Ws': _L0_ffn_in['Ws'], 'L0_ffn_bs': _L0_ffn_in['bs'], 'L1_attn_Wq': _L1_attn_in['Wq'], 'L1_attn_bq': _L1_attn_in['bq'], 'L1_attn_Wk': _L1_attn_in['Wk'], 'L1_attn_bk': _L1_attn_in['bk'], 'L1_attn_Wv': _L1_attn_in['Wv'], 'L1_attn_bv': _L1_attn_in['bv'], 'L1_attn_Wo': _L1_attn_in['Wo'], 'L1_attn_bo': _L1_attn_in['bo'], 'L1_attn_head_mask': _L1_attn_in['head_mask'], 'L1_xattn_wq_w': _L1_xattn_in['wq_w'], 'L1_xattn_wq_b': _L1_xattn_in['wq_b'], 'L1_xattn_wk_w': _L1_xattn_in['wk_w'], 'L1_xattn_wk_b': _L1_xattn_in['wk_b'], 'L1_xattn_wv_w': _L1_xattn_in['wv_w'], 'L1_xattn_wv_b': _L1_xattn_in['wv_b'], 'L1_xattn_dense_w': _L1_xattn_in['dense_w'], 'L1_xattn_dense_b': _L1_xattn_in['dense_b'], 'L1_ffn_sim_matrix': _L1_ffn_in['sim_matrix'], 'L1_ffn_gates': _L1_ffn_in['gates'], 'L1_ffn_q_proj': _L1_ffn_in['q_proj'], 'L1_ffn_k_proj': _L1_ffn_in['k_proj'], 'L1_ffn_v_proj': _L1_ffn_in['v_proj'], 'L1_ffn_o_proj': _L1_ffn_in['o_proj']}

def reference(x, ctx_1024, mask_1x1xSxS2_fk1, L0_attn_w_qkv, L0_attn_b_qkv, L0_attn_qn_w, L0_attn_kn_w, L0_attn_w_proj, L0_attn_b_proj, L0_xattn_Wq, L0_xattn_Wk, L0_xattn_Wv, L0_xattn_gq, L0_xattn_bq, L0_xattn_gk, L0_xattn_bk, L0_xattn_Wo, L0_xattn_bo, L0_ffn_centroids, L0_ffn_expert_biases, L0_ffn_Wr, L0_ffn_br, L0_ffn_Ws, L0_ffn_bs, L1_attn_Wq, L1_attn_bq, L1_attn_Wk, L1_attn_bk, L1_attn_Wv, L1_attn_bv, L1_attn_Wo, L1_attn_bo, L1_attn_head_mask, L1_xattn_wq_w, L1_xattn_wq_b, L1_xattn_wk_w, L1_xattn_wk_b, L1_xattn_wv_w, L1_xattn_wv_b, L1_xattn_dense_w, L1_xattn_dense_b, L1_ffn_sim_matrix, L1_ffn_gates, L1_ffn_q_proj, L1_ffn_k_proj, L1_ffn_v_proj, L1_ffn_o_proj):
    import jax
    import jax.numpy as jnp

    def _L0_attn_ref(x, w_qkv, b_qkv, qn_w, kn_w, w_proj, b_proj):
        import jax, jax.numpy as jnp
        import numpy as np
        EPS = 1e-06
        NUM_HEADS = 16

        def rms_norm(x, w):
            var = jnp.mean(jnp.square(x), axis=-1, keepdims=True)
            return x * jax.lax.rsqrt(var + EPS) * w
        B, N, C = x.shape
        H = NUM_HEADS
        D = C // H
        qkv = x @ w_qkv.T + b_qkv
        qkv = qkv.reshape(B, N, 3, H, D).transpose(2, 0, 3, 1, 4)
        q, k, v = (qkv[0], qkv[1], qkv[2])
        q = rms_norm(q, qn_w)
        k = rms_norm(k, kn_w)
        scale = 1.0 / np.sqrt(D).astype(np.float32)
        attn = jnp.einsum('bhld,bhsd->bhls', q, k) * scale
        attn = jax.nn.softmax(attn, axis=-1)
        out = jnp.einsum('bhls,bhsd->bhld', attn, v)
        out = out.transpose(0, 2, 1, 3).reshape(B, N, C)
        return out @ w_proj.T + b_proj

    def _L0_xattn_ref(q, k, v, Wq, Wk, Wv, gq, bq, gk, bk, Wo, bo):
        import jax, jax.numpy as jnp
        import numpy as np
        DIM = 256
        NUM_HEADS = 16
        HEAD_DIM = DIM // NUM_HEADS
        SCALE = HEAD_DIM ** (-0.5)
        EPS = 1e-05

        def layernorm(x, gamma, beta):
            mu = jnp.mean(x, axis=-1, keepdims=True)
            var = jnp.mean(jnp.square(x - mu), axis=-1, keepdims=True)
            return (x - mu) * jax.lax.rsqrt(var + EPS) * gamma + beta
        B, Lq, _ = q.shape
        Lk = k.shape[1]
        qh = (q @ Wq.T).reshape(B, Lq, NUM_HEADS, HEAD_DIM).transpose(0, 2, 1, 3)
        kh = (k @ Wk.T).reshape(B, Lk, NUM_HEADS, HEAD_DIM).transpose(0, 2, 1, 3)
        vh = (v @ Wv.T).reshape(B, Lk, NUM_HEADS, HEAD_DIM).transpose(0, 2, 1, 3)
        qh = layernorm(qh, gq, bq) * SCALE
        kh = layernorm(kh, gk, bk)
        attn = jax.nn.sigmoid(jnp.einsum('bhqd,bhkd->bhqk', qh, kh))
        x = jnp.einsum('bhqk,bhkd->bhqd', attn, vh)
        x = x.transpose(0, 2, 1, 3).reshape(B, Lq, DIM)
        return x @ Wo.T + bo

    def _L0_ffn_ref(u, centroids, expert_biases, Wr, br, Ws, bs):
        import jax, jax.numpy as jnp
        import numpy as np
        TOP_K = 2
        N_r = centroids.shape[0]
        N_s = Ws.shape[0]
        raw_scores = jnp.einsum('bsd,ed->bse', u, centroids)
        s = jax.nn.softmax(raw_scores + expert_biases, axis=-1)
        topk_vals, topk_idx = jax.lax.top_k(s, TOP_K)
        g_topk = jnp.sum(jax.nn.one_hot(topk_idx, N_r, dtype=s.dtype) * topk_vals[..., None], axis=-2)
        xe = jnp.einsum('bsd,eod->bseo', u, Wr) + br
        routed = jnp.einsum('bse,bseo->bso', g_topk, xe)
        shared = (jnp.einsum('bsd,eod->bso', u, Ws) + jnp.sum(bs, axis=0)) / N_s
        return u + routed + shared

    def _L1_attn_ref(x, Wq, bq, Wk, bk, Wv, bv, Wo, bo, head_mask):
        import jax, jax.numpy as jnp
        import numpy as np
        HIDDEN = 256
        HEADS = 16
        HEAD_DIM = HIDDEN // HEADS
        B, S = (4, 512)
        b, s, _ = x.shape
        q = (x @ Wq.T + bq).reshape(b, s, HEADS, HEAD_DIM)
        k = (x @ Wk.T + bk).reshape(b, s, HEADS, HEAD_DIM)
        v = (x @ Wv.T + bv).reshape(b, s, HEADS, HEAD_DIM)
        attn = jnp.einsum('bqhd,bkhd->bhqk', q, k) / np.sqrt(HEAD_DIM).astype(np.float32)
        attn = jax.nn.softmax(attn, axis=-1)
        attn = attn * head_mask[None, :, None, None]
        out = jnp.einsum('bhqk,bkhd->bqhd', attn, v).reshape(b, s, HIDDEN)
        return out @ Wo.T + bo

    def _L1_xattn_ref(v, k, q, mask, wq_w, wq_b, wk_w, wk_b, wv_w, wv_b, dense_w, dense_b):
        import jax, jax.numpy as jnp
        import numpy as np
        D_MODEL = 256
        NUM_HEADS = 16
        DEPTH = D_MODEL // NUM_HEADS
        B, S = (2, 512)

        def _split_heads(x):
            b, s, _ = x.shape
            return x.reshape(b, s, NUM_HEADS, DEPTH).transpose(0, 2, 1, 3)
        qh = _split_heads(q @ wq_w.T + wq_b)
        kh = _split_heads(k @ wk_w.T + wk_b)
        vh = _split_heads(v @ wv_w.T + wv_b)
        scores = jnp.einsum('bhqd,bhkd->bhqk', qh, kh) / np.sqrt(DEPTH).astype(np.float32)
        scores = scores + mask * -1000000000.0
        attn = jax.nn.softmax(scores, axis=-1)
        av = jnp.einsum('bhqk,bhkd->bhqd', attn, vh)
        concat = av.transpose(0, 2, 1, 3).reshape(q.shape[0], -1, D_MODEL)
        return concat @ dense_w.T + dense_b

    def _L1_ffn_ref(hidden_states, sim_matrix, gates, q_proj, k_proj, v_proj, o_proj):
        import jax, jax.numpy as jnp
        import numpy as np
        B, T, C, D = (2, 1024, 256, 128)
        E = 8
        MIN_E = 2
        EPS = 1e-12
        NEG = -1000000000.0

        def _xavier(key, shape, fan_in, fan_out):
            bound = (6.0 / (fan_in + fan_out)) ** 0.5
            return jax.random.uniform(key, shape, jnp.float32, -bound, bound)

        def _forward(hidden_states, sim_matrix, gates, q_proj, k_proj, v_proj, o_proj):
            b, t, c = hidden_states.shape
            x = hidden_states.reshape(b * t, c)
            xn = x / jnp.maximum(jnp.linalg.norm(x, axis=-1, keepdims=True), EPS)
            sn = sim_matrix / jnp.maximum(jnp.linalg.norm(sim_matrix, axis=0, keepdims=True), EPS)
            logits = xn @ sn - jax.nn.sigmoid(gates)
            gated = jax.nn.relu(logits)
            mask = (gated > 0).astype(logits.dtype)
            inactive = jnp.sum(mask, axis=1) == 0
            top_idx = jax.lax.top_k(logits, MIN_E)[1]
            n = mask.shape[0]
            fb = jnp.zeros_like(mask).at[jnp.arange(n)[:, None], top_idx].set(1.0)
            mask = jnp.where(inactive[:, None] & (fb > 0), 1.0, mask)
            masked_logits = jnp.where(mask > 0, gated, NEG)
            routing_weights = jax.nn.softmax(masked_logits, axis=-1)
            m = jax.lax.stop_gradient(mask)
            q = jnp.einsum('tc,ecd,te->td', x, q_proj, m)
            k = jnp.einsum('tc,ecd,te->td', x, k_proj, m)
            v = jnp.einsum('tc,ecd,te->td', x, v_proj, m)
            qh = q.reshape(b, t, D)
            kh = k.reshape(b, t, D)
            vh = v.reshape(b, t, D)
            scores = jnp.einsum('bqd,bkd->bqk', qh, kh) / jnp.sqrt(jnp.asarray(D, qh.dtype))
            causal = jnp.tril(jnp.ones((t, t), bool))
            scores = jnp.where(causal, scores, jnp.finfo(scores.dtype).min)
            attn = jax.nn.softmax(scores, axis=-1)
            attn_out = jnp.einsum('bqk,bkd->bqd', attn, vh).reshape(b * t, D)
            final = jnp.einsum('td,edc,te->tc', attn_out, o_proj, m * routing_weights)
            return final.reshape(b, t, c)
        return _forward(hidden_states, sim_matrix, gates, q_proj, k_proj, v_proj, o_proj)
    x = x + _L0_attn_ref(_layernorm(x, axis=-1), L0_attn_w_qkv, L0_attn_b_qkv, L0_attn_qn_w, L0_attn_kn_w, L0_attn_w_proj, L0_attn_b_proj)
    x = x + _L0_xattn_ref(_layernorm(x, axis=-1), ctx_1024, ctx_1024, L0_xattn_Wq, L0_xattn_Wk, L0_xattn_Wv, L0_xattn_gq, L0_xattn_bq, L0_xattn_gk, L0_xattn_bk, L0_xattn_Wo, L0_xattn_bo)
    x = x + _L0_ffn_ref(_layernorm(x, axis=-1), L0_ffn_centroids, L0_ffn_expert_biases, L0_ffn_Wr, L0_ffn_br, L0_ffn_Ws, L0_ffn_bs)
    x = x + _L1_attn_ref(_layernorm(x, axis=-1), L1_attn_Wq, L1_attn_bq, L1_attn_Wk, L1_attn_bk, L1_attn_Wv, L1_attn_bv, L1_attn_Wo, L1_attn_bo, L1_attn_head_mask)
    x = x + _L1_xattn_ref(ctx_1024, ctx_1024, _layernorm(x, axis=-1), mask_1x1xSxS2_fk1, L1_xattn_wq_w, L1_xattn_wq_b, L1_xattn_wk_w, L1_xattn_wk_b, L1_xattn_wv_w, L1_xattn_wv_b, L1_xattn_dense_w, L1_xattn_dense_b)
    x = x + _L1_ffn_ref(_layernorm(x, axis=-1), L1_ffn_sim_matrix, L1_ffn_gates, L1_ffn_q_proj, L1_ffn_k_proj, L1_ffn_v_proj, L1_ffn_o_proj)
    return x

_drawn_inputs = setup_inputs


def setup_inputs(seed=0):
    import zlib

    import numpy as np

    out = dict(_drawn_inputs(seed))
    spreads = {'L0_attn_qn_w': (1.0, 0.6),
     'L0_attn_kn_w': (1.0, 0.54),
     'L0_xattn_gq': (1.0, 0.2),
     'L0_xattn_bq': (0.0, 0.1),
     'L0_xattn_gk': (1.0, 0.2),
     'L0_xattn_bk': (0.0, 0.1),
     'L0_xattn_bo': (0.0, 0.1),
     'L0_ffn_expert_biases': (0.0, 0.8),
     'L1_attn_bq': (0.0, 0.8),
     'L1_attn_bk': (0.0, 2.0),
     'L1_attn_bv': (0.0, 0.269),
     'L1_attn_bo': (0.0, 0.1),
     'L1_xattn_wq_b': (0.0, 2.0),
     'L1_xattn_wk_b': (0.0, 2.0),
     'L1_xattn_wv_b': (0.0, 0.358),
     'L1_xattn_dense_b': (0.0, 0.1),
     'L1_ffn_gates': (0.0, 0.1)}
    factors = {'L0_ffn_br': 5.155,
     'L0_ffn_bs': 8.0,
     'L1_attn_Wq': 8.0,
     'L1_attn_Wk': 8.0,
     'L1_xattn_wq_w': 8.0,
     'L1_xattn_wk_w': 8.0,
     'L0_attn_b_proj': 2.803}
    for name, (base, spread) in spreads.items():
        noise = np.random.default_rng([zlib.crc32(name.encode()), seed]).standard_normal(out[name].shape)
        drawn = base * np.exp(spread * noise) if base else spread * noise
        out[name] = jnp.asarray(drawn.astype(out[name].dtype))
    for name, factor in factors.items():
        out[name] = (out[name] * factor).astype(out[name].dtype)
    return out
```

```python
import numpy as np
from contextlib import ExitStack, contextmanager

import concourse.bass as bass
from concourse import mybir

fp32 = mybir.dt.float32
bf16 = mybir.dt.bfloat16
ALU = mybir.AluOpType
ACT = mybir.ActivationFunctionType
AX = mybir.AxisListType

B, S, C = 8, 256, 256
SK = 77
H, DH = 16, 16
P = 128
T = B * S // P
PARTS = 6
LN_EPS = 1e-5
RMS_EPS = 1e-6
SCALE = DH ** -0.5
N_ROUTED = 16
N_ATTN = 8
TILES_OF = (slice(0, 1), slice(1, 3))
NORM_EPS = 1e-12
SK_PAD = 128
HEADS_OF = (slice(0, 2 * H), slice(2 * H, 3 * H))
LN_EXP_TABLES = "natural_log_exp_and_others"


class Signal:

    def __init__(self, sem, per_batch):
        self.sem = sem
        self.per_batch = per_batch

    def after(self, b, n):
        return b * self.per_batch + n


def wait_apart(engine):
    engine.nop(nofuse=True)


@contextmanager
def layer_block_of(nc, signals):
    with nc.Block() as block:
        yield block
    nc.clear_and_free_semaphores(signals)
    nc.all_engine_barrier()


def layer_block(ctx, nc, signals):
    return ctx.enter_context(layer_block_of(nc, signals))


def at(i, n=1):
    if isinstance(i, int):
        return slice(i, i + n)
    return bass.ds(i, n)


def self_attention(nc, shared, name, wqkv, bqkv, wo, qk_gain):
    x = shared.x
    with ExitStack() as ctx:
        def sb(n, shape, dt=fp32):
            return ctx.enter_context(nc.sbuf_tensor(f"{name}_{n}", shape, dt))

        def ps(n, shape, dt=fp32):
            return ctx.enter_context(nc.psum_tensor(f"{name}_{n}", shape, dt))

        signals = []

        def signal(n, per_batch):
            signals.append(nc.alloc_semaphore(f"{name}_{n}"))
            return Signal(signals[-1], per_batch)

        stats = sb("stats", [P, 2, 6])
        mean_var = sb("mean_var", [P, 2, 2])
        var_eps = sb("var_eps", [P, 2])
        rstd = sb("rstd", [P, 2])
        xn = sb("xn", [P, 2, C])
        xn_t = sb("xn_t", [P, 2, S])
        qk = sb("qk", [P, 2, 2 * H, DH])
        qk_sq = sb("qk_sq", [P, 2, 2 * H, DH])
        head_ms = sb("head_ms", [P, 4 * H])
        head_ln = sb("head_ln", [P, 4 * H])
        head_rs = sb("head_rs", [P, 4 * H])
        rest = sb("rest", [P, 2, 2 * H, DH])
        parts = [sb(f"parts_{n}", [P, 2 * H, PARTS, DH], bf16) for n in "qk"]
        stacks = [[sb(f"stack_{n}{u}", [P, H, S], bf16) for n in "qk"] for u in range(2)]
        v = [sb(f"v{u}", [P, 2, H, 2 * DH]) for u in range(2)]
        neg_max = sb("neg_max", [P, 2, H])
        neg_max_parts = sb("neg_max_parts", [P, 2, 2, H], bf16)
        neg_max_t = sb("neg_max_t", [2 * H, S], bf16)
        probs = sb("probs", [P, 4, 2, 2, S])
        den = sb("den", [P, 2, 2, S])
        log_den = sb("log_den", [P, 2, 2, S])
        attn = sb("attn", [P, 2, 2, S])

        max_bank = [ps(f"max_bank{n}", [P, 2, S]) for n in range(2)]
        prob_bank = [ps(f"prob_bank{n}", [P, 2, 2, S]) for n in range(2)]
        work_bank = [ps(f"work_bank{n}", [P, 2, S]) for n in range(2)]

        def stack_bank(n):
            return prob_bank[(n // 2 + 1) % 2][:, n % 2].rearrange("p a s -> p (a s)").bitcast(bf16)\
                .rearrange("p (h s) -> p h s", h=4)

        xn_bank = max_bank[0]
        v_bank = max_bank[1]
        neg_max_bank = max_bank[0][:, 0, 0:S // 2].bitcast(bf16)

        stats_done = signal("stats_done", 2)
        moments_done = signal("moments_done", 2)
        var_done = signal("var_done", 1)
        rstd_done = signal("rstd_done", 1)
        xn_done = signal("xn_done", 2)
        xn_t_in_psum = signal("xn_t_in_psum", 1)
        xn_t_done = signal("xn_t_done", 1)
        qk_in_psum = signal("qk_in_psum", 2)
        v_in_psum = signal("v_in_psum", 1)
        qk_done = signal("qk_done", 2)
        v_done = signal("v_done", 1)
        sq_done = signal("sq_done", 1)
        ms_done = signal("ms_done", 1)
        ln_ms_done = signal("ln_ms_done", 1)
        head_rs_done = signal("head_rs_done", 1)
        qk_scaled = signal("qk_scaled", 1)
        q_gained = signal("q_gained", 1)
        high_done = signal("high_done", 2)
        rest_done = signal("rest_done", 2)
        middle_done = signal("middle_done", 2)
        low_done = signal("low_done", 2)
        stack_in_psum = signal("stack_in_psum", 8)
        k_stack_done = signal("k_stack_done", 4)
        q_stack_done = signal("q_stack_done", 4)
        max_in_psum = signal("max_in_psum", H)
        max_done = signal("max_done", H)
        max_high_done = signal("max_high_done", 1)
        max_parts_done = signal("max_parts_done", 1)
        max_t_in_psum = signal("max_t_in_psum", 1)
        max_t_done = signal("max_t_done", 1)
        max_row_done = signal("max_row_done", 32)
        scores_in_psum = signal("scores_in_psum", H // 2)
        probs_done = signal("probs_done", H // 2)
        attn_in_psum = signal("attn_in_psum", 4)
        den_done = signal("den_done", 2)
        log_done = signal("log_done", 2)
        recip_done = signal("recip_done", 2)
        attn_done = signal("attn_done", 2)
        out_in_psum = signal("out_in_psum", 1)
        x_done = signal("x_done", 1)
        ones_done = signal("ones_done", 4)

        block = layer_block(ctx, nc, signals)

        @block.gpsimd
        def _(pool):
            for u in range(2):
                nc.gpsimd.memset(stacks[u][1][PARTS * DH:P], 1.0).then_inc(ones_done.sem, 1)
                pool.wait_ge(ones_done.sem, 2 * u + 1)
                nc.gpsimd.memset(v[u][:, :, :, DH:2 * DH], 1.0).then_inc(ones_done.sem, 1)
                pool.wait_ge(ones_done.sem, 2 * u + 2)

            def normalise(b):
                pool.wait_ge(moments_done.sem, moments_done.after(b, 2))
                wait_apart(pool)
                nc.gpsimd.tensor_scalar(var_eps[:, :], mean_var[:, :, 1], LN_EPS, None, ALU.add).then_inc(var_done.sem, 1)
                pool.wait_ge(var_done.sem, var_done.after(b, 1))
                nc.gpsimd.tensor_tensor(rstd[:, :], var_eps[:, :], shared.neg_half[:, 0:2], ALU.pow).then_inc(rstd_done.sem, 1)

            def split(b):
                for n in range(2):
                    pool.wait_ge(high_done.sem, high_done.after(b, n + 1))
                    high = parts[n][:, :, (0, 2)[n], :]
                    nc.gpsimd.tensor_tensor(rest[:, n], qk[:, n], high, ALU.subtract).then_inc(rest_done.sem, 1)
                for n in range(2):
                    pool.wait_ge(middle_done.sem, middle_done.after(b, n + 1))
                    nc.gpsimd.tensor_tensor(parts[n][:, :, (4, 1)[n], :], rest[:, n], parts[n][:, :, (3, 0)[n], :],
                                            ALU.subtract).then_inc(low_done.sem, 1)

            normalise(0)
            split(0)
            normalise(1)
            split(1)
            normalise(2)
            with pool.Fori(0, B - 3) as b:
                normalise(b + 3)
                split(b + 2)
            split(B - 1)

        @block.sync
        def _(sp):
            def max_row(b, u):
                sp.wait_ge(max_t_done.sem, max_t_done.after(b, 1))
                for part in range(2):
                    row = PARTS * DH + part
                    sp.dma_start(stacks[u][0][row:row + 1], neg_max_t[part * H:(part + 1) * H, :]).then_inc(max_row_done.sem, 16)

            with sp.Fori(0, B // 2) as pair:
                for u in range(2):
                    max_row(pair * 2 + u, u)
            sp.wait_ge(max_row_done.sem, max_row_done.after(B - 1, 32))

        @block.tensor
        def _(pe):
            def project(b):
                pe.wait_ge(xn_done.sem, xn_done.after(b, 2))
                for t in range(2):
                    for c in range(2):
                        last = nc.tensor.transpose(xn_bank[:, c, t * P:(t + 1) * P], xn[:, t, c * P:(c + 1) * P], shared.ident[:, :])
                last.then_inc(xn_t_in_psum.sem, 1)
                pe.wait_ge(xn_t_done.sem, xn_t_done.after(b, 1))
                for t in range(2):
                    for c in range(2):
                        last = nc.tensor.matmul(prob_bank[1][:, t].rearrange("p a s -> p (a s)"), xn_t[:, c, t * P:(t + 1) * P],
                                                wqkv[:, c, 0:2 * C], start=(c == 0), stop=(c == 1))
                    last.then_inc(qk_in_psum.sem, 1)

            def values(b):
                for t in range(2):
                    for c in range(2):
                        last = nc.tensor.matmul(v_bank[:, t, :], xn_t[:, c, t * P:(t + 1) * P],
                                                wqkv[:, c, 2 * C:3 * C], start=(c == 0), stop=(c == 1))
                last.then_inc(v_in_psum.sem, 1)

            def stack(b, u):
                for n in range(8):
                    which = 1 - n // 4
                    pe.wait_ge(low_done.sem, low_done.after(b, 2))
                    if n >= 4:
                        pe.wait_ge(k_stack_done.sem, k_stack_done.after(b, n - 3))
                    for h in range(4):
                        for t in range(2):
                            src = parts[which][:, t * H + 4 * (n % 4) + h].rearrange("p a d -> p (a d)")
                            last = nc.tensor.transpose(stack_bank(n)[0:PARTS * DH, h, t * P:(t + 1) * P], src, shared.ident_bf[:, :])
                    last.then_inc(stack_in_psum.sem, 1)

            def maxima(b, u, h):
                q, k = stacks[u]
                if h == 0:
                    pe.wait_ge(q_stack_done.sem, q_stack_done.after(b, 4))
                    pe.wait_ge(k_stack_done.sem, k_stack_done.after(b, 4))
                    pe.wait_ge(max_t_done.sem, max_t_done.after(b, 0))
                if h == 1:
                    pe.wait_ge(v_done.sem, v_done.after(b, 1))
                if h >= 2:
                    pe.wait_ge(max_done.sem, max_done.after(b, h - 1))
                for t in range(2):
                    last = nc.tensor.matmul(max_bank[h % 2][:, t, :], q[0:PARTS * DH, h, t * P:(t + 1) * P],
                                            k[0:PARTS * DH, h, :], start=True, stop=True)
                last.then_inc(max_in_psum.sem, 1)

            def max_transposed(b):
                pe.wait_ge(max_parts_done.sem, max_parts_done.after(b, 1))
                for t in range(2):
                    last = nc.tensor.transpose(neg_max_bank[0:2 * H, t * P:(t + 1) * P],
                                               neg_max_parts[:, t].rearrange("p a h -> p (a h)"), shared.ident_bf[:, :])
                last.then_inc(max_t_in_psum.sem, 1)

            def scores(b, u, p, left):
                q, k = stacks[u]
                if p == 0:
                    pe.wait_ge(max_row_done.sem, max_row_done.after(b, 32))
                    pe.wait_ge(q_stack_done.sem, q_stack_done.after(b, 4 * (1 + min(left, 1))))
                    pe.wait_ge(probs_done.sem, probs_done.after(b, 0))
                if p == 1:
                    pe.wait_ge(qk_done.sem, qk_done.after(b, 2 * (1 + min(left, 2))))
                if p >= 2:
                    pe.wait_ge(probs_done.sem, probs_done.after(b, p - 1))
                rows = PARTS * DH + 2
                for h in range(2):
                    for kt in range(2):
                        last = nc.tensor.matmul(prob_bank[p % 2][:, h, kt, :], k[0:rows, 2 * p + h, kt * P:(kt + 1) * P],
                                                q[0:rows, 2 * p + h, :], start=True, stop=True)
                last.then_inc(scores_in_psum.sem, 1)

            def weigh(b, u, g):
                if g % 2 == 0 and g == 0:
                    pe.wait_ge(v_done.sem, v_done.after(b, 1))
                pe.wait_ge(probs_done.sem, probs_done.after(b, 2 * g + 2))
                for kt in range(2):
                    for j in range(4):
                        h = 4 * g + j
                        last = nc.tensor.matmul(work_bank[g // 2][32 * j:32 * j + 32, g % 2, :], v[u][:, kt, h, :],
                                                probs[:, (h // 2) % 4, h % 2, kt, :], start=(kt == 0), stop=(kt == 1))
                last.then_inc(attn_in_psum.sem, 1)

            def output(b):
                pe.wait_ge(attn_done.sem, attn_done.after(b, 2))
                for t in range(2):
                    for g in range(4):
                        last = nc.tensor.matmul(work_bank[0][:, t, :], attn[:, g // 2, g % 2, t * P:(t + 1) * P], wo[:, g, :],
                                                start=(g == 0), stop=(g == 3))
                last.then_inc(out_in_psum.sem, 1)

            def main(b, u, left):
                for p in range(H // 2):
                    scores(b, u, p, left)
                    if left >= 1:
                        maxima(b + 1, 1 - u, 2 * p)
                        maxima(b + 1, 1 - u, 2 * p + 1)
                    if p == 2:
                        pe.wait_ge(x_done.sem, x_done.after(b, 0))
                    if p % 2 == 0 and p >= 2:
                        weigh(b, u, p // 2 - 1)
                weigh(b, u, 3)

            def batch(b, u, left=3):
                main(b, u, left)
                if left >= 1:
                    pe.wait_ge(max_done.sem, max_done.after(b + 1, H))
                if left >= 2:
                    pe.wait_ge(probs_done.sem, probs_done.after(b, H // 2))
                    values(b + 2)
                    stack(b + 2, u)
                if left >= 1:
                    max_transposed(b + 1)
                output(b)
                if left >= 3:
                    pe.wait_ge(max_t_done.sem, max_t_done.after(b + 1, 1))
                    pe.wait_ge(q_stack_done.sem, q_stack_done.after(b + 2, 2))
                    project(b + 3)

            pe.wait_ge(ones_done.sem, 4)
            for b in range(2):
                project(b)
                values(b)
                stack(b, b)
                pe.wait_ge(v_done.sem, v_done.after(b, 1))
                pe.wait_ge(q_stack_done.sem, q_stack_done.after(b, 4))
            project(2)
            for h in range(H):
                maxima(0, 0, h)
            pe.wait_ge(max_done.sem, max_done.after(0, H))
            max_transposed(0)
            with pe.Fori(0, (B - 4) // 2) as pair:
                for u in range(2):
                    batch(pair * 2 + u, u)
            for b in range(B - 4, B):
                batch(b, b % 2, min(3, B - 1 - b))

        @block.scalar
        def _(act):
            def xn_transposed(b):
                act.wait_ge(xn_t_in_psum.sem, xn_t_in_psum.after(b, 1))
                nc.scalar.activation(xn_t[:, :, :], xn_bank[:, :, :], ACT.Copy).then_inc(xn_t_done.sem, 1)

            def square(b):
                act.wait_ge(qk_done.sem, qk_done.after(b, 2))
                nc.scalar.activation(qk_sq[:, :], qk[:, :], ACT.Square).then_inc(sq_done.sem, 1)

            def head_rms(b):
                act.wait_ge(ms_done.sem, ms_done.after(b, 1))
                nc.scalar.activation(head_ln[:, :], head_ms[:, :], ACT.Ln, bias=shared.rms_eps[:, :], scale=1.0 / DH).then_inc(ln_ms_done.sem, 1)
                act.wait_ge(ln_ms_done.sem, ln_ms_done.after(b, 1))
                nc.scalar.activation(head_rs[:, :], head_ln[:, :], ACT.Exp, scale=-0.5).then_inc(head_rs_done.sem, 1)

            def high(b):
                if qk_gain is not None:
                    act.wait_ge(qk_scaled.sem, qk_scaled.after(b, 1))
                    act.wait_ge(q_gained.sem, q_gained.after(b, 1))
                else:
                    act.wait_ge(qk_done.sem, qk_done.after(b, 2))
                for n in range(2):
                    first = (0, 2)[n]
                    nc.scalar.activation(parts[n][:, :, first:first + 3, :], qk[:, n].unsqueeze(2).broadcast_to([P, 2 * H, 3, DH]),
                                         ACT.Copy).then_inc(high_done.sem, 1)

            def stack_k(b, u):
                for n in range(4):
                    act.wait_ge(stack_in_psum.sem, stack_in_psum.after(b, n + 1))
                    nc.scalar.activation(stacks[u][1][0:PARTS * DH, 4 * n:4 * n + 4, :], stack_bank(n)[0:PARTS * DH], ACT.Copy)\
                        .then_inc(k_stack_done.sem, 1)

            def max_transposed(b):
                act.wait_ge(max_t_in_psum.sem, max_t_in_psum.after(b, 1))
                nc.scalar.activation(neg_max_t[:, :], neg_max_bank[0:2 * H, :], ACT.Copy).then_inc(max_t_done.sem, 1)

            def reciprocal(b, pair):
                act.wait_ge(den_done.sem, den_done.after(b, pair + 1))
                nc.scalar.activation(log_den[:, pair], den[:, pair], ACT.Ln).then_inc(log_done.sem, 1)
                act.wait_ge(log_done.sem, log_done.after(b, pair + 1))
                nc.scalar.activation(den[:, pair], log_den[:, pair], ACT.Exp, scale=-1.0).then_inc(recip_done.sem, 1)

            def front(b, u):
                xn_transposed(b)
                if qk_gain is not None:
                    square(b)
                    head_rms(b)
                high(b)
                stack_k(b, u)

            def batch(b, u, left=3):
                if left >= 2 and qk_gain is not None:
                    square(b + 2)
                for p in range(H // 2):
                    act.wait_ge(scores_in_psum.sem, scores_in_psum.after(b, p + 1))
                    if p >= 4:
                        act.wait_ge(attn_in_psum.sem, attn_in_psum.after(b, p // 2 - 1))
                    nc.scalar.activation(probs[:, p % 4], prob_bank[p % 2][:, :], ACT.Exp, scale=SCALE).then_inc(probs_done.sem, 1)
                    if left >= 2 and p == 1 and qk_gain is not None:
                        head_rms(b + 2)
                    if left >= 2 and p == 3:
                        high(b + 2)
                    if p == 6:
                        reciprocal(b, 0)
                reciprocal(b, 1)
                if left >= 2:
                    stack_k(b + 2, u)
                if left >= 1:
                    max_transposed(b + 1)
                if left >= 3:
                    xn_transposed(b + 3)

            front(0, 0)
            front(1, 1)
            xn_transposed(2)
            max_transposed(0)
            with act.Fori(0, (B - 4) // 2) as pair:
                for u in range(2):
                    batch(pair * 2 + u, u)
            for b in range(B - 4, B):
                batch(b, b % 2, min(3, B - 1 - b))

        @block.vector
        def _(dve):
            def moments(b):
                for t in range(2):
                    nc.vector.bn_stats(stats[:, t], x[:, at(2 * b + t), :]).then_inc(stats_done.sem, 1)
                for t in range(2):
                    dve.wait_ge(stats_done.sem, stats_done.after(b, t + 1))
                    wait_apart(dve)
                    nc.vector.bn_aggr(mean_var[:, t], stats[:, t]).then_inc(moments_done.sem, 1)

            def normalise(b):
                dve.wait_ge(rstd_done.sem, rstd_done.after(b, 1))
                dve.wait_ge(moments_done.sem, moments_done.after(b, 2))
                dve.wait_ge(xn_t_in_psum.sem, xn_t_in_psum.after(b, 0))
                for t in range(2):
                    nc.vector.tensor_scalar(xn[:, t], x[:, at(2 * b + t), :], mean_var[:, t, 0:1], rstd[:, t:t + 1],
                                            ALU.subtract, ALU.mult).then_inc(xn_done.sem, 1)

            def projected(b):
                for t in range(2):
                    dve.wait_ge(qk_in_psum.sem, qk_in_psum.after(b, t + 1))
                    nc.vector.tensor_tensor(qk[:, :, t * H:(t + 1) * H, :],
                                            prob_bank[1][:, t].rearrange("p a (h d) -> p a h d", d=DH),
                                            bqkv[:, 0:2 * C].rearrange("p (a h d) -> p a h d", a=2, d=DH), ALU.add).then_inc(qk_done.sem, 1)

            def values(b, u):
                dve.wait_ge(v_in_psum.sem, v_in_psum.after(b, 1))
                bias = bqkv[:, 2 * C:3 * C].rearrange("p (h d) -> p h d", d=DH).unsqueeze(1).broadcast_to([P, 2, H, DH])
                nc.vector.tensor_tensor(v[u][:, :, :, 0:DH], v_bank[:, :, :].rearrange("p t (h d) -> p t h d", d=DH), bias, ALU.add)\
                    .then_inc(v_done.sem, 1)

            def head_ms_sum(b):
                dve.wait_ge(sq_done.sem, sq_done.after(b, 1))
                nc.vector.tensor_reduce(head_ms[:, :], qk_sq[:, :].rearrange("p a h d -> p (a h) d"), AX.X, ALU.add).then_inc(ms_done.sem, 1)

            def head_rms(b):
                dve.wait_ge(head_rs_done.sem, head_rs_done.after(b, 1))
                qk_all = qk[:, :].rearrange("p a h d -> p (a h) d")
                nc.vector.tensor_tensor(qk_all, qk_all, head_rs[:, :].unsqueeze(2).broadcast_to([P, 4 * H, DH]), ALU.mult)\
                    .then_inc(qk_scaled.sem, 1)
                dve.wait_ge(qk_scaled.sem, qk_scaled.after(b, 1))
                nc.vector.tensor_tensor(qk[:, 0], qk[:, 0], qk_gain[:, :].unsqueeze(1).broadcast_to([P, 2 * H, DH]), ALU.mult)\
                    .then_inc(q_gained.sem, 1)

            def middle(b):
                for n in range(2):
                    dve.wait_ge(rest_done.sem, rest_done.after(b, n + 1))
                    first, step = ((3, 2), (0, 5))[n]
                    nc.vector.tensor_copy(parts[n][:, :, first:6:step, :], rest[:, n].unsqueeze(2).broadcast_to([P, 2 * H, 2, DH]))\
                        .then_inc(middle_done.sem, 1)

            def stack_q(b, u):
                for n in range(4):
                    dve.wait_ge(stack_in_psum.sem, stack_in_psum.after(b, n + 5))
                    nc.vector.tensor_copy(stacks[u][0][0:PARTS * DH, 4 * n:4 * n + 4, :], stack_bank(4 + n)[0:PARTS * DH])\
                        .then_inc(q_stack_done.sem, 1)

            def maximum(b, h):
                dve.wait_ge(max_in_psum.sem, max_in_psum.after(b, h + 1))
                nc.vector.tensor_reduce(neg_max[:, :, h], max_bank[h % 2][:, :, :], AX.X, ALU.max, negate=True).then_inc(max_done.sem, 1)

            def max_parts(b):
                dve.wait_ge(max_done.sem, max_done.after(b, H))
                nc.vector.tensor_copy(neg_max_parts[:, :, 0, :], neg_max[:, :, :]).then_inc(max_high_done.sem, 1)
                dve.wait_ge(max_high_done.sem, max_high_done.after(b, 1))
                nc.vector.tensor_tensor(neg_max_parts[:, :, 1, :], neg_max[:, :, :], neg_max_parts[:, :, 0, :], ALU.subtract)\
                    .then_inc(max_parts_done.sem, 1)

            def denominator(b, pair):
                dve.wait_ge(attn_in_psum.sem, attn_in_psum.after(b, 2 * pair + 2))
                wait_apart(dve)
                nc.vector.stream_shuffle(den[:, pair], work_bank[pair][:, :, :], [DH] * 32).then_inc(den_done.sem, 1)

            def divide(b, pair):
                dve.wait_ge(recip_done.sem, recip_done.after(b, pair + 1))
                nc.vector.tensor_tensor(attn[:, pair], work_bank[pair][:, :, :], den[:, pair], ALU.mult).then_inc(attn_done.sem, 1)

            def residual(b):
                dve.wait_ge(out_in_psum.sem, out_in_psum.after(b, 1))
                xb = x[:, at(2 * b, 2), :]
                nc.vector.tensor_tensor(xb, work_bank[0][:, :, :], xb, ALU.add).then_inc(x_done.sem, 1)

            def front(b, u):
                moments(b)
                normalise(b)
                projected(b)
                values(b, u)
                if qk_gain is not None:
                    head_ms_sum(b)
                    head_rms(b)
                middle(b)
                stack_q(b, u)

            def batch(b, u, left=3):
                if left >= 3:
                    moments(b + 3)
                for p in range(H // 2):
                    if left >= 1:
                        maximum(b + 1, 2 * p)
                        maximum(b + 1, 2 * p + 1)
                    if left >= 2 and qk_gain is not None:
                        if p == 0:
                            head_ms_sum(b + 2)
                        if p == 2:
                            head_rms(b + 2)
                    if left >= 3 and p == 1:
                        normalise(b + 3)
                    if left >= 2 and p == 6:
                        middle(b + 2)
                    if p == 5:
                        denominator(b, 0)
                    if p == 7:
                        divide(b, 0)
                if left >= 1:
                    max_parts(b + 1)
                denominator(b, 1)
                if left >= 2:
                    values(b + 2, u)
                divide(b, 1)
                if left >= 2:
                    stack_q(b + 2, u)
                residual(b)
                if left >= 3:
                    projected(b + 3)

            front(0, 0)
            front(1, 1)
            moments(2)
            normalise(2)
            projected(2)
            for h in range(H):
                maximum(0, h)
            max_parts(0)
            with dve.Fori(0, (B - 4) // 2) as pair:
                for u in range(2):
                    batch(pair * 2 + u, u)
            for b in range(B - 4, B):
                batch(b, b % 2, min(3, B - 1 - b))


def cross_attention(nc, shared, name, ctx_dram, wq, wkv, wo, bqkv=None, mask=None, gain=None, offset=None):
    x = shared.x
    masked = mask is not None
    with ExitStack() as ctx:
        def sb(n, shape, dt=fp32):
            return ctx.enter_context(nc.sbuf_tensor(f"{name}_{n}", shape, dt))

        def ps(n, shape, dt=fp32):
            return ctx.enter_context(nc.psum_tensor(f"{name}_{n}", shape, dt))

        signals = []

        def signal(n, per_batch):
            signals.append(nc.alloc_semaphore(f"{name}_{n}"))
            return Signal(signals[-1], per_batch)

        stats = sb("stats", [P, 2, 6])
        mean_var = sb("mean_var", [P, 2, 2])
        var_eps = sb("var_eps", [P, 2])
        rstd = sb("rstd", [P, 2])
        xn = sb("xn", [P, 2, C])
        xn_t = sb("xn_t", [P, 2, S])
        ctx_t = [sb(f"ctx_t{u}", [P, 2, SK]) for u in range(2)]
        qk = sb("qk", [P, 3 * H, DH])
        qk_sq = sb("qk_sq", [P, 3 * H, DH])
        head_sum = sb("head_sum", [P, 3 * H])
        head_ss = sb("head_ss", [P, 3 * H])
        head_ln = sb("head_ln", [P, 3 * H])
        head_rs = sb("head_rs", [P, 3 * H])
        rest = sb("rest", [P, 3 * H, DH])
        parts = [sb("parts_q", [P, 2 * H, PARTS, DH], bf16), sb("parts_k", [P, H, PARTS, DH], bf16)]
        q_stack = sb("q_stack", [PARTS * DH, H, S], bf16)
        k_stack = sb("k_stack", [PARTS * DH, H, SK], bf16)
        v = [sb(f"v{u}", [SK, H, 2 * DH]) for u in range(2)]
        masked_scores = sb("masked_scores", [P, 2, H, SK])
        neg_max = sb("neg_max", [P, 2, H])
        shifted = sb("shifted", [P, 2, H, SK])
        exps = sb("exps", [P, 2, H, SK])
        probs = sb("probs", [SK, H, S])
        den = sb("den", [P, 2, 2, S])
        log_den = sb("log_den", [P, 2, 2, S])
        attn = sb("attn", [P, 2, 2, S])

        ring = [ps(f"ring{n}", [P, 2, 2 * S]) for n in range(2)]
        work_bank = [ps(f"work_bank{n}", [P, 2, S]) for n in range(2)]
        q_bank = ps("q_bank", [P, 2, S])
        kv_bank = ps("kv_bank", [P, 2 * C])

        loaded = [signal(f"ctx_loaded{u}", 16) for u in range(2)]
        zeros_done = signal("zeros_done", 4)
        stats_done = signal("stats_done", 2)
        moments_done = signal("moments_done", 2)
        var_done = signal("var_done", 1)
        rstd_done = signal("rstd_done", 1)
        xn_done = signal("xn_done", 2)
        xn_t_in_psum = signal("xn_t_in_psum", 1)
        xn_t_done = signal("xn_t_done", 1)
        kv_in_psum = signal("kv_in_psum", 1)
        q_in_psum = signal("q_in_psum", 1)
        qk_done = signal("qk_done", 2)
        v_done = signal("v_done", 1)
        sum_done = signal("sum_done", 1)
        centred = signal("centred", 1)
        sq_done = signal("sq_done", 1)
        ss_done = signal("ss_done", 1)
        ln_done = signal("ln_done", 1)
        head_rs_done = signal("head_rs_done", 1)
        scaled = signal("scaled", 1)
        gained = signal("gained", 1)
        normed = signal("normed", 1)
        high_done = signal("high_done", 2)
        rest_done = signal("rest_done", 2)
        middle_done = signal("middle_done", 2)
        low_done = signal("low_done", 2)
        k_stack_in_psum = signal("k_stack_in_psum", 1)
        q_stack_in_psum = signal("q_stack_in_psum", 2)
        k_stack_done = signal("k_stack_done", 1)
        q_low_stack_done = signal("q_low_stack_done", 1)
        q_high_stack_done = signal("q_high_stack_done", 1)
        scores_in_psum = signal("scores_in_psum", 4)
        masked_done = signal("masked_done", 4)
        max_done = signal("max_done", 4)
        shifted_done = signal("shifted_done", 4)
        exps_done = signal("exps_done", 4)
        probs_in_psum = signal("probs_in_psum", 4)
        probs_done = signal("probs_done", 4)
        attn_in_psum = signal("attn_in_psum", 4)
        den_done = signal("den_done", 2)
        log_done = signal("log_done", 2)
        recip_done = signal("recip_done", 2)
        attn_done = signal("attn_done", 2)
        out_in_psum = signal("out_in_psum", 1)
        x_done = signal("x_done", 1)

        qk_ready = qk_done if masked else normed
        n_qk_ready = 2 if masked else 1

        block = layer_block(ctx, nc, signals)

        @block.sync
        def _(sp):
            for u in range(2):
                sp.dma_start(ctx_t[u][:, :, :], ctx_dram[:, u]).then_inc(loaded[u].sem, 16)
            with sp.Fori(0, (B - 2) // 2) as pair:
                for u in range(2):
                    b = pair * 2 + u
                    sp.wait_ge(kv_in_psum.sem, kv_in_psum.after(b, 1))
                    sp.dma_start(ctx_t[u][:, :, :], ctx_dram[:, at(b + 2), :, :].rearrange("p o a s -> p (o a) s"))\
                        .then_inc(loaded[u].sem, 16)
            for u in range(2):
                sp.wait_ge(loaded[u].sem, 16 * B // 2)

        @block.gpsimd
        def _(pool):
            nc.gpsimd.memset(qk[:, 2 * H:3 * H, :], 0.0).then_inc(zeros_done.sem, 1)
            pool.wait_ge(zeros_done.sem, 1)
            for u in range(2):
                nc.gpsimd.memset(v[u][:, :, DH:2 * DH], 1.0 if masked else 0.0).then_inc(zeros_done.sem, 1)
                pool.wait_ge(zeros_done.sem, 2 + u)

            def normalise(b):
                pool.wait_ge(moments_done.sem, moments_done.after(b, 2))
                wait_apart(pool)
                nc.gpsimd.tensor_scalar(var_eps[:, :], mean_var[:, :, 1], LN_EPS, None, ALU.add).then_inc(var_done.sem, 1)
                pool.wait_ge(var_done.sem, var_done.after(b, 1))
                nc.gpsimd.tensor_tensor(rstd[:, :], var_eps[:, :], shared.neg_half[:, 0:2], ALU.pow).then_inc(rstd_done.sem, 1)

            def split(b):
                for n in range(2):
                    pool.wait_ge(high_done.sem, high_done.after(b, n + 1))
                    nc.gpsimd.tensor_tensor(rest[:, HEADS_OF[n]], qk[:, HEADS_OF[n]], parts[n][:, :, (0, 2)[n], :], ALU.subtract)\
                        .then_inc(rest_done.sem, 1)
                for n in range(2):
                    pool.wait_ge(middle_done.sem, middle_done.after(b, n + 1))
                    nc.gpsimd.tensor_tensor(parts[n][:, :, (4, 1)[n], :], rest[:, HEADS_OF[n]], parts[n][:, :, (3, 0)[n], :],
                                            ALU.subtract).then_inc(low_done.sem, 1)

            def shift(b):
                for n in range(4):
                    t, half = n % 2, n // 2
                    heads = slice(8 * half, 8 * half + 8)
                    pool.wait_ge(max_done.sem, max_done.after(b, n + 1))
                    nc.gpsimd.tensor_tensor(shifted[:, t, heads, :], masked_scores[:, t, heads, :],
                                            neg_max[:, t, heads].unsqueeze(2).broadcast_to([P, 8, SK]), ALU.add)\
                        .then_inc(shifted_done.sem, 1)

            def batch(b, left=2):
                if masked:
                    shift(b)
                if left >= 2:
                    normalise(b + 2)
                if left >= 1:
                    split(b + 1)

            normalise(0)
            split(0)
            normalise(1)
            with pool.Fori(0, B - 2) as b:
                batch(b)
            batch(B - 2, 1)
            batch(B - 1, 0)

        @block.tensor
        def _(pe):
            def project(b, u):
                pe.wait_ge(loaded[u].sem, 8 * (b - u) + 16)
                pe.wait_ge(v_done.sem, v_done.after(b, 0))
                pe.wait_ge(qk_done.sem, qk_done.after(b, 0))
                for c in range(2):
                    last = nc.tensor.matmul(kv_bank[0:SK, :], ctx_t[u][:, c, :], wkv[:, c, :], start=(c == 0), stop=(c == 1))
                last.then_inc(kv_in_psum.sem, 1)
                pe.wait_ge(xn_done.sem, xn_done.after(b, 2))
                for t in range(2):
                    for c in range(2):
                        last = nc.tensor.transpose(q_bank[:, c, t * P:(t + 1) * P], xn[:, t, c * P:(c + 1) * P], shared.ident[:, :])
                last.then_inc(xn_t_in_psum.sem, 1)
                pe.wait_ge(xn_t_done.sem, xn_t_done.after(b, 1))
                for t in range(2):
                    for c in range(2):
                        last = nc.tensor.matmul(q_bank[:, t, :], xn_t[:, c, t * P:(t + 1) * P], wq[:, c, :], start=(c == 0), stop=(c == 1))
                last.then_inc(q_in_psum.sem, 1)

            def stack(b):
                pe.wait_ge(low_done.sem, low_done.after(b, 2))
                out = ring[0][:, :, :].bitcast(bf16)
                for h in range(H):
                    last = nc.tensor.transpose(out[0:PARTS * DH, h // 8, SK_PAD * (h % 8):SK_PAD * (h % 8) + SK],
                                               parts[1][0:SK, h].rearrange("p a d -> p (a d)"), shared.ident_bf[0:SK, 0:SK])
                last.then_inc(k_stack_in_psum.sem, 1)
                for half in range(2):
                    if half == 1:
                        pe.wait_ge(k_stack_done.sem, k_stack_done.after(b, 1))
                    out = ring[1 - half][:, :, :].bitcast(bf16)
                    for h in range(8):
                        for t in range(2):
                            last = nc.tensor.transpose(out[0:PARTS * DH, h // 4, S * (h % 4) + t * P:S * (h % 4) + (t + 1) * P],
                                                       parts[0][:, t * H + 8 * half + h].rearrange("p a d -> p (a d)"), shared.ident_bf[:, :])
                    last.then_inc(q_stack_in_psum.sem, 1)

            def stacks_ready(b):
                pe.wait_ge(k_stack_done.sem, k_stack_done.after(b, 1))
                pe.wait_ge(q_low_stack_done.sem, q_low_stack_done.after(b, 1))
                pe.wait_ge(q_high_stack_done.sem, q_high_stack_done.after(b, 1))

            def sigmoid_scores(b):
                for n in range(4):
                    if n >= 2:
                        pe.wait_ge(probs_done.sem, probs_done.after(b, n - 1))
                    for h in range(4):
                        last = nc.tensor.matmul(ring[n % 2][0:SK, h // 2, S * (h % 2):S * (h % 2) + S], k_stack[:, 4 * n + h, :],
                                                q_stack[:, 4 * n + h, :], start=True, stop=True)
                    last.then_inc(scores_in_psum.sem, 1)

            def softmax_scores(b):
                pe.wait_ge(probs_done.sem, probs_done.after(b, 0))
                for n in range(4):
                    t, half = n % 2, n // 2
                    if n >= 2:
                        pe.wait_ge(masked_done.sem, masked_done.after(b, n - 1))
                    for h in range(8):
                        last = nc.tensor.matmul(ring[n % 2][:, h // 4, P * (h % 4):P * (h % 4) + SK],
                                                q_stack[:, 8 * half + h, t * P:(t + 1) * P], k_stack[:, 8 * half + h, :],
                                                start=True, stop=True)
                    last.then_inc(scores_in_psum.sem, 1)

            def transpose_probs(b, n):
                pe.wait_ge(exps_done.sem, exps_done.after(b, 2 * (n // 2) + 2))
                if n == 0:
                    pe.wait_ge(masked_done.sem, masked_done.after(b, 4))
                if n == 1:
                    pe.wait_ge(masked_done.sem, masked_done.after(b, 4))
                if n >= 2:
                    pe.wait_ge(probs_done.sem, probs_done.after(b, n - 1))
                for h in range(4):
                    for t in range(2):
                        last = nc.tensor.transpose(ring[1 - n % 2][0:SK, h // 2, S * (h % 2) + t * P:S * (h % 2) + (t + 1) * P],
                                                   exps[:, t, 4 * n + h, :], shared.ident[:, :])
                last.then_inc(probs_in_psum.sem, 1)

            def weigh(b, u, g):
                if g == 0:
                    pe.wait_ge(x_done.sem, x_done.after(b, 0))
                    pe.wait_ge(v_done.sem, v_done.after(b, 1))
                pe.wait_ge(probs_done.sem, probs_done.after(b, g + 1))
                for j in range(4):
                    last = nc.tensor.matmul(work_bank[g // 2][32 * j:32 * j + 32, g % 2, :], v[u][:, 4 * g + j, :],
                                            probs[:, 4 * g + j, :], start=True, stop=True)
                last.then_inc(attn_in_psum.sem, 1)

            def output(b):
                pe.wait_ge(attn_done.sem, attn_done.after(b, 2))
                for t in range(2):
                    for g in range(4):
                        last = nc.tensor.matmul(work_bank[0][:, t, :], attn[:, g // 2, g % 2, t * P:(t + 1) * P], wo[:, g, :],
                                                start=(g == 0), stop=(g == 3))
                last.then_inc(out_in_psum.sem, 1)

            def batch(b, u, left=2):
                stacks_ready(b)
                if masked:
                    softmax_scores(b)
                    for n in range(4):
                        transpose_probs(b, n)
                        if n >= 1:
                            weigh(b, u, n - 1)
                    weigh(b, u, 3)
                else:
                    sigmoid_scores(b)
                    for g in range(4):
                        weigh(b, u, g)
                if left >= 1:
                    pe.wait_ge(probs_done.sem, probs_done.after(b, 4))
                    stack(b + 1)
                if left >= 2:
                    project(b + 2, u)
                output(b)

            pe.wait_ge(zeros_done.sem, 3)
            project(0, 0)
            stack(0)
            project(1, 1)
            with pe.Fori(0, (B - 2) // 2) as pair:
                for u in range(2):
                    batch(pair * 2 + u, u)
            batch(B - 2, 0, 1)
            batch(B - 1, 1, 0)

        @block.scalar
        def _(act):
            def xn_transposed(b):
                act.wait_ge(xn_t_in_psum.sem, xn_t_in_psum.after(b, 1))
                nc.scalar.activation(xn_t[:, :, :], q_bank[:, :, :], ACT.Copy).then_inc(xn_t_done.sem, 1)

            def projected(b):
                act.wait_ge(q_in_psum.sem, q_in_psum.after(b, 1))
                nc.scalar.activation(qk[:, 0:2 * H, :], q_bank[:, :, :].rearrange("p t (h d) -> p (t h) d", d=DH), ACT.Copy)\
                    .then_inc(qk_done.sem, 1)
                act.wait_ge(kv_in_psum.sem, kv_in_psum.after(b, 1))
                act.wait_ge(v_done.sem, v_done.after(b, 1))
                nc.scalar.activation(qk[0:SK, 2 * H:3 * H, :], kv_bank[0:SK, 0:C].rearrange("p (h d) -> p h d", d=DH), ACT.Copy)\
                    .then_inc(qk_done.sem, 1)

            def head_norm(b):
                act.wait_ge(centred.sem, centred.after(b, 1))
                nc.scalar.activation(qk_sq[:, :, :], qk[:, :, :], ACT.Square).then_inc(sq_done.sem, 1)
                act.wait_ge(ss_done.sem, ss_done.after(b, 1))
                wait_apart(act)
                nc.scalar.preload_act_table_set(LN_EXP_TABLES)
                nc.scalar.activation(head_ln[:, :], head_ss[:, :], ACT.Ln, bias=shared.ln_eps[:, :], scale=1.0 / DH).then_inc(ln_done.sem, 1)
                act.wait_ge(ln_done.sem, ln_done.after(b, 1))
                nc.scalar.activation(head_rs[:, :], head_ln[:, :], ACT.Exp, scale=-0.5).then_inc(head_rs_done.sem, 1)

            def high(b):
                act.wait_ge(qk_ready.sem, qk_ready.after(b, n_qk_ready))
                for n in range(2):
                    first = (0, 2)[n]
                    heads = (2 * H, H)[n]
                    nc.scalar.activation(parts[n][:, :, first:first + 3, :], qk[:, HEADS_OF[n]].unsqueeze(2).broadcast_to([P, heads, 3, DH]),
                                         ACT.Copy).then_inc(high_done.sem, 1)

            def stack_k(b):
                act.wait_ge(k_stack_in_psum.sem, k_stack_in_psum.after(b, 1))
                src = ring[0][:, :, :].bitcast(bf16)[0:PARTS * DH].rearrange("p a (h s) -> p (a h) s", s=SK_PAD)
                nc.scalar.activation(k_stack[:, :, :], src[:, :, 0:SK], ACT.Copy).then_inc(k_stack_done.sem, 1)

            def stack_q(b):
                act.wait_ge(q_stack_in_psum.sem, q_stack_in_psum.after(b, 2))
                nc.scalar.activation(q_stack[:, 8:16, :], ring[0][:, :, :].bitcast(bf16)[0:PARTS * DH].rearrange("p a (h s) -> p (a h) s", s=S),
                                     ACT.Copy).then_inc(q_high_stack_done.sem, 1)

            def sigmoids(b):
                for n in range(4):
                    act.wait_ge(scores_in_psum.sem, scores_in_psum.after(b, n + 1))
                    nc.scalar.activation(probs[:, 4 * n:4 * n + 4, :], ring[n % 2][0:SK].rearrange("p a (h s) -> p (a h) s", s=S),
                                         ACT.Sigmoid, scale=SCALE).then_inc(probs_done.sem, 1)

            def copy_attn(b):
                for pair in range(2):
                    act.wait_ge(attn_in_psum.sem, attn_in_psum.after(b, 2 * pair + 2))
                    nc.scalar.activation(attn[:, pair], work_bank[pair][:, :, :], ACT.Identity, bias=shared.bias_row[:, :]).then_inc(attn_done.sem, 1)

            def exponentials(b, n):
                t, half = n % 2, n // 2
                heads = slice(8 * half, 8 * half + 8)
                act.wait_ge(shifted_done.sem, shifted_done.after(b, n + 1))
                nc.scalar.activation(exps[:, t, heads, :], shifted[:, t, heads, :], ACT.Exp).then_inc(exps_done.sem, 1)

            def copy_probs(b, n):
                act.wait_ge(probs_in_psum.sem, probs_in_psum.after(b, n + 1))
                nc.scalar.activation(probs[:, 4 * n:4 * n + 4, :], ring[1 - n % 2][0:SK].rearrange("p a (h s) -> p (a h) s", s=S),
                                     ACT.Copy).then_inc(probs_done.sem, 1)

            def reciprocal(b, pair):
                act.wait_ge(den_done.sem, den_done.after(b, pair + 1))
                nc.scalar.activation(log_den[:, pair], den[:, pair], ACT.Ln).then_inc(log_done.sem, 1)
                act.wait_ge(log_done.sem, log_done.after(b, pair + 1))
                nc.scalar.activation(den[:, pair], log_den[:, pair], ACT.Exp, scale=-1.0).then_inc(recip_done.sem, 1)

            def batch(b, left=2):
                if masked:
                    for n in range(4):
                        exponentials(b, n)
                    for n in range(4):
                        copy_probs(b, n)
                    if left >= 1:
                        high(b + 1)
                    for pair in range(2):
                        reciprocal(b, pair)
                else:
                    sigmoids(b)
                    if left >= 1:
                        head_norm(b + 1)
                    copy_attn(b)
                    if left >= 1:
                        high(b + 1)
                if left >= 1:
                    stack_k(b + 1)
                    stack_q(b + 1)
                if left >= 2:
                    xn_transposed(b + 2)
                    if not masked:
                        projected(b + 2)

            act.wait_ge(zeros_done.sem, 3)
            xn_transposed(0)
            if not masked:
                projected(0)
                head_norm(0)
            high(0)
            stack_k(0)
            stack_q(0)
            xn_transposed(1)
            if not masked:
                projected(1)
            with act.Fori(0, B - 2) as b:
                batch(b)
            batch(B - 2, 1)
            batch(B - 1, 0)

        @block.vector
        def _(dve):
            def moments(b):
                for t in range(2):
                    nc.vector.bn_stats(stats[:, t], x[:, at(2 * b + t), :]).then_inc(stats_done.sem, 1)
                for t in range(2):
                    dve.wait_ge(stats_done.sem, stats_done.after(b, t + 1))
                    wait_apart(dve)
                    nc.vector.bn_aggr(mean_var[:, t], stats[:, t]).then_inc(moments_done.sem, 1)

            def normalise(b):
                dve.wait_ge(rstd_done.sem, rstd_done.after(b, 1))
                dve.wait_ge(moments_done.sem, moments_done.after(b, 2))
                dve.wait_ge(xn_t_in_psum.sem, xn_t_in_psum.after(b, 0))
                for t in range(2):
                    nc.vector.tensor_scalar(xn[:, t], x[:, at(2 * b + t), :], mean_var[:, t, 0:1], rstd[:, t:t + 1],
                                            ALU.subtract, ALU.mult).then_inc(xn_done.sem, 1)

            def projected(b, u):
                dve.wait_ge(kv_in_psum.sem, kv_in_psum.after(b, 1))
                v_src = kv_bank[0:SK, C:2 * C].rearrange("p (h d) -> p h d", d=DH)
                if not masked:
                    nc.vector.tensor_copy(v[u][:, :, 0:DH], v_src).then_inc(v_done.sem, 1)
                    return
                nc.vector.tensor_tensor(v[u][:, :, 0:DH], v_src, bqkv[0:SK, 2 * C:3 * C].rearrange("p (h d) -> p h d", d=DH), ALU.add)\
                    .then_inc(v_done.sem, 1)
                nc.vector.tensor_tensor(qk[0:SK, 2 * H:3 * H, :], kv_bank[0:SK, 0:C].rearrange("p (h d) -> p h d", d=DH),
                                        bqkv[0:SK, C:2 * C].rearrange("p (h d) -> p h d", d=DH), ALU.add).then_inc(qk_done.sem, 1)
                dve.wait_ge(q_in_psum.sem, q_in_psum.after(b, 1))
                nc.vector.tensor_tensor(qk[:, 0:2 * H, :].rearrange("p (t h) d -> p t (h d)", t=2), q_bank[:, :, :],
                                        bqkv[:, 0:C].unsqueeze(1).broadcast_to([P, 2, C]), ALU.add).then_inc(qk_done.sem, 1)

            def centre(b):
                dve.wait_ge(qk_done.sem, qk_done.after(b, 2))
                nc.vector.tensor_reduce(head_sum[:, :], qk[:, :, :], AX.X, ALU.add).then_inc(sum_done.sem, 1)
                dve.wait_ge(sum_done.sem, sum_done.after(b, 1))
                nc.vector.scalar_tensor_tensor(qk[:, :, :], head_sum[:, :].unsqueeze(2).broadcast_to([P, 3 * H, DH]), -1.0 / DH,
                                               qk[:, :, :], ALU.mult, ALU.add).then_inc(centred.sem, 1)

            def sum_squares(b):
                dve.wait_ge(sq_done.sem, sq_done.after(b, 1))
                nc.vector.tensor_reduce(head_ss[:, :], qk_sq[:, :, :], AX.X, ALU.add).then_inc(ss_done.sem, 1)

            def head_norm(b):
                dve.wait_ge(head_rs_done.sem, head_rs_done.after(b, 1))
                nc.vector.tensor_tensor(qk[:, :, :], qk[:, :, :], head_rs[:, :].unsqueeze(2).broadcast_to([P, 3 * H, DH]), ALU.mult)\
                    .then_inc(scaled.sem, 1)
                qk_t = qk[:, :, :].rearrange("p (t h) d -> p t h d", t=3)
                for before, op, what, after in ((scaled, ALU.mult, gain, gained), (gained, ALU.add, offset, normed)):
                    dve.wait_ge(before.sem, before.after(b, 1))
                    nc.vector.tensor_tensor(qk_t, qk_t, what[:, :, :].unsqueeze(2).broadcast_to([P, 3, H, DH]), op).then_inc(after.sem, 1)

            def middle(b):
                for n in range(2):
                    dve.wait_ge(rest_done.sem, rest_done.after(b, n + 1))
                    first, step = ((3, 2), (0, 5))[n]
                    heads = (2 * H, H)[n]
                    nc.vector.tensor_copy(parts[n][:, :, first:6:step, :], rest[:, HEADS_OF[n]].unsqueeze(2).broadcast_to([P, heads, 2, DH]))\
                        .then_inc(middle_done.sem, 1)

            def stack_q(b):
                dve.wait_ge(q_stack_in_psum.sem, q_stack_in_psum.after(b, 1))
                nc.vector.tensor_copy(q_stack[:, 0:8, :], ring[1][:, :, :].bitcast(bf16)[0:PARTS * DH].rearrange("p a (h s) -> p (a h) s", s=S))\
                    .then_inc(q_low_stack_done.sem, 1)

            def mask_scores(b, n):
                t, half = n % 2, n // 2
                heads = slice(8 * half, 8 * half + 8)
                dve.wait_ge(scores_in_psum.sem, scores_in_psum.after(b, n + 1))
                src = ring[n % 2][:, :, :].rearrange("p a (h s) -> p (a h) s", s=P)[:, :, 0:SK]
                nc.vector.scalar_tensor_tensor(masked_scores[:, t, heads, :], src, SCALE, mask[:, t, :].unsqueeze(1).broadcast_to([P, 8, SK]),
                                               ALU.mult, ALU.add).then_inc(masked_done.sem, 1)
                dve.wait_ge(masked_done.sem, masked_done.after(b, n + 1))
                nc.vector.tensor_reduce(neg_max[:, t, heads], masked_scores[:, t, heads, :], AX.X, ALU.max, negate=True).then_inc(max_done.sem, 1)

            def divide(b, pair):
                dve.wait_ge(recip_done.sem, recip_done.after(b, pair + 1))
                nc.vector.tensor_tensor(attn[:, pair], work_bank[pair][:, :, :], den[:, pair], ALU.mult).then_inc(attn_done.sem, 1)

            def denominator(b, pair):
                dve.wait_ge(attn_in_psum.sem, attn_in_psum.after(b, 2 * pair + 2))
                wait_apart(dve)
                nc.vector.stream_shuffle(den[:, pair], work_bank[pair][:, :, :], [DH] * 32).then_inc(den_done.sem, 1)

            def residual(b):
                dve.wait_ge(out_in_psum.sem, out_in_psum.after(b, 1))
                xb = x[:, at(2 * b, 2), :]
                nc.vector.tensor_tensor(xb, work_bank[0][:, :, :], xb, ALU.add).then_inc(x_done.sem, 1)

            def batch(b, u, left=2):
                if masked:
                    for n in range(4):
                        mask_scores(b, n)
                    if left >= 2:
                        moments(b + 2)
                    if left >= 1:
                        middle(b + 1)
                    if left >= 2:
                        normalise(b + 2)
                    for pair in range(2):
                        denominator(b, pair)
                    for pair in range(2):
                        divide(b, pair)
                else:
                    if left >= 1:
                        centre(b + 1)
                    if left >= 2:
                        moments(b + 2)
                    if left >= 1:
                        sum_squares(b + 1)
                        head_norm(b + 1)
                    if left >= 2:
                        normalise(b + 2)
                    if left >= 1:
                        middle(b + 1)
                if left >= 1:
                    stack_q(b + 1)
                if left >= 2:
                    projected(b + 2, u)
                residual(b)

            dve.wait_ge(zeros_done.sem, 3)
            moments(0)
            normalise(0)
            projected(0, 0)
            if not masked:
                centre(0)
                sum_squares(0)
                head_norm(0)
            moments(1)
            middle(0)
            stack_q(0)
            normalise(1)
            projected(1, 1)
            with dve.Fori(0, (B - 2) // 2) as pair:
                for u in range(2):
                    batch(pair * 2 + u, u)
            batch(B - 2, 0, 1)
            batch(B - 1, 1, 0)


def shared_and_routed_experts(nc, shared, name, centroids, bias, wr, ws, wb):
    x = shared.x
    with ExitStack() as ctx:
        def sb(n, shape, dt=fp32):
            return ctx.enter_context(nc.sbuf_tensor(f"{name}_{n}", shape, dt))

        def ps(n, shape, dt=fp32):
            return ctx.enter_context(nc.psum_tensor(f"{name}_{n}", shape, dt))

        signals = []

        def signal(n, per_batch):
            signals.append(nc.alloc_semaphore(f"{name}_{n}"))
            return Signal(signals[-1], per_batch)

        stats = sb("stats", [P, 2, 6])
        mean_var = sb("mean_var", [P, 2, 2])
        var_eps = sb("var_eps", [P, 2])
        rstd = sb("rstd", [P, 2])
        un = [sb(f"un{u}", [P, 2, C]) for u in range(2)]
        u_t = [sb(f"u_t{u}", [P, 2, S]) for u in range(2)]
        logits = sb("logits", [P, 2, N_ROUTED])
        top_logits = sb("top_logits", [P, 2, 8])
        neg_top = sb("neg_top", [P, 2])
        exps = sb("exps", [P, 2, N_ROUTED])
        total = sb("total", [P, 2])
        recip = sb("recip", [P, 2])
        softmax = sb("softmax", [P, 2, N_ROUTED + 6])
        top = sb("top", [P, 2, 8])
        best_two = sb("best_two", [P, 2, 8])
        others = sb("others", [P, 2, N_ROUTED + 6])
        gates = [sb(f"gates{u}", [P, 2, 32]) for u in range(2)]
        gates_t = [sb(f"gates_t{u}", [32, S]) for u in range(2)]
        acc = sb("acc", [P, 2, C])

        expert_bank = [ps(f"expert_bank{n}", [P, 2, C]) for n in range(4)]
        u_t_bank = ps("u_t_bank", [P, 2, S])
        logits_bank = ps("logits_bank", [P, 2, N_ROUTED])
        gates_bank = ps("gates_bank", [32, S])
        shared_bank = ps("shared_bank", [P, 2, C])

        constants_done = signal("constants_done", 4)
        stats_done = signal("stats_done", 2)
        moments_done = signal("moments_done", 2)
        var_done = signal("var_done", 1)
        rstd_done = signal("rstd_done", 1)
        u_done = signal("u_done", 2)
        u_t_in_psum = signal("u_t_in_psum", 1)
        u_t_done = signal("u_t_done", 1)
        logits_in_psum = signal("logits_in_psum", 1)
        logits_done = signal("logits_done", 1)
        top_logits_done = signal("top_logits_done", 2)
        neg_top_done = signal("neg_top_done", 1)
        exps_done = signal("exps_done", 2)
        recip_done = signal("recip_done", 1)
        softmax_done = signal("softmax_done", 2)
        top_done = signal("top_done", 2)
        best_two_done = signal("best_two_done", 1)
        others_done = signal("others_done", 2)
        gates_done = signal("gates_done", 1)
        gates_t_in_psum = signal("gates_t_in_psum", 1)
        gates_t_done = signal("gates_t_done", 1)
        shared_in_psum = signal("shared_in_psum", 1)
        expert_in_psum = signal("expert_in_psum", N_ROUTED)
        acc_done = signal("acc_done", 2 * (N_ROUTED + 1))
        x_done = signal("x_done", 1)

        block = layer_block(ctx, nc, signals)

        @block.gpsimd
        def _(pool):
            nc.gpsimd.memset(softmax[:, :, N_ROUTED:], -1.0).then_inc(constants_done.sem, 1)
            pool.wait_ge(constants_done.sem, 1)
            nc.gpsimd.memset(best_two[:, :, 2:8], -1.0).then_inc(constants_done.sem, 1)
            for u in range(2):
                pool.wait_ge(constants_done.sem, 2 + 3 * u)
                nc.gpsimd.memset(gates[u][:, :, :], 0.0).then_inc(constants_done.sem, 1)
                pool.wait_ge(constants_done.sem, 3 + 3 * u)
                nc.gpsimd.memset(gates[u][:, :, N_ROUTED:N_ROUTED + 2], 0.5).then_inc(constants_done.sem, 1)
                pool.wait_ge(constants_done.sem, 4 + 3 * u)
                nc.gpsimd.memset(gates[u][:, :, N_ROUTED + 2:], 0.0).then_inc(constants_done.sem, 1)

            def normalise(b):
                pool.wait_ge(moments_done.sem, moments_done.after(b, 2))
                wait_apart(pool)
                nc.gpsimd.tensor_scalar(var_eps[:, :], mean_var[:, :, 1], LN_EPS, None, ALU.add).then_inc(var_done.sem, 1)
                pool.wait_ge(var_done.sem, var_done.after(b, 1))
                nc.gpsimd.tensor_tensor(rstd[:, :], var_eps[:, :], shared.neg_half[:, 0:2], ALU.pow).then_inc(rstd_done.sem, 1)

            with pool.Fori(0, B) as b:
                normalise(b)

        @block.tensor
        def _(pe):
            def route(b, u):
                pe.wait_ge(u_done.sem, u_done.after(b, 2))
                pe.wait_ge(logits_done.sem, logits_done.after(b, 0))
                for t in range(2):
                    for c in range(2):
                        last = nc.tensor.transpose(u_t_bank[:, c, t * P:(t + 1) * P], un[u][:, t, c * P:(c + 1) * P], shared.ident[:, :])
                last.then_inc(u_t_in_psum.sem, 1)
                pe.wait_ge(u_t_done.sem, u_t_done.after(b, 1))
                for t in range(2):
                    for c in range(2):
                        last = nc.tensor.matmul(logits_bank[:, t, :], u_t[u][:, c, t * P:(t + 1) * P], centroids[:, c, :],
                                                start=(c == 0), stop=(c == 1))
                last.then_inc(logits_in_psum.sem, 1)

            def transpose_gates(b, u):
                pe.wait_ge(gates_done.sem, gates_done.after(b, 1))
                for t in range(2):
                    last = nc.tensor.transpose(gates_bank[:, t * P:(t + 1) * P], gates[u][:, t, :], shared.ident[:, :])
                last.then_inc(gates_t_in_psum.sem, 1)

            def shared_experts(b, u):
                pe.wait_ge(gates_t_done.sem, gates_t_done.after(b, 1))
                pe.wait_ge(acc_done.sem, acc_done.after(b, 0))
                for t in range(2):
                    for c in range(2):
                        nc.tensor.matmul(shared_bank[:, t, :], u_t[u][:, c, t * P:(t + 1) * P], ws[:, c, :], start=(c == 0), stop=False)
                    last = nc.tensor.matmul(shared_bank[:, t, :], gates_t[u][0:N_ROUTED + 2, t * P:(t + 1) * P], wb[:, :],
                                            start=False, stop=True)
                last.then_inc(shared_in_psum.sem, 1)

            def experts(b, u, n):
                e, t = 2 * (n // 2), n % 2
                if n >= 4:
                    pe.wait_ge(acc_done.sem, acc_done.after(b, 2 + 2 * (n - 3)))
                for c in range(2):
                    last = nc.tensor.matmul(expert_bank[n % 4][:, :, :].rearrange("p a c -> p (a c)"), u_t[u][:, c, t * P:(t + 1) * P],
                                            wr[:, c, e:e + 2, :].rearrange("p a c -> p (a c)"), start=(c == 0), stop=(c == 1))
                last.then_inc(expert_in_psum.sem, 1)

            def batch(b, u, left=1):
                shared_experts(b, u)
                for n in range(N_ROUTED):
                    experts(b, u, n)
                    if left and n == 3:
                        route(b + 1, 1 - u)
                    if left and n == 12:
                        transpose_gates(b + 1, 1 - u)

            pe.wait_ge(constants_done.sem, 8)
            route(0, 0)
            transpose_gates(0, 0)
            with pe.Fori(0, (B - 2) // 2) as pair:
                for u in range(2):
                    batch(pair * 2 + u, u)
            batch(B - 2, 0)
            batch(B - 1, 1, 0)

        @block.scalar
        def _(act):
            def front(b, u):
                act.wait_ge(u_t_in_psum.sem, u_t_in_psum.after(b, 1))
                nc.scalar.activation(u_t[u][:, :, :], u_t_bank[:, :, :], ACT.Copy).then_inc(u_t_done.sem, 1)
                act.wait_ge(neg_top_done.sem, neg_top_done.after(b, 1))
                for t in range(2):
                    nc.scalar.activation(exps[:, t, :], logits[:, t, :], ACT.Exp, bias=neg_top[:, t:t + 1],
                                         accum_out=total[:, t:t + 1]).then_inc(exps_done.sem, 1)
                act.wait_ge(gates_t_in_psum.sem, gates_t_in_psum.after(b, 1))
                nc.scalar.activation(gates_t[u][:, :], gates_bank[:, :], ACT.Copy).then_inc(gates_t_done.sem, 1)

            with act.Fori(0, B // 2) as pair:
                for u in range(2):
                    front(pair * 2 + u, u)

        @block.vector
        def _(dve):
            def moments(b):
                for t in range(2):
                    nc.vector.bn_stats(stats[:, t], x[:, at(2 * b + t), :]).then_inc(stats_done.sem, 1)
                for t in range(2):
                    dve.wait_ge(stats_done.sem, stats_done.after(b, t + 1))
                    wait_apart(dve)
                    nc.vector.bn_aggr(mean_var[:, t], stats[:, t]).then_inc(moments_done.sem, 1)

            def normalise(b, u):
                dve.wait_ge(rstd_done.sem, rstd_done.after(b, 1))
                dve.wait_ge(moments_done.sem, moments_done.after(b, 2))
                for t in range(2):
                    nc.vector.tensor_scalar(un[u][:, t], x[:, at(2 * b + t), :], mean_var[:, t, 0:1], rstd[:, t:t + 1],
                                            ALU.subtract, ALU.mult).then_inc(u_done.sem, 1)

            def route(b):
                dve.wait_ge(logits_in_psum.sem, logits_in_psum.after(b, 1))
                nc.vector.tensor_tensor(logits[:, :, :], logits_bank[:, :, :], bias[:, :].unsqueeze(1).broadcast_to([P, 2, N_ROUTED]), ALU.add)\
                    .then_inc(logits_done.sem, 1)
                dve.wait_ge(logits_done.sem, logits_done.after(b, 1))
                nc.vector.tensor_reduce(neg_top[:, :], logits[:, :, :], AX.X, ALU.max, negate=True).then_inc(neg_top_done.sem, 1)

            def gate(b, u):
                dve.wait_ge(exps_done.sem, exps_done.after(b, 2))
                nc.vector.reciprocal(recip[:, :], total[:, :]).then_inc(recip_done.sem, 1)
                dve.wait_ge(recip_done.sem, recip_done.after(b, 1))
                for t in range(2):
                    nc.vector.tensor_scalar(softmax[:, t, 0:N_ROUTED], exps[:, t, :], recip[:, t:t + 1], None, ALU.mult)\
                        .then_inc(softmax_done.sem, 1)
                for t in range(2):
                    dve.wait_ge(softmax_done.sem, softmax_done.after(b, t + 1))
                    wait_apart(dve)
                    nc.vector.max(top[:, t, :], softmax[:, t, :]).then_inc(top_done.sem, 1)
                dve.wait_ge(top_done.sem, top_done.after(b, 2))
                nc.vector.tensor_copy(best_two[:, :, 0:2], top[:, :, 0:2]).then_inc(best_two_done.sem, 1)
                dve.wait_ge(best_two_done.sem, best_two_done.after(b, 1))
                wait_apart(dve)
                for t in range(2):
                    nc.vector.match_replace(others[:, t, :], best_two[:, t, :], softmax[:, t, :], 0.0).then_inc(others_done.sem, 1)
                dve.wait_ge(others_done.sem, others_done.after(b, 2))
                nc.vector.tensor_tensor(gates[u][:, :, 0:N_ROUTED], softmax[:, :, 0:N_ROUTED], others[:, :, 0:N_ROUTED], ALU.subtract)\
                    .then_inc(gates_done.sem, 1)

            def start_acc(b, u):
                dve.wait_ge(shared_in_psum.sem, shared_in_psum.after(b, 1))
                dve.wait_ge(x_done.sem, x_done.after(b, 0))
                for t in range(2):
                    nc.vector.tensor_tensor(acc[:, t, :], shared_bank[:, t, :], un[u][:, t, :], ALU.add).then_inc(acc_done.sem, 1)

            def add_experts(b, u, n):
                e, t = 2 * (n // 2), n % 2
                dve.wait_ge(expert_in_psum.sem, expert_in_psum.after(b, n + 1))
                for k in range(2):
                    sums = 2 + 2 * n + 1 if k else (t + 1 if n < 2 else 2 + 2 * (n - 1))
                    dve.wait_ge(acc_done.sem, acc_done.after(b, sums))
                    nc.vector.scalar_tensor_tensor(acc[:, t, :], expert_bank[n % 4][:, k, :], gates[u][:, t, e + k:e + k + 1],
                                                          acc[:, t, :], ALU.mult, ALU.add).then_inc(acc_done.sem, 1)

            def residual(b):
                dve.wait_ge(acc_done.sem, acc_done.after(b + 1, 0))
                xb = x[:, at(2 * b, 2), :]
                nc.vector.tensor_tensor(xb, xb, acc[:, :, :], ALU.add).then_inc(x_done.sem, 1)

            def batch(b, u, left=1):
                if left:
                    moments(b + 1)
                start_acc(b, u)
                if left:
                    normalise(b + 1, 1 - u)
                for n in range(N_ROUTED):
                    add_experts(b, u, n)
                    if left and n == 4:
                        route(b + 1)
                    if left and n == 7:
                        gate(b + 1, 1 - u)
                residual(b)

            dve.wait_ge(constants_done.sem, 8)
            moments(0)
            normalise(0, 0)
            route(0)
            gate(0, 0)
            with dve.Fori(0, (B - 2) // 2) as pair:
                for u in range(2):
                    batch(pair * 2 + u, u)
            batch(B - 2, 0)
            batch(B - 1, 1, 0)


def attention_of_experts(nc, shared, name, sim, gate, wq, wk, wv, wo, causal):
    x = shared.x
    with ExitStack() as ctx:
        def sb(n, shape, dt=fp32):
            return ctx.enter_context(nc.sbuf_tensor(f"{name}_{n}", shape, dt))

        def ps(n, shape, dt=fp32):
            return ctx.enter_context(nc.psum_tensor(f"{name}_{n}", shape, dt))

        signals = []

        def signal(n, per_batch):
            signals.append(nc.alloc_semaphore(f"{name}_{n}"))
            return Signal(signals[-1], per_batch)

        stats = sb("stats", [P, 2, 6])
        mean_var = sb("mean_var", [P, 2, 2])
        var_eps = sb("var_eps", [P, 2])
        rstd = sb("rstd", [P, 2])
        un = sb("un", [P, 2, C])
        un_sq = sb("un_sq", [P, 2, C])
        norm_sq = sb("norm_sq", [P, 2])
        norm_sq_eps = sb("norm_sq_eps", [P, 2])
        norm_recip = sb("norm_recip", [P, 2])
        u_t = sb("u_t", [P, 2, S])
        logits = sb("logits", [P, 2, N_ATTN + 6])
        active = sb("active", [P, 2, N_ATTN])
        n_active = sb("n_active", [P, 2])
        inactive = sb("inactive", [P, 2])
        top = sb("top", [P, 2, 8])
        best_two = sb("best_two", [P, 2, 8])
        others = sb("others", [P, 2, N_ATTN + 6])
        fallback = sb("fallback", [P, 2, N_ATTN])
        experts = sb("experts", [P, 2, N_ATTN])
        gated = sb("gated", [P, 2, N_ATTN])
        absent = sb("absent", [P, 2, N_ATTN])
        gated_used = sb("gated_used", [P, 2, N_ATTN])
        masked_logits = sb("masked_logits", [P, 2, N_ATTN])
        neg_top = sb("neg_top", [P, 2])
        route_exps = sb("route_exps", [P, 2, N_ATTN])
        route_total = sb("route_total", [P, 2])
        route_recip = sb("route_recip", [P, 2])
        route_softmax = sb("route_softmax", [P, 2, N_ATTN])
        weights = [sb(f"weights{u}", [P, 2, N_ATTN]) for u in range(2)]
        masked_u = sb("masked_u", [P, 4, 2, C])
        masked_u_t = sb("masked_u_t", [P, N_ATTN, 2, S])
        q_t = sb("q_t", [P, S])
        k_t = sb("k_t", [P, S])
        v = sb("v", [P, 2, P])
        scores = sb("scores", [P, 3, P])
        neg_max = sb("neg_max", [P, 2])
        exps = sb("exps", [P, 3, P])
        total = sb("total", [P, 2])
        recip = sb("recip", [P, 2])
        probs = sb("probs", [P, 3, P])
        probs_t = sb("probs_t", [P, 3, P])
        attn_t = sb("attn_t", [P, S])
        acc = sb("acc", [P, 2, C])

        qkv_bank = [ps(f"{n}_bank", [P, S]) for n in "qkv"]
        u_t_bank = [ps(f"u_t_bank{n}", [P, 2, S]) for n in range(2)]
        attn_bank = ps("attn_bank", [P, 3, P])
        out_bank = [ps(f"out_bank{n}", [P, 2, C]) for n in range(2)]
        logits_bank = attn_bank

        sentinels_done = signal("sentinels_done", 2)
        stats_done = signal("stats_done", 2)
        moments_done = signal("moments_done", 2)
        var_done = signal("var_done", 1)
        rstd_done = signal("rstd_done", 1)
        u_done = signal("u_done", 2)
        sq_done = signal("sq_done", 2)
        norm_eps_done = signal("norm_eps_done", 1)
        norm_done = signal("norm_done", 1)
        transposed_in_psum = signal("transposed_in_psum", 1 + N_ATTN)
        transposed_done = signal("transposed_done", 1 + N_ATTN)
        logits_in_psum = signal("logits_in_psum", 1)
        logits_done = signal("logits_done", 2)
        active_done = signal("active_done", 1)
        n_active_done = signal("n_active_done", 1)
        inactive_done = signal("inactive_done", 1)
        top_done = signal("top_done", 2)
        best_two_done = signal("best_two_done", 1)
        others_done = signal("others_done", 2)
        fallback_done = signal("fallback_done", 1)
        experts_done = signal("experts_done", 2)
        gated_done = signal("gated_done", 1)
        absent_done = signal("absent_done", 1)
        gated_used_done = signal("gated_used_done", 1)
        masked_logits_done = signal("masked_logits_done", 1)
        neg_top_done = signal("neg_top_done", 1)
        route_exps_done = signal("route_exps_done", 2)
        route_recip_done = signal("route_recip_done", 1)
        route_softmax_done = signal("route_softmax_done", 2)
        weights_done = signal("weights_done", 1)
        masked_u_done = signal("masked_u_done", 2 * N_ATTN)
        q_in_psum = signal("q_in_psum", 1)
        k_in_psum = signal("k_in_psum", 1)
        v_in_psum = signal("v_in_psum", 1)
        q_done = signal("q_done", 1)
        k_done = signal("k_done", 1)
        v_done = signal("v_done", 1)
        scores_in_psum = signal("scores_in_psum", 1)
        scores_done = signal("scores_done", 1)
        max_done = signal("max_done", 2)
        exps_done = signal("exps_done", 2)
        recip_done = signal("recip_done", 1)
        probs_done = signal("probs_done", 2)
        probs_t_in_psum = signal("probs_t_in_psum", 1)
        probs_t_done = signal("probs_t_done", 1)
        attn_in_psum = signal("attn_in_psum", 1)
        attn_done = signal("attn_done", 1)
        out_in_psum = signal("out_in_psum", N_ATTN)
        acc_done = signal("acc_done", 2 * N_ATTN)

        block = layer_block(ctx, nc, signals)

        @block.gpsimd
        def _(pool):
            nc.gpsimd.memset(logits[:, :, N_ATTN:], -4.0).then_inc(sentinels_done.sem, 1)
            pool.wait_ge(sentinels_done.sem, 1)
            nc.gpsimd.memset(best_two[:, :, 2:8], -4.0).then_inc(sentinels_done.sem, 1)

            def normalise(b):
                pool.wait_ge(moments_done.sem, moments_done.after(b, 2))
                wait_apart(pool)
                nc.gpsimd.tensor_scalar(var_eps[:, :], mean_var[:, :, 1], LN_EPS, None, ALU.add).then_inc(var_done.sem, 1)
                pool.wait_ge(var_done.sem, var_done.after(b, 1))
                nc.gpsimd.tensor_tensor(rstd[:, :], var_eps[:, :], shared.neg_half[:, 0:2], ALU.pow).then_inc(rstd_done.sem, 1)

            def token_norms(b):
                pool.wait_ge(sq_done.sem, sq_done.after(b, 2))
                wait_apart(pool)
                nc.gpsimd.tensor_scalar(norm_sq_eps[:, :], norm_sq[:, :], NORM_EPS ** 2, None, ALU.max).then_inc(norm_eps_done.sem, 1)
                pool.wait_ge(norm_eps_done.sem, norm_eps_done.after(b, 1))
                nc.gpsimd.tensor_tensor(norm_recip[:, :], norm_sq_eps[:, :], shared.neg_half[:, 0:2], ALU.pow).then_inc(norm_done.sem, 1)

            with pool.Fori(0, B) as b:
                normalise(b)
                token_norms(b)

        @block.tensor
        def _(pe):
            def route(b):
                pe.wait_ge(u_done.sem, u_done.after(b, 2))
                for t in range(2):
                    for c in range(2):
                        last = nc.tensor.transpose(u_t_bank[0][:, c, t * P:(t + 1) * P], un[:, t, c * P:(c + 1) * P], shared.ident[:, :])
                last.then_inc(transposed_in_psum.sem, 1)
                pe.wait_ge(transposed_done.sem, transposed_done.after(b, 1))
                pe.wait_ge(attn_done.sem, attn_done.after(b, 0))
                for t in range(2):
                    for c in range(2):
                        last = nc.tensor.matmul(logits_bank[:, t, 0:N_ATTN], u_t[:, c, t * P:(t + 1) * P], sim[:, c, :],
                                                start=(c == 0), stop=(c == 1))
                last.then_inc(logits_in_psum.sem, 1)

            def transpose_masked(b, e):
                pe.wait_ge(masked_u_done.sem, masked_u_done.after(b, 2 * e + 2))
                if e >= 1:
                    pe.wait_ge(transposed_done.sem, transposed_done.after(b, e))
                for t in range(2):
                    for c in range(2):
                        last = nc.tensor.transpose(u_t_bank[(e + 1) % 2][:, c, t * P:(t + 1) * P],
                                                   masked_u[:, e % 4, t, c * P:(c + 1) * P], shared.ident[:, :])
                last.then_inc(transposed_in_psum.sem, 1)

            def project(b):
                pe.wait_ge(transposed_done.sem, transposed_done.after(b, 1 + N_ATTN))
                for bank, w, in_psum, done in ((qkv_bank[0], wq, q_in_psum, q_done), (qkv_bank[1], wk, k_in_psum, k_done)):
                    pe.wait_ge(done.sem, done.after(b, 0))
                    for e in range(N_ATTN):
                        for c in range(2):
                            last = nc.tensor.matmul(bank[:, :], w[:, c, e, :], masked_u_t[:, e, c, :],
                                                    start=(e == 0 and c == 0), stop=(e == N_ATTN - 1 and c == 1))
                    last.then_inc(in_psum.sem, 1)
                pe.wait_ge(v_done.sem, v_done.after(b, 0))
                for t in range(2):
                    for e in range(N_ATTN):
                        for c in range(2):
                            last = nc.tensor.matmul(qkv_bank[2][:, t * P:(t + 1) * P], masked_u_t[:, e, c, t * P:(t + 1) * P], wv[:, c, e, :],
                                                    start=(e == 0 and c == 0), stop=(e == N_ATTN - 1 and c == 1))
                last.then_inc(v_in_psum.sem, 1)

            def attend(b):
                pe.wait_ge(q_done.sem, q_done.after(b, 1))
                pe.wait_ge(k_done.sem, k_done.after(b, 1))
                pe.wait_ge(logits_done.sem, logits_done.after(b, 2))
                nc.tensor.matmul(attn_bank[:, 0, :], q_t[:, 0:P], k_t[:, 0:P], start=True, stop=True)
                nc.tensor.matmul(attn_bank[:, 1:3, :].rearrange("p a k -> p (a k)"), q_t[:, P:S], k_t[:, :],
                                 start=True, stop=True).then_inc(scores_in_psum.sem, 1)

            def transpose_probs(b):
                pe.wait_ge(probs_done.sem, probs_done.after(b, 2))
                for n, (q_tile, k_tile) in enumerate(((0, 0), (1, 0), (1, 1))):
                    last = nc.tensor.transpose(attn_bank[:, n, :], probs[:, n, :], shared.ident[:, :])
                last.then_inc(probs_t_in_psum.sem, 1)

            def weigh(b):
                pe.wait_ge(probs_t_done.sem, probs_t_done.after(b, 1))
                pe.wait_ge(v_done.sem, v_done.after(b, 1))
                out = attn_bank[:, 0:2, :].rearrange("p a k -> p (a k)")
                nc.tensor.matmul(out, v[:, 0, :], probs_t[:, 0:2, :].rearrange("p a k -> p (a k)"), start=True, stop=False)
                nc.tensor.matmul(out[:, P:S], v[:, 1, :], probs_t[:, 2, :], start=False, stop=True).then_inc(attn_in_psum.sem, 1)

            def output(b, n):
                e, t = 2 * (n // 2), n % 2
                if n == 0:
                    pe.wait_ge(attn_done.sem, attn_done.after(b, 1))
                if n < 2:
                    pe.wait_ge(acc_done.sem, acc_done.after(b, 0))
                else:
                    pe.wait_ge(acc_done.sem, acc_done.after(b, 2 * (n - 1)))
                nc.tensor.matmul(out_bank[n % 2][:, :, :].rearrange("p a c -> p (a c)"), attn_t[:, t * P:(t + 1) * P],
                                 wo[:, e:e + 2, :].rearrange("p a c -> p (a c)"), start=True, stop=True).then_inc(out_in_psum.sem, 1)

            def batch(b, last=False):
                project(b)
                attend(b)
                transpose_probs(b)
                weigh(b)
                if not last:
                    route(b + 1)
                for n in range(N_ATTN):
                    output(b, n)
                if not last:
                    for e in range(N_ATTN):
                        transpose_masked(b + 1, e)

            pe.wait_ge(sentinels_done.sem, 2)
            route(0)
            for e in range(N_ATTN):
                transpose_masked(0, e)
            with pe.Fori(0, B - 1) as b:
                batch(b)
            batch(B - 1, last=True)

        @block.scalar
        def _(act):
            def square(b):
                for t in range(2):
                    act.wait_ge(u_done.sem, u_done.after(b, t + 1))
                    nc.scalar.activation(un_sq[:, t, :], un[:, t, :], ACT.Square, accum_out=norm_sq[:, t:t + 1]).then_inc(sq_done.sem, 1)

            def copy_transposed(b, n):
                act.wait_ge(transposed_in_psum.sem, transposed_in_psum.after(b, n + 1))
                dst = u_t[:, :, :] if n == 0 else masked_u_t[:, n - 1, :, :]
                nc.scalar.activation(dst, u_t_bank[n % 2][:, :, :], ACT.Copy).then_inc(transposed_done.sem, 1)

            def route_softmax_exps(b):
                act.wait_ge(neg_top_done.sem, neg_top_done.after(b, 1))
                for t in range(2):
                    nc.scalar.activation(route_exps[:, t, :], masked_logits[:, t, :], ACT.Exp, bias=neg_top[:, t:t + 1],
                                         accum_out=route_total[:, t:t + 1]).then_inc(route_exps_done.sem, 1)

            def exponentials(b):
                for t, tiles in enumerate(TILES_OF):
                    act.wait_ge(max_done.sem, max_done.after(b, t + 1))
                    nc.scalar.activation(exps[:, tiles, :], scores[:, tiles, :], ACT.Exp, bias=neg_max[:, t:t + 1],
                                         accum_out=total[:, t:t + 1]).then_inc(exps_done.sem, 1)

            def copies(b):
                act.wait_ge(q_in_psum.sem, q_in_psum.after(b, 1))
                nc.scalar.activation(q_t[:, :], qkv_bank[0][:, :], ACT.Copy).then_inc(q_done.sem, 1)
                act.wait_ge(k_in_psum.sem, k_in_psum.after(b, 1))
                nc.scalar.activation(k_t[:, :], qkv_bank[1][:, :], ACT.Copy).then_inc(k_done.sem, 1)
                act.wait_ge(v_in_psum.sem, v_in_psum.after(b, 1))
                nc.scalar.activation(v[:, :, :], qkv_bank[2][:, :].rearrange("p (t c) -> p t c", t=2), ACT.Copy).then_inc(v_done.sem, 1)
                exponentials(b)
                act.wait_ge(probs_t_in_psum.sem, probs_t_in_psum.after(b, 1))
                nc.scalar.activation(probs_t[:, :, :], attn_bank[:, :, :], ACT.Copy).then_inc(probs_t_done.sem, 1)
                act.wait_ge(attn_in_psum.sem, attn_in_psum.after(b, 1))
                nc.scalar.activation(attn_t[:, :].rearrange("p (a k) -> p a k", a=2), attn_bank[:, 0:2, :], ACT.Copy).then_inc(attn_done.sem, 1)

            def front(b):
                copy_transposed(b, 0)
                route_softmax_exps(b)
                for n in range(1, N_ATTN + 1):
                    copy_transposed(b, n)

            square(0)
            front(0)
            with act.Fori(0, B - 1) as b:
                square(b + 1)
                copies(b)
                front(b + 1)
            copies(B - 1)

        @block.vector
        def _(dve):
            def moments(b):
                for t in range(2):
                    nc.vector.bn_stats(stats[:, t], x[:, at(2 * b + t), :]).then_inc(stats_done.sem, 1)
                for t in range(2):
                    dve.wait_ge(stats_done.sem, stats_done.after(b, t + 1))
                    wait_apart(dve)
                    nc.vector.bn_aggr(mean_var[:, t], stats[:, t]).then_inc(moments_done.sem, 1)

            def normalise(b):
                dve.wait_ge(rstd_done.sem, rstd_done.after(b, 1))
                dve.wait_ge(moments_done.sem, moments_done.after(b, 2))
                dve.wait_ge(masked_u_done.sem, masked_u_done.after(b, 0))
                for t in range(2):
                    nc.vector.tensor_scalar(un[:, t], x[:, at(2 * b + t), :], mean_var[:, t, 0:1], rstd[:, t:t + 1],
                                            ALU.subtract, ALU.mult).then_inc(u_done.sem, 1)

            def route(b):
                dve.wait_ge(logits_in_psum.sem, logits_in_psum.after(b, 1))
                dve.wait_ge(norm_done.sem, norm_done.after(b, 1))
                for t in range(2):
                    nc.vector.scalar_tensor_tensor(logits[:, t, 0:N_ATTN], logits_bank[:, t, 0:N_ATTN], norm_recip[:, t:t + 1],
                                                   gate[:, :], ALU.mult, ALU.subtract).then_inc(logits_done.sem, 1)
                dve.wait_ge(logits_done.sem, logits_done.after(b, 2))
                real = logits[:, :, 0:N_ATTN]
                nc.vector.tensor_scalar(active[:, :, :], real, 0.0, None, ALU.is_gt).then_inc(active_done.sem, 1)
                nc.vector.tensor_scalar(gated[:, :, :], real, 0.0, None, ALU.max).then_inc(gated_done.sem, 1)
                for t in range(2):
                    nc.vector.max(top[:, t, :], logits[:, t, :]).then_inc(top_done.sem, 1)
                dve.wait_ge(active_done.sem, active_done.after(b, 1))
                nc.vector.tensor_reduce(n_active[:, :], active[:, :, :], AX.X, ALU.add).then_inc(n_active_done.sem, 1)
                dve.wait_ge(top_done.sem, top_done.after(b, 2))
                nc.vector.tensor_copy(best_two[:, :, 0:2], top[:, :, 0:2]).then_inc(best_two_done.sem, 1)
                dve.wait_ge(n_active_done.sem, n_active_done.after(b, 1))
                nc.vector.tensor_scalar(inactive[:, :], n_active[:, :], 0.0, None, ALU.is_equal).then_inc(inactive_done.sem, 1)
                dve.wait_ge(best_two_done.sem, best_two_done.after(b, 1))
                wait_apart(dve)
                for t in range(2):
                    nc.vector.match_replace(others[:, t, :], best_two[:, t, :], logits[:, t, :], 4.0).then_inc(others_done.sem, 1)
                dve.wait_ge(others_done.sem, others_done.after(b, 2))
                nc.vector.tensor_tensor(fallback[:, :, :], others[:, :, 0:N_ATTN], real, ALU.not_equal).then_inc(fallback_done.sem, 1)
                dve.wait_ge(fallback_done.sem, fallback_done.after(b, 1))
                dve.wait_ge(inactive_done.sem, inactive_done.after(b, 1))
                for t in range(2):
                    nc.vector.scalar_tensor_tensor(experts[:, t, :], fallback[:, t, :], inactive[:, t:t + 1], active[:, t, :],
                                                   ALU.mult, ALU.add).then_inc(experts_done.sem, 1)
                dve.wait_ge(experts_done.sem, experts_done.after(b, 2))
                dve.wait_ge(gated_done.sem, gated_done.after(b, 1))
                nc.vector.tensor_scalar(absent[:, :, :], experts[:, :, :], 1.0, 1e9, ALU.subtract, ALU.mult).then_inc(absent_done.sem, 1)
                nc.vector.tensor_tensor(gated_used[:, :, :], gated[:, :, :], experts[:, :, :], ALU.mult).then_inc(gated_used_done.sem, 1)
                dve.wait_ge(absent_done.sem, absent_done.after(b, 1))
                dve.wait_ge(gated_used_done.sem, gated_used_done.after(b, 1))
                nc.vector.tensor_tensor(masked_logits[:, :, :], absent[:, :, :], gated_used[:, :, :], ALU.add).then_inc(masked_logits_done.sem, 1)
                dve.wait_ge(masked_logits_done.sem, masked_logits_done.after(b, 1))
                nc.vector.tensor_reduce(neg_top[:, :], masked_logits[:, :, :], AX.X, ALU.max, negate=True).then_inc(neg_top_done.sem, 1)

            def mask_inputs(b, e):
                if e < 4:
                    dve.wait_ge(transposed_in_psum.sem, transposed_in_psum.after(b, 0))
                else:
                    dve.wait_ge(transposed_in_psum.sem, transposed_in_psum.after(b, e - 2))
                for t in range(2):
                    nc.vector.tensor_scalar(masked_u[:, e % 4, t, :], un[:, t, :], experts[:, t, e:e + 1], None, ALU.mult)\
                        .then_inc(masked_u_done.sem, 1)

            def route_weights(b, u):
                dve.wait_ge(route_exps_done.sem, route_exps_done.after(b, 2))
                nc.vector.reciprocal(route_recip[:, :], route_total[:, :]).then_inc(route_recip_done.sem, 1)
                dve.wait_ge(route_recip_done.sem, route_recip_done.after(b, 1))
                for t in range(2):
                    nc.vector.tensor_scalar(route_softmax[:, t, :], route_exps[:, t, :], route_recip[:, t:t + 1], None, ALU.mult)\
                        .then_inc(route_softmax_done.sem, 1)
                dve.wait_ge(route_softmax_done.sem, route_softmax_done.after(b, 2))
                nc.vector.tensor_tensor(weights[u][:, :, :], route_softmax[:, :, :], experts[:, :, :], ALU.mult).then_inc(weights_done.sem, 1)

            def softmax(b):
                dve.wait_ge(scores_in_psum.sem, scores_in_psum.after(b, 1))
                nc.vector.scalar_tensor_tensor(scores[:, :, :], attn_bank[:, :, :], P ** -0.5, causal[:, :, :], ALU.mult, ALU.add)\
                    .then_inc(scores_done.sem, 1)
                dve.wait_ge(scores_done.sem, scores_done.after(b, 1))
                for t, tiles in enumerate(TILES_OF):
                    nc.vector.tensor_reduce(neg_max[:, t:t + 1], scores[:, tiles, :], AX.XY, ALU.max, negate=True).then_inc(max_done.sem, 1)
                dve.wait_ge(exps_done.sem, exps_done.after(b, 2))
                nc.vector.reciprocal(recip[:, :], total[:, :]).then_inc(recip_done.sem, 1)
                dve.wait_ge(recip_done.sem, recip_done.after(b, 1))
                for t, tiles in enumerate(TILES_OF):
                    nc.vector.tensor_scalar(probs[:, tiles, :], exps[:, tiles, :], recip[:, t:t + 1], None, ALU.mult).then_inc(probs_done.sem, 1)

            def add_output(b, u, n):
                e, t = 2 * (n // 2), n % 2
                dve.wait_ge(out_in_psum.sem, out_in_psum.after(b, n + 1))
                for k in range(2):
                    if k == 1:
                        dve.wait_ge(acc_done.sem, acc_done.after(b, 2 * n + 1))
                    elif n >= 2:
                        dve.wait_ge(acc_done.sem, acc_done.after(b, 2 * (n - 1)))
                    xb = x[:, at(2 * b + t), :]
                    src = xb if n < 2 and k == 0 else acc[:, t, :]
                    dst = xb if n >= N_ATTN - 2 and k == 1 else acc[:, t, :]
                    nc.vector.scalar_tensor_tensor(dst, out_bank[n % 2][:, k, :], weights[u][:, t, e + k:e + k + 1], src,
                                                   ALU.mult, ALU.add).then_inc(acc_done.sem, 1)

            def front(b, u):
                route(b)
                for e in range(4):
                    mask_inputs(b, e)
                route_weights(b, u)

            def rest_of_front(b):
                for e in range(4, N_ATTN):
                    mask_inputs(b, e)

            def batch(b, u, last=False):
                if not last:
                    moments(b + 1)
                    normalise(b + 1)
                softmax(b)
                if not last:
                    front(b + 1, 1 - u)
                for n in range(N_ATTN):
                    add_output(b, u, n)
                if not last:
                    rest_of_front(b + 1)

            dve.wait_ge(sentinels_done.sem, 2)
            moments(0)
            normalise(0)
            front(0, 0)
            rest_of_front(0)
            with dve.Fori(0, (B - 2) // 2) as pair:
                for u in range(2):
                    batch(pair * 2 + u, u)
            batch(B - 2, 0)
            batch(B - 1, 1, last=True)


N_LOADS = 27
LEAST = float(np.finfo(np.float32).min)


def decoder(nc, w, out, first=1, last=6):
    with ExitStack() as ctx:
        def sb(n, shape, dt=fp32):
            return ctx.enter_context(nc.sbuf_tensor(n, shape, dt))

        class Shared:
            pass

        shared = Shared()
        shared.x = sb("x_res", [P, T, C])
        shared.ident = sb("ident", [P, P])
        shared.ident_bf = sb("ident_bf", [P, P], bf16)
        shared.neg_half = sb("neg_half", [P, 64])
        shared.rms_eps = sb("rms_eps", [P, 1])
        shared.ln_eps = sb("ln_eps", [P, 1])
        shared.bias_row = sb("bias_row", [P, 1])
        x0 = dict(wq=sb("x0_wq", [P, 2, C]), wkv=sb("x0_wkv", [P, 2, 2 * C]), wo=sb("x0_wo", [P, 4, C]),
                  gain=sb("x0_gain", [P, 3, DH]), offset=sb("x0_offset", [P, 3, DH]))
        big = sb("big", [P, 2 * (N_ROUTED + 1) * C])
        f0_wr = big[:, 0:2 * N_ROUTED * C].rearrange("p (a e c) -> p a e c", a=2, e=N_ROUTED)
        f0_ws = big[:, 2 * N_ROUTED * C:].rearrange("p (a c) -> p a c", a=2)
        ws_pair = sb("f0_ws_pair", [P, 2, 2, C])
        f0 = dict(centroids=sb("f0_centroids", [P, 2, N_ROUTED]), bias=sb("f0_bias", [P, N_ROUTED]),
                  wr=f0_wr, ws=f0_ws, wb=sb("f0_wb", [N_ROUTED + 2, C]))
        size = 2 * N_ATTN * P
        f1_wq, f1_wk, f1_wv = (big[:, n * size:(n + 1) * size].rearrange("p (a e d) -> p a e d", a=2, e=N_ATTN) for n in range(3))
        f1_wo = big[:, 3 * size:3 * size + N_ATTN * C].rearrange("p (e c) -> p e c", e=N_ATTN)
        f1 = dict(sim=sb("f1_sim", [P, 2, N_ATTN]), gate=sb("f1_gate", [P, N_ATTN]), wq=f1_wq, wk=f1_wk, wv=f1_wv, wo=f1_wo,
                  causal=sb("f1_causal", [P, 3, P]))
        sim_sq = sb("f1_sim_sq", [P, 2, N_ATTN])
        sim_norm = sb("f1_sim_norm", [P, N_ATTN])
        ones = sb("ones", [P, P])
        x1 = dict(wq=sb("x1_wq", [P, 2, C]), wkv=sb("x1_wkv", [P, 2, 2 * C]), wo=sb("x1_wo", [P, 4, C]),
                  bqkv=sb("x1_bqkv", [P, 3 * C]), mask=sb("x1_mask", [P, 2, SK]))
        a0 = dict(wqkv=sb("a0_wqkv", [P, 2, 3 * C]), bqkv=sb("a0_bqkv", [P, 3 * C]), wo=sb("a0_wo", [P, 4, C]))
        a1 = dict(wqkv=sb("a1_wqkv", [P, 2, 3 * C]), bqkv=sb("a1_bqkv", [P, 3 * C]), wo=sb("a1_wo", [P, 4, C]))
        gain = sb("a0_gain", [P, 2, DH])
        qk_gain = sb("a0_qk_gain", [P, DH])
        head_mask = sb("a1_head_mask", [P, 4])

        loaded = nc.alloc_semaphore("loaded")
        prepared = nc.alloc_semaphore("prepared")
        causal_done, ones_done, sim_sq_done, sim_in_psum, sim_norm_done, sim_recip_done, sim_done, gate_done = (
            nc.alloc_semaphore(n) for n in ("causal_done", "ones_done", "sim_sq_done", "sim_in_psum", "sim_norm_done",
                                            "sim_recip_done", "sim_done", "gate_done"))
        with nc.psum_tensor("sim_bank", [P, N_ATTN], fp32) as sim_bank, nc.Block() as block:
            @block.sync
            def _(sp):
                loads = [
                    (shared.x[:, :, :], w["x"].rearrange("b (t p) c -> p (b t) c", p=P)),
                    (a0["wqkv"][:, :, :], w["a0_wqkv"]),
                    (a0["bqkv"][:, :], w["a0_bqkv"].partition_broadcast(P)),
                    (a0["wo"][:, :, :], w["a0_wo"]),
                    (gain[:, :, :], w["a0_gain"].partition_broadcast(P)),
                    (a1["wqkv"][:, :, :], w["a1_wqkv"]),
                    (a1["bqkv"][:, :], w["a1_bqkv"].partition_broadcast(P)),
                    (a1["wo"][:, :, :], w["a1_wo"]),
                    (head_mask[:, :], w["a1_head_mask"]),
                    (shared.bias_row[:, :], w["bias_row"]),
                    (f0_wr, w["f0_wr"]),
                    (ws_pair[:, :, :, :], w["f0_ws"]),
                    (f0["centroids"][:, :, :], w["f0_centroids"]),
                    (f0["bias"][:, :], w["f0_bias"].partition_broadcast(P)),
                    (f0["wb"][:, :], w["f0_wb"]),
                    (f1["sim"][:, :, :], w["f1_sim"]),
                    (f1["gate"][:, :], w["f1_gates"].partition_broadcast(P)),
                    (x0["wq"][:, :, :], w["x0_wq"]),
                    (x0["wkv"][:, :, :], w["x0_wkv"]),
                    (x0["wo"][:, :, :], w["x0_wo"]),
                    (x0["gain"][:, :, :], w["x0_gain"].partition_broadcast(P)),
                    (x0["offset"][:, :, :], w["x0_offset"].partition_broadcast(P)),
                    (x1["wq"][:, :, :], w["x1_wq"]),
                    (x1["wkv"][:, :, :], w["x1_wkv"]),
                    (x1["wo"][:, :, :], w["x1_wo"]),
                    (x1["bqkv"][:, :], w["x1_bqkv"].partition_broadcast(P)),
                    (x1["mask"][:, :, :], w["x1_mask"].rearrange("(t p) s -> p t s", p=P)),
                ]
                for dst, src in loads:
                    sp.dma_start(dst, src).then_inc(loaded, 16)
                assert len(loads) == N_LOADS
                sp.wait_ge(loaded, 16 * N_LOADS)

            @block.gpsimd
            def _(pool):
                nc.gpsimd.memset(shared.ln_eps[:, :], LN_EPS).then_inc(prepared, 1)
                nc.gpsimd.memset(shared.ident[:, :], 0.0).then_inc(prepared, 1)
                nc.gpsimd.memset(shared.neg_half[:, :], -0.5).then_inc(prepared, 1)
                nc.gpsimd.memset(shared.rms_eps[:, :], RMS_EPS).then_inc(prepared, 1)
                pool.wait_ge(prepared, 4)
                nc.gpsimd.affine_select(out=shared.ident[:, :], in_=shared.ident[:, :], compare_op=ALU.not_equal, fill=1.0,
                                        base=0, pattern=[[-1, P]], channel_multiplier=1).then_inc(prepared, 1)
                pool.wait_ge(prepared, 5)
                nc.gpsimd.tensor_copy(shared.ident_bf[:, :], shared.ident[:, :]).then_inc(prepared, 1)
                pool.wait_ge(loaded, 16 * N_LOADS)
                nc.gpsimd.tensor_tensor(qk_gain[:, :], gain[:, 0], gain[:, 1], ALU.mult).then_inc(prepared, 1)
                nc.gpsimd.tensor_tensor(a1["wo"][:, :, :], a1["wo"][:, :, :], head_mask[:, :].unsqueeze(2).broadcast_to([P, 4, C]), ALU.mult)\
                    .then_inc(prepared, 1)

                nc.gpsimd.tensor_tensor(f0_ws, ws_pair[:, :, 0, :], ws_pair[:, :, 1, :], ALU.add).then_inc(prepared, 1)
                pool.wait_ge(prepared, 9)
                nc.gpsimd.tensor_scalar(f0_ws, f0_ws, 0.5, None, ALU.mult).then_inc(prepared, 1)
                nc.gpsimd.tensor_scalar(x1["mask"][:, :, :], x1["mask"][:, :, :], -1e9, None, ALU.mult).then_inc(prepared, 1)

                nc.gpsimd.memset(f1["causal"][:, :, :], 0.0).then_inc(causal_done, 1)
                nc.gpsimd.memset(ones[:, :], 1.0).then_inc(ones_done, 1)
                for n, tile in enumerate((0, 2)):
                    pool.wait_ge(causal_done, 1 + n)
                    nc.gpsimd.affine_select(out=f1["causal"][:, tile, :], in_=f1["causal"][:, tile, :], compare_op=ALU.is_ge,
                                            fill=LEAST, base=0, pattern=[[-1, P]], channel_multiplier=1).then_inc(causal_done, 1)
                pool.wait_ge(sim_norm_done, 1)
                nc.gpsimd.tensor_tensor(sim_norm[:, :], sim_norm[:, :], shared.neg_half[:, 0:N_ATTN], ALU.pow).then_inc(sim_recip_done, 1)
                pool.wait_ge(sim_recip_done, 1)
                nc.gpsimd.tensor_tensor(f1["sim"][:, :, :], f1["sim"][:, :, :], sim_norm[:, :].unsqueeze(1).broadcast_to([P, 2, N_ATTN]),
                                        ALU.mult).then_inc(sim_done, 1)
                pool.wait_ge(gate_done, 3)
                pool.wait_ge(sim_done, 1)

            @block.tensor
            def _(pe):
                pe.wait_ge(sim_sq_done, 1)
                pe.wait_ge(ones_done, 1)
                for c in range(2):
                    last = nc.tensor.matmul(sim_bank[:, :], ones[:, :], sim_sq[:, c, :], start=(c == 0), stop=(c == 1))
                last.then_inc(sim_in_psum, 1)

            @block.vector
            def _(dve):
                dve.wait_ge(sim_in_psum, 1)
                nc.vector.tensor_scalar(sim_norm[:, :], sim_bank[:, :], NORM_EPS ** 2, None, ALU.max).then_inc(sim_norm_done, 1)
                dve.wait_ge(gate_done, 1)
                nc.vector.tensor_scalar(f1["gate"][:, :], f1["gate"][:, :], 1.0, None, ALU.add).then_inc(gate_done, 1)
                dve.wait_ge(gate_done, 2)
                nc.vector.reciprocal(f1["gate"][:, :], f1["gate"][:, :]).then_inc(gate_done, 1)

            @block.scalar
            def _(act):
                nc.scalar.preload_act_table_set(LN_EXP_TABLES)
                act.wait_ge(loaded, 16 * N_LOADS)
                nc.scalar.activation(sim_sq[:, :, :], f1["sim"][:, :, :], ACT.Square).then_inc(sim_sq_done, 1)
                nc.scalar.activation(f1["gate"][:, :], f1["gate"][:, :], ACT.Exp, scale=-1.0).then_inc(gate_done, 1)

        if first <= 1 <= last:
            self_attention(nc, shared, "a0", qk_gain=qk_gain, **a0)
        if first <= 2 <= last:
            cross_attention(nc, shared, "x0", w["ctx"], **x0)
        if first <= 3 <= last:
            with nc.Block() as block:
                @block.scalar
                def _(act):
                    nc.scalar.preload_act_table_set(LN_EXP_TABLES)
            shared_and_routed_experts(nc, shared, "f0", **f0)
        if first <= 4 <= last:
            self_attention(nc, shared, "a1", qk_gain=None, **a1)
        if first <= 5 <= last:
            with nc.Block() as block:
                @block.scalar
                def _(act):
                    nc.scalar.preload_act_table_set(LN_EXP_TABLES)
            cross_attention(nc, shared, "x1", w["ctx"], **x1)

        if first <= 6 <= last:
            big_loaded = nc.alloc_semaphore("big_loaded")
            with nc.Block() as block:
                @block.sync
                def _(sp):
                    for dst, src in zip((f1_wq, f1_wk, f1_wv, f1_wo), ("f1_wq", "f1_wk", "f1_wv", "f1_wo")):
                        sp.dma_start(dst, w[src]).then_inc(big_loaded, 16)
                    sp.wait_ge(big_loaded, 64)
            attention_of_experts(nc, shared, "f1", **f1)
        stored = nc.alloc_semaphore("stored")
        with nc.Block() as block:
            @block.sync
            def _(sp):
                sp.dma_start(out.rearrange("b (t p) c -> p (b t) c", p=P), shared.x[:, :, :]).then_inc(stored, 16)
                sp.wait_ge(stored, 16)


def laid_out(inputs):
    f = {k: np.asarray(v) for k, v in inputs.items()}

    def rows(w):
        return np.ascontiguousarray(w.reshape(-1, P, w.shape[1]).transpose(1, 0, 2))

    def per_head(w, bias):
        o = np.zeros((4, 2 * DH, 4, w.shape[0]), w.dtype)
        o[:, 0:DH] = w.T.reshape(4, 4, DH, w.shape[0]).transpose(1, 2, 0, 3)
        if bias is not None:
            o[0, DH, 0] = bias
        return o.reshape(P, 4, w.shape[0])

    mask = np.ones((4, 2 * DH, 4), f["L1_attn_head_mask"].dtype)
    mask[:, 0:DH] = f["L1_attn_head_mask"].reshape(4, 4).T[:, None, :]
    a = {
        "x": f["x"],
        "a0_wqkv": rows(f["L0_attn_w_qkv"].T),
        "a0_bqkv": f["L0_attn_b_qkv"],
        "a0_wo": per_head(f["L0_attn_w_proj"], f["L0_attn_b_proj"]),
        "a0_gain": np.stack([f["L0_attn_qn_w"], f["L0_attn_kn_w"]]),
        "a1_wqkv": rows(np.concatenate([f["L1_attn_Wq"], f["L1_attn_Wk"], f["L1_attn_Wv"]]).T),
        "a1_bqkv": np.concatenate([f["L1_attn_bq"], f["L1_attn_bk"], f["L1_attn_bv"]]),
        "a1_wo": per_head(f["L1_attn_Wo"], f["L1_attn_bo"]),
        "a1_head_mask": mask.reshape(P, 4),
        "bias_row": (np.arange(P) == DH).astype(np.float32).reshape(P, 1),
        "ctx": np.ascontiguousarray(f["ctx_1024"].reshape(B, SK, 2, P).transpose(3, 0, 2, 1)),
        "f0_wr": np.ascontiguousarray(f["L0_ffn_Wr"].reshape(N_ROUTED, C, 2, P).transpose(3, 2, 0, 1)),
        "f0_ws": np.ascontiguousarray(f["L0_ffn_Ws"].reshape(2, C, 2, P).transpose(3, 2, 0, 1)),
        "f0_centroids": rows(f["L0_ffn_centroids"].T),
        "f0_bias": f["L0_ffn_expert_biases"],
        "f0_wb": np.concatenate([f["L0_ffn_br"], f["L0_ffn_bs"]]),
        "f1_sim": rows(f["L1_ffn_sim_matrix"]),
        "f1_gates": f["L1_ffn_gates"],
        "f1_wo": np.ascontiguousarray(f["L1_ffn_o_proj"].transpose(1, 0, 2)),
        "x0_wq": rows(f["L0_xattn_Wq"].T),
        "x0_wkv": rows(np.concatenate([f["L0_xattn_Wk"], f["L0_xattn_Wv"]]).T),
        "x0_wo": per_head(f["L0_xattn_Wo"], f["L0_xattn_bo"]),
        "x0_gain": np.stack([f["L0_xattn_gq"], f["L0_xattn_gq"], f["L0_xattn_gk"]]),
        "x0_offset": np.stack([f["L0_xattn_bq"], f["L0_xattn_bq"], f["L0_xattn_bk"]]),
        "x1_wq": rows(f["L1_xattn_wq_w"].T),
        "x1_wkv": rows(np.concatenate([f["L1_xattn_wk_w"], f["L1_xattn_wv_w"]]).T),
        "x1_wo": per_head(f["L1_xattn_dense_w"], f["L1_xattn_dense_b"]),
        "x1_bqkv": np.concatenate([f["L1_xattn_wq_b"], f["L1_xattn_wk_b"], f["L1_xattn_wv_b"]]),
        "x1_mask": f["mask_1x1xSxS2_fk1"].reshape(S, SK),
    }
    for n in "qkv":
        a[f"f1_w{n}"] = np.ascontiguousarray(f[f"L1_ffn_{n}_proj"].reshape(N_ATTN, 2, P, P).transpose(2, 1, 0, 3))
    return a


def kernel(**inputs):
    import concourse.bacc as bacc
    from concourse.bass_utils import run_bass_kernel_spmd

    arrays = laid_out(inputs)
    nc = bacc.Bacc("TRN2", target_bir_lowering=False, num_devices=1)
    w = {n: nc.dram_tensor(f"in_{n}", a.shape, mybir.dt.from_np(a.dtype), kind="ExternalInput").ap() for n, a in arrays.items()}
    out = nc.dram_tensor("out_x", (B, S, C), fp32, kind="ExternalOutput").ap()
    decoder(nc, w, out)
    r = run_bass_kernel_spmd(nc, [{f"in_{n}": a for n, a in arrays.items()}], core_ids=[0])
    return r.results[0]["out_x"]
```

```python
import numpy as np
from contextlib import ExitStack, contextmanager

import concourse.bass as bass
from concourse import mybir

fp32 = mybir.dt.float32
bf16 = mybir.dt.bfloat16
ALU = mybir.AluOpType
ACT = mybir.ActivationFunctionType
AX = mybir.AxisListType

B, S, C = 8, 256, 256
SK = 77
H, DH = 16, 16
P = 128
T = B * S // P
PARTS = 6
LN_EPS = 1e-5
RMS_EPS = 1e-6
SCALE = DH ** -0.5
N_ROUTED = 16
N_ATTN = 8
TILES_OF = (slice(0, 1), slice(1, 3))
NORM_EPS = 1e-12
SK_PAD = 128
HEADS_OF = (slice(0, 2 * H), slice(2 * H, 3 * H))
LN_EXP_TABLES = "natural_log_exp_and_others"


class Signal:

    def __init__(self, sem, per_batch, opening=0):
        self.sem = sem
        self.per_batch = per_batch
        self.opening = opening

    def after(self, b, n):
        value = b * self.per_batch + n + self.opening
        assert isinstance(value, int) or value.min_val > 0
        return value


def wait_apart(engine):
    engine.nop(nofuse=True)


@contextmanager
def layer_block_of(nc, signals):
    with nc.Block() as block:
        yield block
    nc.clear_and_free_semaphores(signals)
    nc.all_engine_barrier()


def layer_block(ctx, nc, signals):
    return ctx.enter_context(layer_block_of(nc, signals))


def at(i, n=1):
    if isinstance(i, int):
        return slice(i, i + n)
    return bass.ds(i, n)


def self_attention(nc, shared, name, wqkv, bqkv, wo, qk_gain, at_end=None):
    x = shared.x
    with ExitStack() as ctx:
        def sb(n, shape, dt=fp32):
            return ctx.enter_context(nc.sbuf_tensor(f"{name}_{n}", shape, dt))

        def ps(n, shape, dt=fp32):
            return ctx.enter_context(nc.psum_tensor(f"{name}_{n}", shape, dt))

        signals = []

        def signal(n, per_batch, opening=0):
            signals.append(nc.alloc_semaphore(f"{name}_{n}"))
            return Signal(signals[-1], per_batch, opening)

        stats = sb("stats", [P, 2, 6])
        mean_var = sb("mean_var", [P, 2, 2])
        var_eps = sb("var_eps", [P, 2])
        rstd = sb("rstd", [P, 2])
        xn = sb("xn", [P, 2, C])
        xn_t = sb("xn_t", [P, 2, S])
        qk = sb("qk", [P, 2, 2 * H, DH])
        qk_sq = sb("qk_sq", [P, 2, 2 * H, DH])
        head_ms = sb("head_ms", [P, 4 * H])
        head_ln = sb("head_ln", [P, 4 * H])
        head_rs = sb("head_rs", [P, 4 * H])
        rest = sb("rest", [P, 2, 2 * H, DH])
        parts = [sb(f"parts_{n}", [P, 2 * H, PARTS, DH], bf16) for n in "qk"]
        stacks = [[sb(f"stack_{n}{u}", [P, H, S], bf16) for n in "qk"] for u in range(2)]
        v = [sb(f"v{u}", [P, 2, H, 2 * DH]) for u in range(2)]
        neg_max = sb("neg_max", [P, 2, H])
        neg_max_parts = sb("neg_max_parts", [P, 2, 2, H], bf16)
        neg_max_t = sb("neg_max_t", [2 * H, S], bf16)
        probs = sb("probs", [P, 4, 2, 2, S])
        den = sb("den", [P, 2, 2, S])
        log_den = sb("log_den", [P, 2, 2, S])
        attn = sb("attn", [P, 2, 2, S])

        max_bank = [ps(f"max_bank{n}", [P, 2, S]) for n in range(2)]
        prob_bank = [ps(f"prob_bank{n}", [P, 2, 2, S]) for n in range(2)]
        work_bank = [ps(f"work_bank{n}", [P, 2, S]) for n in range(2)]

        def stack_bank(n):
            return prob_bank[(n // 2 + 1) % 2][:, n % 2].rearrange("p a s -> p (a s)").bitcast(bf16)\
                .rearrange("p (h s) -> p h s", h=4)

        xn_bank = max_bank[0]
        v_bank = max_bank[1]
        neg_max_bank = max_bank[0][:, 0, 0:S // 2].bitcast(bf16)

        stats_done = signal("stats_done", 2)
        moments_done = signal("moments_done", 2)
        var_done = signal("var_done", 1)
        rstd_done = signal("rstd_done", 1)
        xn_done = signal("xn_done", 2)
        xn_t_in_psum = signal("xn_t_in_psum", 1)
        xn_t_done = signal("xn_t_done", 1)
        qk_in_psum = signal("qk_in_psum", 2)
        v_in_psum = signal("v_in_psum", 1)
        qk_done = signal("qk_done", 2)
        v_done = signal("v_done", 1)
        sq_done = signal("sq_done", 1)
        ms_done = signal("ms_done", 1)
        ln_ms_done = signal("ln_ms_done", 1)
        head_rs_done = signal("head_rs_done", 1)
        qk_scaled = signal("qk_scaled", 1)
        q_gained = signal("q_gained", 1)
        high_done = signal("high_done", 2)
        rest_done = signal("rest_done", 2)
        middle_done = signal("middle_done", 2)
        low_done = signal("low_done", 2)
        stack_in_psum = signal("stack_in_psum", 8)
        k_stack_done = signal("k_stack_done", 4)
        q_stack_done = signal("q_stack_done", 4)
        max_in_psum = signal("max_in_psum", H)
        max_done = signal("max_done", H)
        max_high_done = signal("max_high_done", 1)
        max_parts_done = signal("max_parts_done", 1)
        max_t_in_psum = signal("max_t_in_psum", 1)
        max_t_done = signal("max_t_done", 1)
        max_row_done = signal("max_row_done", 32)
        scores_in_psum = signal("scores_in_psum", H // 2)
        probs_done = signal("probs_done", H // 2, opening=1)
        attn_in_psum = signal("attn_in_psum", 4)
        den_done = signal("den_done", 2)
        log_done = signal("log_done", 2)
        recip_done = signal("recip_done", 2)
        attn_done = signal("attn_done", 2)
        out_in_psum = signal("out_in_psum", 1)
        x_done = signal("x_done", 1, opening=1)
        ones_done = signal("ones_done", 4)

        block = layer_block(ctx, nc, signals)

        @block.gpsimd
        def _(pool):
            for u in range(2):
                nc.gpsimd.memset(stacks[u][1][PARTS * DH:P], 1.0).then_inc(ones_done.sem, 1)
                pool.wait_ge(ones_done.sem, 2 * u + 1)
                nc.gpsimd.memset(v[u][:, :, :, DH:2 * DH], 1.0).then_inc(ones_done.sem, 1)
                pool.wait_ge(ones_done.sem, 2 * u + 2)

            def normalise(b):
                pool.wait_ge(moments_done.sem, moments_done.after(b, 2))
                wait_apart(pool)
                nc.gpsimd.tensor_scalar(var_eps[:, :], mean_var[:, :, 1], LN_EPS, None, ALU.add).then_inc(var_done.sem, 1)
                pool.wait_ge(var_done.sem, var_done.after(b, 1))
                nc.gpsimd.tensor_tensor(rstd[:, :], var_eps[:, :], shared.neg_half[:, 0:2], ALU.pow).then_inc(rstd_done.sem, 1)

            def split(b):
                for n in range(2):
                    pool.wait_ge(high_done.sem, high_done.after(b, n + 1))
                    high = parts[n][:, :, (0, 2)[n], :]
                    nc.gpsimd.tensor_tensor(rest[:, n], qk[:, n], high, ALU.subtract).then_inc(rest_done.sem, 1)
                for n in range(2):
                    pool.wait_ge(middle_done.sem, middle_done.after(b, n + 1))
                    nc.gpsimd.tensor_tensor(parts[n][:, :, (4, 1)[n], :], rest[:, n], parts[n][:, :, (3, 0)[n], :],
                                            ALU.subtract).then_inc(low_done.sem, 1)

            normalise(0)
            split(0)
            normalise(1)
            split(1)
            normalise(2)
            with pool.Fori(0, B - 3) as b:
                normalise(b + 3)
                split(b + 2)
            split(B - 1)
            if at_end:
                at_end(pool)

        @block.sync
        def _(sp):
            def max_row(b, u):
                sp.wait_ge(max_t_done.sem, max_t_done.after(b, 1))
                for part in range(2):
                    row = PARTS * DH + part
                    sp.dma_start(stacks[u][0][row:row + 1], neg_max_t[part * H:(part + 1) * H, :]).then_inc(max_row_done.sem, 16)

            with sp.Fori(0, B // 2) as pair:
                for u in range(2):
                    max_row(pair * 2 + u, u)
            sp.wait_ge(max_row_done.sem, max_row_done.after(B - 1, 32))

        @block.tensor
        def _(pe):
            def project(b):
                pe.wait_ge(xn_done.sem, xn_done.after(b, 2))
                for t in range(2):
                    for c in range(2):
                        last = nc.tensor.transpose(xn_bank[:, c, t * P:(t + 1) * P], xn[:, t, c * P:(c + 1) * P], shared.ident[:, :])
                last.then_inc(xn_t_in_psum.sem, 1)
                pe.wait_ge(xn_t_done.sem, xn_t_done.after(b, 1))
                for t in range(2):
                    for c in range(2):
                        last = nc.tensor.matmul(prob_bank[1][:, t].rearrange("p a s -> p (a s)"), xn_t[:, c, t * P:(t + 1) * P],
                                                wqkv[:, c, 0:2 * C], start=(c == 0), stop=(c == 1))
                    last.then_inc(qk_in_psum.sem, 1)

            def values(b):
                for t in range(2):
                    for c in range(2):
                        last = nc.tensor.matmul(v_bank[:, t, :], xn_t[:, c, t * P:(t + 1) * P],
                                                wqkv[:, c, 2 * C:3 * C], start=(c == 0), stop=(c == 1))
                last.then_inc(v_in_psum.sem, 1)

            def stack(b, u):
                for n in range(8):
                    which = 1 - n // 4
                    pe.wait_ge(low_done.sem, low_done.after(b, 2))
                    if n >= 4:
                        pe.wait_ge(k_stack_done.sem, k_stack_done.after(b, n - 3))
                    for h in range(4):
                        for t in range(2):
                            src = parts[which][:, t * H + 4 * (n % 4) + h].rearrange("p a d -> p (a d)")
                            last = nc.tensor.transpose(stack_bank(n)[0:PARTS * DH, h, t * P:(t + 1) * P], src, shared.ident_bf[:, :])
                    last.then_inc(stack_in_psum.sem, 1)

            def maxima(b, u, h):
                q, k = stacks[u]
                if h == 0:
                    pe.wait_ge(q_stack_done.sem, q_stack_done.after(b, 4))
                    pe.wait_ge(k_stack_done.sem, k_stack_done.after(b, 4))
                    pe.wait_ge(max_t_done.sem, max_t_done.after(b, 0))
                if h == 1:
                    pe.wait_ge(v_done.sem, v_done.after(b, 1))
                if h >= 2:
                    pe.wait_ge(max_done.sem, max_done.after(b, h - 1))
                for t in range(2):
                    last = nc.tensor.matmul(max_bank[h % 2][:, t, :], q[0:PARTS * DH, h, t * P:(t + 1) * P],
                                            k[0:PARTS * DH, h, :], start=True, stop=True)
                last.then_inc(max_in_psum.sem, 1)

            def max_transposed(b):
                pe.wait_ge(max_parts_done.sem, max_parts_done.after(b, 1))
                for t in range(2):
                    last = nc.tensor.transpose(neg_max_bank[0:2 * H, t * P:(t + 1) * P],
                                               neg_max_parts[:, t].rearrange("p a h -> p (a h)"), shared.ident_bf[:, :])
                last.then_inc(max_t_in_psum.sem, 1)

            def scores(b, u, p, left):
                q, k = stacks[u]
                if p == 0:
                    pe.wait_ge(max_row_done.sem, max_row_done.after(b, 32))
                    pe.wait_ge(q_stack_done.sem, q_stack_done.after(b, 4 * (1 + min(left, 1))))
                    pe.wait_ge(probs_done.sem, probs_done.after(b, 0))
                if p == 1:
                    pe.wait_ge(qk_done.sem, qk_done.after(b, 2 * (1 + min(left, 2))))
                if p >= 2:
                    pe.wait_ge(probs_done.sem, probs_done.after(b, p - 1))
                rows = PARTS * DH + 2
                for h in range(2):
                    for kt in range(2):
                        last = nc.tensor.matmul(prob_bank[p % 2][:, h, kt, :], k[0:rows, 2 * p + h, kt * P:(kt + 1) * P],
                                                q[0:rows, 2 * p + h, :], start=True, stop=True)
                last.then_inc(scores_in_psum.sem, 1)

            def weigh(b, u, g):
                if g % 2 == 0 and g == 0:
                    pe.wait_ge(v_done.sem, v_done.after(b, 1))
                pe.wait_ge(probs_done.sem, probs_done.after(b, 2 * g + 2))
                for kt in range(2):
                    for j in range(4):
                        h = 4 * g + j
                        last = nc.tensor.matmul(work_bank[g // 2][32 * j:32 * j + 32, g % 2, :], v[u][:, kt, h, :],
                                                probs[:, (h // 2) % 4, h % 2, kt, :], start=(kt == 0), stop=(kt == 1))
                last.then_inc(attn_in_psum.sem, 1)

            def output(b):
                pe.wait_ge(attn_done.sem, attn_done.after(b, 2))
                for t in range(2):
                    for g in range(4):
                        last = nc.tensor.matmul(work_bank[0][:, t, :], attn[:, g // 2, g % 2, t * P:(t + 1) * P], wo[:, g, :],
                                                start=(g == 0), stop=(g == 3))
                last.then_inc(out_in_psum.sem, 1)

            def main(b, u, left):
                for p in range(H // 2):
                    scores(b, u, p, left)
                    if left >= 1:
                        maxima(b + 1, 1 - u, 2 * p)
                        maxima(b + 1, 1 - u, 2 * p + 1)
                    if p == 2:
                        pe.wait_ge(x_done.sem, x_done.after(b, 0))
                    if p % 2 == 0 and p >= 2:
                        weigh(b, u, p // 2 - 1)
                weigh(b, u, 3)

            def batch(b, u, left=3):
                main(b, u, left)
                if left >= 1:
                    pe.wait_ge(max_done.sem, max_done.after(b + 1, H))
                if left >= 2:
                    pe.wait_ge(probs_done.sem, probs_done.after(b, H // 2))
                    values(b + 2)
                    stack(b + 2, u)
                if left >= 1:
                    max_transposed(b + 1)
                output(b)
                if left >= 3:
                    pe.wait_ge(max_t_done.sem, max_t_done.after(b + 1, 1))
                    pe.wait_ge(q_stack_done.sem, q_stack_done.after(b + 2, 2))
                    project(b + 3)

            for opened in (probs_done, x_done):
                pe.sem_inc(opened.sem, 1)
            pe.wait_ge(ones_done.sem, 4)
            for b in range(2):
                project(b)
                values(b)
                stack(b, b)
                pe.wait_ge(v_done.sem, v_done.after(b, 1))
                pe.wait_ge(q_stack_done.sem, q_stack_done.after(b, 4))
            project(2)
            for h in range(H):
                maxima(0, 0, h)
            pe.wait_ge(max_done.sem, max_done.after(0, H))
            max_transposed(0)
            with pe.Fori(0, (B - 4) // 2) as pair:
                for u in range(2):
                    batch(pair * 2 + u, u)
            for b in range(B - 4, B):
                batch(b, b % 2, min(3, B - 1 - b))

        @block.scalar
        def _(act):
            def xn_transposed(b):
                act.wait_ge(xn_t_in_psum.sem, xn_t_in_psum.after(b, 1))
                nc.scalar.activation(xn_t[:, :, :], xn_bank[:, :, :], ACT.Copy).then_inc(xn_t_done.sem, 1)

            def square(b):
                act.wait_ge(qk_done.sem, qk_done.after(b, 2))
                nc.scalar.activation(qk_sq[:, :], qk[:, :], ACT.Square).then_inc(sq_done.sem, 1)

            def head_rms(b):
                act.wait_ge(ms_done.sem, ms_done.after(b, 1))
                nc.scalar.activation(head_ln[:, :], head_ms[:, :], ACT.Ln, bias=shared.rms_eps[:, :], scale=1.0 / DH).then_inc(ln_ms_done.sem, 1)
                act.wait_ge(ln_ms_done.sem, ln_ms_done.after(b, 1))
                nc.scalar.activation(head_rs[:, :], head_ln[:, :], ACT.Exp, scale=-0.5).then_inc(head_rs_done.sem, 1)

            def high(b):
                if qk_gain is not None:
                    act.wait_ge(qk_scaled.sem, qk_scaled.after(b, 1))
                    act.wait_ge(q_gained.sem, q_gained.after(b, 1))
                else:
                    act.wait_ge(qk_done.sem, qk_done.after(b, 2))
                for n in range(2):
                    first = (0, 2)[n]
                    nc.scalar.activation(parts[n][:, :, first:first + 3, :], qk[:, n].unsqueeze(2).broadcast_to([P, 2 * H, 3, DH]),
                                         ACT.Copy).then_inc(high_done.sem, 1)

            def stack_k(b, u):
                for n in range(4):
                    act.wait_ge(stack_in_psum.sem, stack_in_psum.after(b, n + 1))
                    nc.scalar.activation(stacks[u][1][0:PARTS * DH, 4 * n:4 * n + 4, :], stack_bank(n)[0:PARTS * DH], ACT.Copy)\
                        .then_inc(k_stack_done.sem, 1)

            def max_transposed(b):
                act.wait_ge(max_t_in_psum.sem, max_t_in_psum.after(b, 1))
                nc.scalar.activation(neg_max_t[:, :], neg_max_bank[0:2 * H, :], ACT.Copy).then_inc(max_t_done.sem, 1)

            def reciprocal(b, pair):
                act.wait_ge(den_done.sem, den_done.after(b, pair + 1))
                nc.scalar.activation(log_den[:, pair], den[:, pair], ACT.Ln).then_inc(log_done.sem, 1)
                act.wait_ge(log_done.sem, log_done.after(b, pair + 1))
                nc.scalar.activation(den[:, pair], log_den[:, pair], ACT.Exp, scale=-1.0).then_inc(recip_done.sem, 1)

            def front(b, u):
                xn_transposed(b)
                if qk_gain is not None:
                    square(b)
                    head_rms(b)
                high(b)
                stack_k(b, u)

            def batch(b, u, left=3):
                if left >= 2 and qk_gain is not None:
                    square(b + 2)
                for p in range(H // 2):
                    act.wait_ge(scores_in_psum.sem, scores_in_psum.after(b, p + 1))
                    if p >= 4:
                        act.wait_ge(attn_in_psum.sem, attn_in_psum.after(b, p // 2 - 1))
                    nc.scalar.activation(probs[:, p % 4], prob_bank[p % 2][:, :], ACT.Exp, scale=SCALE).then_inc(probs_done.sem, 1)
                    if left >= 2 and p == 1 and qk_gain is not None:
                        head_rms(b + 2)
                    if left >= 2 and p == 3:
                        high(b + 2)
                    if p == 6:
                        reciprocal(b, 0)
                reciprocal(b, 1)
                if left >= 2:
                    stack_k(b + 2, u)
                if left >= 1:
                    max_transposed(b + 1)
                if left >= 3:
                    xn_transposed(b + 3)

            front(0, 0)
            front(1, 1)
            xn_transposed(2)
            max_transposed(0)
            with act.Fori(0, (B - 4) // 2) as pair:
                for u in range(2):
                    batch(pair * 2 + u, u)
            for b in range(B - 4, B):
                batch(b, b % 2, min(3, B - 1 - b))

        @block.vector
        def _(dve):
            def moments(b):
                for t in range(2):
                    nc.vector.bn_stats(stats[:, t], x[:, at(2 * b + t), :]).then_inc(stats_done.sem, 1)
                for t in range(2):
                    dve.wait_ge(stats_done.sem, stats_done.after(b, t + 1))
                    wait_apart(dve)
                    nc.vector.bn_aggr(mean_var[:, t], stats[:, t]).then_inc(moments_done.sem, 1)

            def normalise(b):
                dve.wait_ge(rstd_done.sem, rstd_done.after(b, 1))
                dve.wait_ge(moments_done.sem, moments_done.after(b, 2))
                dve.wait_ge(xn_t_in_psum.sem, xn_t_in_psum.after(b, 0))
                for t in range(2):
                    nc.vector.tensor_scalar(xn[:, t], x[:, at(2 * b + t), :], mean_var[:, t, 0:1], rstd[:, t:t + 1],
                                            ALU.subtract, ALU.mult).then_inc(xn_done.sem, 1)

            def projected(b):
                for t in range(2):
                    dve.wait_ge(qk_in_psum.sem, qk_in_psum.after(b, t + 1))
                    nc.vector.tensor_tensor(qk[:, :, t * H:(t + 1) * H, :],
                                            prob_bank[1][:, t].rearrange("p a (h d) -> p a h d", d=DH),
                                            bqkv[:, 0:2 * C].rearrange("p (a h d) -> p a h d", a=2, d=DH), ALU.add).then_inc(qk_done.sem, 1)

            def values(b, u):
                dve.wait_ge(v_in_psum.sem, v_in_psum.after(b, 1))
                bias = bqkv[:, 2 * C:3 * C].rearrange("p (h d) -> p h d", d=DH).unsqueeze(1).broadcast_to([P, 2, H, DH])
                nc.vector.tensor_tensor(v[u][:, :, :, 0:DH], v_bank[:, :, :].rearrange("p t (h d) -> p t h d", d=DH), bias, ALU.add)\
                    .then_inc(v_done.sem, 1)

            def head_ms_sum(b):
                dve.wait_ge(sq_done.sem, sq_done.after(b, 1))
                nc.vector.tensor_reduce(head_ms[:, :], qk_sq[:, :].rearrange("p a h d -> p (a h) d"), AX.X, ALU.add).then_inc(ms_done.sem, 1)

            def head_rms(b):
                dve.wait_ge(head_rs_done.sem, head_rs_done.after(b, 1))
                qk_all = qk[:, :].rearrange("p a h d -> p (a h) d")
                nc.vector.tensor_tensor(qk_all, qk_all, head_rs[:, :].unsqueeze(2).broadcast_to([P, 4 * H, DH]), ALU.mult)\
                    .then_inc(qk_scaled.sem, 1)
                dve.wait_ge(qk_scaled.sem, qk_scaled.after(b, 1))
                nc.vector.tensor_tensor(qk[:, 0], qk[:, 0], qk_gain[:, :].unsqueeze(1).broadcast_to([P, 2 * H, DH]), ALU.mult)\
                    .then_inc(q_gained.sem, 1)

            def middle(b):
                for n in range(2):
                    dve.wait_ge(rest_done.sem, rest_done.after(b, n + 1))
                    first, step = ((3, 2), (0, 5))[n]
                    nc.vector.tensor_copy(parts[n][:, :, first:6:step, :], rest[:, n].unsqueeze(2).broadcast_to([P, 2 * H, 2, DH]))\
                        .then_inc(middle_done.sem, 1)

            def stack_q(b, u):
                for n in range(4):
                    dve.wait_ge(stack_in_psum.sem, stack_in_psum.after(b, n + 5))
                    nc.vector.tensor_copy(stacks[u][0][0:PARTS * DH, 4 * n:4 * n + 4, :], stack_bank(4 + n)[0:PARTS * DH])\
                        .then_inc(q_stack_done.sem, 1)

            def maximum(b, h):
                dve.wait_ge(max_in_psum.sem, max_in_psum.after(b, h + 1))
                nc.vector.tensor_reduce(neg_max[:, :, h], max_bank[h % 2][:, :, :], AX.X, ALU.max, negate=True).then_inc(max_done.sem, 1)

            def max_parts(b):
                dve.wait_ge(max_done.sem, max_done.after(b, H))
                nc.vector.tensor_copy(neg_max_parts[:, :, 0, :], neg_max[:, :, :]).then_inc(max_high_done.sem, 1)
                dve.wait_ge(max_high_done.sem, max_high_done.after(b, 1))
                nc.vector.tensor_tensor(neg_max_parts[:, :, 1, :], neg_max[:, :, :], neg_max_parts[:, :, 0, :], ALU.subtract)\
                    .then_inc(max_parts_done.sem, 1)

            def denominator(b, pair):
                dve.wait_ge(attn_in_psum.sem, attn_in_psum.after(b, 2 * pair + 2))
                wait_apart(dve)
                nc.vector.stream_shuffle(den[:, pair], work_bank[pair][:, :, :], [DH] * 32).then_inc(den_done.sem, 1)

            def divide(b, pair):
                dve.wait_ge(recip_done.sem, recip_done.after(b, pair + 1))
                nc.vector.tensor_tensor(attn[:, pair], work_bank[pair][:, :, :], den[:, pair], ALU.mult).then_inc(attn_done.sem, 1)

            def residual(b):
                dve.wait_ge(out_in_psum.sem, out_in_psum.after(b, 1))
                xb = x[:, at(2 * b, 2), :]
                nc.vector.tensor_tensor(xb, work_bank[0][:, :, :], xb, ALU.add).then_inc(x_done.sem, 1)

            def front(b, u):
                moments(b)
                normalise(b)
                projected(b)
                values(b, u)
                if qk_gain is not None:
                    head_ms_sum(b)
                    head_rms(b)
                middle(b)
                stack_q(b, u)

            def batch(b, u, left=3):
                if left >= 3:
                    moments(b + 3)
                for p in range(H // 2):
                    if left >= 1:
                        maximum(b + 1, 2 * p)
                        maximum(b + 1, 2 * p + 1)
                    if left >= 2 and qk_gain is not None:
                        if p == 0:
                            head_ms_sum(b + 2)
                        if p == 2:
                            head_rms(b + 2)
                    if left >= 3 and p == 1:
                        normalise(b + 3)
                    if left >= 2 and p == 6:
                        middle(b + 2)
                    if p == 5:
                        denominator(b, 0)
                    if p == 7:
                        divide(b, 0)
                if left >= 1:
                    max_parts(b + 1)
                denominator(b, 1)
                if left >= 2:
                    values(b + 2, u)
                divide(b, 1)
                if left >= 2:
                    stack_q(b + 2, u)
                residual(b)
                if left >= 3:
                    projected(b + 3)

            front(0, 0)
            front(1, 1)
            moments(2)
            normalise(2)
            projected(2)
            for h in range(H):
                maximum(0, h)
            max_parts(0)
            with dve.Fori(0, (B - 4) // 2) as pair:
                for u in range(2):
                    batch(pair * 2 + u, u)
            for b in range(B - 4, B):
                batch(b, b % 2, min(3, B - 1 - b))


def cross_attention(nc, shared, name, ctx_dram, wq, wkv, wo, bqkv=None, mask=None, gain=None, offset=None, at_end=None):
    x = shared.x
    masked = mask is not None
    with ExitStack() as ctx:
        def sb(n, shape, dt=fp32):
            return ctx.enter_context(nc.sbuf_tensor(f"{name}_{n}", shape, dt))

        def ps(n, shape, dt=fp32):
            return ctx.enter_context(nc.psum_tensor(f"{name}_{n}", shape, dt))

        signals = []

        def signal(n, per_batch, opening=0):
            signals.append(nc.alloc_semaphore(f"{name}_{n}"))
            return Signal(signals[-1], per_batch, opening)

        stats = sb("stats", [P, 2, 6])
        mean_var = sb("mean_var", [P, 2, 2])
        var_eps = sb("var_eps", [P, 2])
        rstd = sb("rstd", [P, 2])
        xn = sb("xn", [P, 2, C])
        xn_t = sb("xn_t", [P, 2, S])
        ctx_t = [sb(f"ctx_t{u}", [P, 2, SK]) for u in range(2)]
        qk = [sb(f"qk{u}", [P, 3 * H, DH]) for u in range(2)]
        qk_sq = sb("qk_sq", [P, 3 * H, DH])
        head_sum = sb("head_sum", [P, 3 * H])
        head_ss = sb("head_ss", [P, 3 * H])
        head_ln = sb("head_ln", [P, 3 * H])
        head_rs = sb("head_rs", [P, 3 * H])
        rest = sb("rest", [P, 3 * H, DH])
        parts = [sb("parts_q", [P, 2 * H, PARTS, DH], bf16), sb("parts_k", [P, H, PARTS, DH], bf16)]
        q_stack = sb("q_stack", [PARTS * DH, H, S], bf16)
        k_stack = sb("k_stack", [PARTS * DH, H, SK], bf16)
        v = [sb(f"v{u}", [SK, H, 2 * DH]) for u in range(2)]
        masked_scores = sb("masked_scores", [P, 2, H, SK])
        neg_max = sb("neg_max", [P, 2, H])
        shifted = sb("shifted", [P, 2, H, SK])
        exps = sb("exps", [P, 2, H, SK])
        probs = sb("probs", [SK, H, S])
        den = sb("den", [P, 2, 2, S])
        log_den = sb("log_den", [P, 2, 2, S])
        attn = sb("attn", [P, 2, 2, S])

        ring = [ps(f"ring{n}", [P, 2, 2 * S]) for n in range(2)]
        work_bank = [ps(f"work_bank{n}", [P, 2, S]) for n in range(2)]
        q_bank = ps("q_bank", [P, 2, S])
        kv_bank = ps("kv_bank", [P, 2 * C])

        loaded = [signal(f"ctx_loaded{u}", 16) for u in range(2)]
        zeros_done = signal("zeros_done", 4)
        stats_done = signal("stats_done", 2)
        moments_done = signal("moments_done", 2)
        var_done = signal("var_done", 1)
        rstd_done = signal("rstd_done", 1)
        xn_done = signal("xn_done", 2)
        xn_t_in_psum = signal("xn_t_in_psum", 1)
        xn_t_done = signal("xn_t_done", 1)
        k_in_psum = signal("k_in_psum", 1)
        v_in_psum = signal("v_in_psum", 1)
        q_in_psum = signal("q_in_psum", 1)
        qk_done = signal("qk_done", 2)
        v_done = signal("v_done", 1)
        sum_done = signal("sum_done", 1)
        centred = signal("centred", 1)
        sq_done = signal("sq_done", 1)
        ss_done = signal("ss_done", 1)
        ln_done = signal("ln_done", 1)
        head_rs_done = signal("head_rs_done", 1)
        scaled = signal("scaled", 1)
        gained = signal("gained", 1)
        normed = signal("normed", 1)
        high_done = signal("high_done", 2)
        rest_done = signal("rest_done", 2)
        middle_done = signal("middle_done", 2)
        low_done = signal("low_done", 2)
        k_stack_in_psum = signal("k_stack_in_psum", 1)
        q_stack_in_psum = signal("q_stack_in_psum", 2)
        k_stack_done = signal("k_stack_done", 1)
        q_low_stack_done = signal("q_low_stack_done", 1)
        q_high_stack_done = signal("q_high_stack_done", 1)
        scores_in_psum = signal("scores_in_psum", 4)
        masked_done = signal("masked_done", 4)
        max_done = signal("max_done", 4)
        shifted_done = signal("shifted_done", 4)
        exps_done = signal("exps_done", 4)
        probs_in_psum = signal("probs_in_psum", 4)
        probs_done = signal("probs_done", 4, opening=1)
        attn_in_psum = signal("attn_in_psum", 4)
        den_done = signal("den_done", 2)
        log_done = signal("log_done", 2)
        recip_done = signal("recip_done", 2)
        attn_done = signal("attn_done", 2)
        out_in_psum = signal("out_in_psum", 1)
        x_done = signal("x_done", 1, opening=1)

        qk_ready = qk_done if masked else normed
        n_qk_ready = 2 if masked else 1

        block = layer_block(ctx, nc, signals)

        @block.sync
        def _(sp):
            for u in range(2):
                sp.dma_start(ctx_t[u][:, :, :], ctx_dram[:, u]).then_inc(loaded[u].sem, 16)
            with sp.Fori(0, (B - 2) // 2) as pair:
                for u in range(2):
                    b = pair * 2 + u
                    sp.wait_ge(v_in_psum.sem, v_in_psum.after(b, 1))
                    sp.dma_start(ctx_t[u][:, :, :], ctx_dram[:, at(b + 2), :, :].rearrange("p o a s -> p (o a) s"))\
                        .then_inc(loaded[u].sem, 16)
            for u in range(2):
                sp.wait_ge(loaded[u].sem, 16 * B // 2)

        @block.gpsimd
        def _(pool):
            for u in range(2):
                nc.gpsimd.memset(qk[u][:, 2 * H:3 * H, :], 0.0).then_inc(zeros_done.sem, 1)
                pool.wait_ge(zeros_done.sem, 2 * u + 1)
                nc.gpsimd.memset(v[u][:, :, DH:2 * DH], 1.0 if masked else 0.0).then_inc(zeros_done.sem, 1)
                pool.wait_ge(zeros_done.sem, 2 * u + 2)

            def normalise(b):
                pool.wait_ge(moments_done.sem, moments_done.after(b, 2))
                wait_apart(pool)
                nc.gpsimd.tensor_scalar(var_eps[:, :], mean_var[:, :, 1], LN_EPS, None, ALU.add).then_inc(var_done.sem, 1)
                pool.wait_ge(var_done.sem, var_done.after(b, 1))
                nc.gpsimd.tensor_tensor(rstd[:, :], var_eps[:, :], shared.neg_half[:, 0:2], ALU.pow).then_inc(rstd_done.sem, 1)

            def split(b, u):
                for n in range(2):
                    pool.wait_ge(high_done.sem, high_done.after(b, n + 1))
                    nc.gpsimd.tensor_tensor(rest[:, HEADS_OF[n]], qk[u][:, HEADS_OF[n]], parts[n][:, :, (0, 2)[n], :], ALU.subtract)\
                        .then_inc(rest_done.sem, 1)
                for n in range(2):
                    pool.wait_ge(middle_done.sem, middle_done.after(b, n + 1))
                    nc.gpsimd.tensor_tensor(parts[n][:, :, (4, 1)[n], :], rest[:, HEADS_OF[n]], parts[n][:, :, (3, 0)[n], :],
                                            ALU.subtract).then_inc(low_done.sem, 1)

            def shift(b):
                for n in range(4):
                    t, half = n % 2, n // 2
                    heads = slice(8 * half, 8 * half + 8)
                    pool.wait_ge(max_done.sem, max_done.after(b, n + 1))
                    nc.gpsimd.tensor_tensor(shifted[:, t, heads, :], masked_scores[:, t, heads, :],
                                            neg_max[:, t, heads].unsqueeze(2).broadcast_to([P, 8, SK]), ALU.add)\
                        .then_inc(shifted_done.sem, 1)

            def batch(b, u, left=4):
                if masked:
                    shift(b)
                if left >= 4:
                    normalise(b + 4)
                if left >= 2:
                    split(b + 2, u)

            normalise(0)
            normalise(1)
            split(0, 0)
            normalise(2)
            split(1, 1)
            normalise(3)
            with pool.Fori(0, (B - 4) // 2) as pair:
                for u in range(2):
                    batch(pair * 2 + u, u)
            for b in range(B - 4, B):
                batch(b, b % 2, B - 1 - b)
            if at_end:
                at_end(pool)

        @block.tensor
        def _(pe):
            def keys(b, u, values_before):
                pe.wait_ge(loaded[u].sem, 8 * (b - u) + 16)
                pe.wait_ge(v_done.sem, v_done.after(values_before, 0))
                pe.wait_ge(qk_done.sem, qk_done.after(b, 0))
                for c in range(2):
                    last = nc.tensor.matmul(kv_bank[0:SK, 0:C], ctx_t[u][:, c, :], wkv[:, c, 0:C], start=(c == 0), stop=(c == 1))
                last.then_inc(k_in_psum.sem, 1)

            def values(b, u, keys_before):
                pe.wait_ge(qk_done.sem, qk_done.after(keys_before, 2))
                for c in range(2):
                    last = nc.tensor.matmul(kv_bank[0:SK, C:2 * C], ctx_t[u][:, c, :], wkv[:, c, C:2 * C], start=(c == 0), stop=(c == 1))
                last.then_inc(v_in_psum.sem, 1)

            def transpose_xn(b):
                pe.wait_ge(xn_done.sem, xn_done.after(b, 2))
                pe.wait_ge(qk_done.sem, qk_done.after(b, 0))
                for t in range(2):
                    for c in range(2):
                        last = nc.tensor.transpose(q_bank[:, c, t * P:(t + 1) * P], xn[:, t, c * P:(c + 1) * P], shared.ident[:, :])
                last.then_inc(xn_t_in_psum.sem, 1)

            def queries(b):
                pe.wait_ge(xn_t_done.sem, xn_t_done.after(b, 1))
                for t in range(2):
                    for c in range(2):
                        last = nc.tensor.matmul(q_bank[:, t, :], xn_t[:, c, t * P:(t + 1) * P], wq[:, c, :], start=(c == 0), stop=(c == 1))
                last.then_inc(q_in_psum.sem, 1)

            def stack(b):
                pe.wait_ge(low_done.sem, low_done.after(b, 2))
                out = ring[0][:, :, :].bitcast(bf16)
                for h in range(H):
                    last = nc.tensor.transpose(out[0:PARTS * DH, h // 8, SK_PAD * (h % 8):SK_PAD * (h % 8) + SK],
                                               parts[1][0:SK, h].rearrange("p a d -> p (a d)"), shared.ident_bf[0:SK, 0:SK])
                last.then_inc(k_stack_in_psum.sem, 1)
                for half in range(2):
                    if half == 1:
                        pe.wait_ge(k_stack_done.sem, k_stack_done.after(b, 1))
                    out = ring[1 - half][:, :, :].bitcast(bf16)
                    for h in range(8):
                        for t in range(2):
                            last = nc.tensor.transpose(out[0:PARTS * DH, h // 4, S * (h % 4) + t * P:S * (h % 4) + (t + 1) * P],
                                                       parts[0][:, t * H + 8 * half + h].rearrange("p a d -> p (a d)"), shared.ident_bf[:, :])
                    last.then_inc(q_stack_in_psum.sem, 1)

            def stacks_ready(b):
                pe.wait_ge(k_stack_done.sem, k_stack_done.after(b, 1))
                pe.wait_ge(q_low_stack_done.sem, q_low_stack_done.after(b, 1))
                pe.wait_ge(q_high_stack_done.sem, q_high_stack_done.after(b, 1))

            def sigmoid_scores(b, n):
                if n >= 2:
                    pe.wait_ge(probs_done.sem, probs_done.after(b, n - 1))
                for h in range(4):
                    last = nc.tensor.matmul(ring[n % 2][0:SK, h // 2, S * (h % 2):S * (h % 2) + S], k_stack[:, 4 * n + h, :],
                                            q_stack[:, 4 * n + h, :], start=True, stop=True)
                last.then_inc(scores_in_psum.sem, 1)

            def softmax_scores(b, n):
                t, half = n % 2, n // 2
                if n == 0:
                    pe.wait_ge(probs_done.sem, probs_done.after(b, 0))
                if n >= 2:
                    pe.wait_ge(masked_done.sem, masked_done.after(b, n - 1))
                for h in range(8):
                    last = nc.tensor.matmul(ring[n % 2][:, h // 4, P * (h % 4):P * (h % 4) + SK],
                                            q_stack[:, 8 * half + h, t * P:(t + 1) * P], k_stack[:, 8 * half + h, :],
                                            start=True, stop=True)
                last.then_inc(scores_in_psum.sem, 1)

            def transpose_probs(b, n):
                pe.wait_ge(exps_done.sem, exps_done.after(b, 2 * (n // 2) + 2))
                if n == 0:
                    pe.wait_ge(masked_done.sem, masked_done.after(b, 4))
                if n == 1:
                    pe.wait_ge(masked_done.sem, masked_done.after(b, 4))
                if n >= 2:
                    pe.wait_ge(probs_done.sem, probs_done.after(b, n - 1))
                for h in range(4):
                    for t in range(2):
                        last = nc.tensor.transpose(ring[1 - n % 2][0:SK, h // 2, S * (h % 2) + t * P:S * (h % 2) + (t + 1) * P],
                                                   exps[:, t, 4 * n + h, :], shared.ident[:, :])
                last.then_inc(probs_in_psum.sem, 1)

            def weigh(b, u, g):
                if g == 0:
                    pe.wait_ge(x_done.sem, x_done.after(b, 0))
                    pe.wait_ge(v_done.sem, v_done.after(b, 1))
                pe.wait_ge(probs_done.sem, probs_done.after(b, g + 1))
                for j in range(4):
                    last = nc.tensor.matmul(work_bank[g // 2][32 * j:32 * j + 32, g % 2, :], v[u][:, 4 * g + j, :],
                                            probs[:, 4 * g + j, :], start=True, stop=True)
                last.then_inc(attn_in_psum.sem, 1)

            def output(b):
                pe.wait_ge(attn_done.sem, attn_done.after(b, 2))
                for t in range(2):
                    for g in range(4):
                        last = nc.tensor.matmul(work_bank[0][:, t, :], attn[:, g // 2, g % 2, t * P:(t + 1) * P], wo[:, g, :],
                                                start=(g == 0), stop=(g == 3))
                last.then_inc(out_in_psum.sem, 1)

            def batch(b, u, left=4):
                scores = softmax_scores if masked else sigmoid_scores
                stacks_ready(b)
                scores(b, 0)
                scores(b, 1)
                if left >= 3:
                    transpose_xn(b + 3)
                scores(b, 2)
                if not masked:
                    weigh(b, u, 0)
                scores(b, 3)
                if not masked:
                    weigh(b, u, 1)
                if left >= 3:
                    keys(b + 3, 1 - u, b + 2)
                    queries(b + 3)
                if masked:
                    for n in range(4):
                        transpose_probs(b, n)
                        if n >= 1:
                            weigh(b, u, n - 1)
                    weigh(b, u, 3)
                else:
                    weigh(b, u, 2)
                    weigh(b, u, 3)
                if left >= 1:
                    pe.wait_ge(probs_done.sem, probs_done.after(b, 4))
                    stack(b + 1)
                if left >= 2:
                    values(b + 2, u, b + 2 + min(left - 2, 1))
                output(b)

            for opened in (probs_done, x_done):
                pe.sem_inc(opened.sem, 1)
            pe.wait_ge(zeros_done.sem, 4)
            for b in range(3):
                keys(b, b % 2, b)
                transpose_xn(b)
                queries(b)
                if b < 2:
                    values(b, b, b)
                if b == 1:
                    stack(0)
            with pe.Fori(0, (B - 4) // 2) as pair:
                for u in range(2):
                    batch(pair * 2 + u, u)
            for b in range(B - 4, B):
                batch(b, b % 2, B - 1 - b)

        @block.scalar
        def _(act):
            def xn_transposed(b):
                act.wait_ge(xn_t_in_psum.sem, xn_t_in_psum.after(b, 1))
                nc.scalar.activation(xn_t[:, :, :], q_bank[:, :, :], ACT.Copy).then_inc(xn_t_done.sem, 1)

            def projected(b, u):
                act.wait_ge(q_in_psum.sem, q_in_psum.after(b, 1))
                if not (isinstance(b, int) and b < 2):
                    act.wait_ge(rest_done.sem, rest_done.after(b - 1, 0))
                nc.scalar.activation(qk[u][:, 0:2 * H, :], q_bank[:, :, :].rearrange("p t (h d) -> p (t h) d", d=DH), ACT.Copy)\
                    .then_inc(qk_done.sem, 1)
                act.wait_ge(k_in_psum.sem, k_in_psum.after(b, 1))
                nc.scalar.activation(qk[u][0:SK, 2 * H:3 * H, :], kv_bank[0:SK, 0:C].rearrange("p (h d) -> p h d", d=DH), ACT.Copy)\
                    .then_inc(qk_done.sem, 1)

            def square(b, u):
                act.wait_ge(centred.sem, centred.after(b, 1))
                nc.scalar.activation(qk_sq[:, :, :], qk[u][:, :, :], ACT.Square).then_inc(sq_done.sem, 1)

            def head_rs_of(b):
                act.wait_ge(ss_done.sem, ss_done.after(b, 1))
                act.wait_ge(scaled.sem, scaled.after(b, 0))
                wait_apart(act)
                nc.scalar.preload_act_table_set(LN_EXP_TABLES)
                nc.scalar.activation(head_ln[:, :], head_ss[:, :], ACT.Ln, bias=shared.ln_eps[:, :], scale=1.0 / DH).then_inc(ln_done.sem, 1)
                act.wait_ge(ln_done.sem, ln_done.after(b, 1))
                nc.scalar.activation(head_rs[:, :], head_ln[:, :], ACT.Exp, scale=-0.5).then_inc(head_rs_done.sem, 1)

            def high(b, u):
                act.wait_ge(qk_ready.sem, qk_ready.after(b, n_qk_ready))
                for n in range(2):
                    first = (0, 2)[n]
                    heads = (2 * H, H)[n]
                    nc.scalar.activation(parts[n][:, :, first:first + 3, :], qk[u][:, HEADS_OF[n]].unsqueeze(2).broadcast_to([P, heads, 3, DH]),
                                         ACT.Copy).then_inc(high_done.sem, 1)

            def stack_k(b):
                act.wait_ge(k_stack_in_psum.sem, k_stack_in_psum.after(b, 1))
                src = ring[0][:, :, :].bitcast(bf16)[0:PARTS * DH].rearrange("p a (h s) -> p (a h) s", s=SK_PAD)
                nc.scalar.activation(k_stack[:, :, :], src[:, :, 0:SK], ACT.Copy).then_inc(k_stack_done.sem, 1)

            def stack_q(b):
                act.wait_ge(q_stack_in_psum.sem, q_stack_in_psum.after(b, 2))
                nc.scalar.activation(q_stack[:, 8:16, :], ring[0][:, :, :].bitcast(bf16)[0:PARTS * DH].rearrange("p a (h s) -> p (a h) s", s=S),
                                     ACT.Copy).then_inc(q_high_stack_done.sem, 1)

            def sigmoids(b, which):
                for n in which:
                    act.wait_ge(scores_in_psum.sem, scores_in_psum.after(b, n + 1))
                    nc.scalar.activation(probs[:, 4 * n:4 * n + 4, :], ring[n % 2][0:SK].rearrange("p a (h s) -> p (a h) s", s=S),
                                         ACT.Sigmoid, scale=SCALE).then_inc(probs_done.sem, 1)

            def copy_attn(b):
                for pair in range(2):
                    act.wait_ge(attn_in_psum.sem, attn_in_psum.after(b, 2 * pair + 2))
                    nc.scalar.activation(attn[:, pair], work_bank[pair][:, :, :], ACT.Identity, bias=shared.bias_row[:, :]).then_inc(attn_done.sem, 1)

            def exponentials(b, n):
                t, half = n % 2, n // 2
                heads = slice(8 * half, 8 * half + 8)
                act.wait_ge(shifted_done.sem, shifted_done.after(b, n + 1))
                nc.scalar.activation(exps[:, t, heads, :], shifted[:, t, heads, :], ACT.Exp).then_inc(exps_done.sem, 1)

            def copy_probs(b, n):
                act.wait_ge(probs_in_psum.sem, probs_in_psum.after(b, n + 1))
                nc.scalar.activation(probs[:, 4 * n:4 * n + 4, :], ring[1 - n % 2][0:SK].rearrange("p a (h s) -> p (a h) s", s=S),
                                     ACT.Copy).then_inc(probs_done.sem, 1)

            def reciprocal(b, pair):
                act.wait_ge(den_done.sem, den_done.after(b, pair + 1))
                nc.scalar.activation(log_den[:, pair], den[:, pair], ACT.Ln).then_inc(log_done.sem, 1)
                act.wait_ge(log_done.sem, log_done.after(b, pair + 1))
                nc.scalar.activation(den[:, pair], log_den[:, pair], ACT.Exp, scale=-1.0).then_inc(recip_done.sem, 1)

            def batch(b, u, left=4):
                if masked:
                    if left >= 3:
                        xn_transposed(b + 3)
                    for n in range(4):
                        exponentials(b, n)
                    for n in range(4):
                        copy_probs(b, n)
                    for pair in range(2):
                        reciprocal(b, pair)
                else:
                    if left >= 2:
                        head_rs_of(b + 2)
                    sigmoids(b, (0, 1))
                    if left >= 3:
                        xn_transposed(b + 3)
                    sigmoids(b, (2, 3))
                    if left >= 3:
                        projected(b + 3, 1 - u)
                    copy_attn(b)
                    if left >= 3:
                        square(b + 3, 1 - u)
                if left >= 1:
                    stack_k(b + 1)
                    stack_q(b + 1)
                if left >= 2:
                    high(b + 2, u)

            act.wait_ge(zeros_done.sem, 4)
            for b in range(2):
                xn_transposed(b)
                if not masked:
                    projected(b, b)
                    square(b, b)
                    head_rs_of(b)
                if b == 0:
                    high(0, 0)
            stack_k(0)
            stack_q(0)
            high(1, 1)
            xn_transposed(2)
            if not masked:
                projected(2, 0)
                square(2, 0)
            with act.Fori(0, (B - 4) // 2) as pair:
                for u in range(2):
                    batch(pair * 2 + u, u)
            for b in range(B - 4, B):
                batch(b, b % 2, B - 1 - b)

        @block.vector
        def _(dve):
            def moments(b):
                for t in range(2):
                    nc.vector.bn_stats(stats[:, t], x[:, at(2 * b + t), :]).then_inc(stats_done.sem, 1)
                for t in range(2):
                    dve.wait_ge(stats_done.sem, stats_done.after(b, t + 1))
                    wait_apart(dve)
                    nc.vector.bn_aggr(mean_var[:, t], stats[:, t]).then_inc(moments_done.sem, 1)

            def normalise(b):
                dve.wait_ge(rstd_done.sem, rstd_done.after(b, 1))
                dve.wait_ge(moments_done.sem, moments_done.after(b, 2))
                dve.wait_ge(xn_t_in_psum.sem, xn_t_in_psum.after(b, 0))
                for t in range(2):
                    nc.vector.tensor_scalar(xn[:, t], x[:, at(2 * b + t), :], mean_var[:, t, 0:1], rstd[:, t:t + 1],
                                            ALU.subtract, ALU.mult).then_inc(xn_done.sem, 1)

            def values(b, u):
                dve.wait_ge(v_in_psum.sem, v_in_psum.after(b, 1))
                v_src = kv_bank[0:SK, C:2 * C].rearrange("p (h d) -> p h d", d=DH)
                if masked:
                    nc.vector.tensor_tensor(v[u][:, :, 0:DH], v_src, bqkv[0:SK, 2 * C:3 * C].rearrange("p (h d) -> p h d", d=DH), ALU.add)\
                        .then_inc(v_done.sem, 1)
                else:
                    nc.vector.tensor_copy(v[u][:, :, 0:DH], v_src).then_inc(v_done.sem, 1)

            def projected(b, u):
                dve.wait_ge(k_in_psum.sem, k_in_psum.after(b, 1))
                if not (isinstance(b, int) and b < 2):
                    dve.wait_ge(rest_done.sem, rest_done.after(b - 1, 0))
                nc.vector.tensor_tensor(qk[u][0:SK, 2 * H:3 * H, :], kv_bank[0:SK, 0:C].rearrange("p (h d) -> p h d", d=DH),
                                        bqkv[0:SK, C:2 * C].rearrange("p (h d) -> p h d", d=DH), ALU.add).then_inc(qk_done.sem, 1)
                dve.wait_ge(q_in_psum.sem, q_in_psum.after(b, 1))
                nc.vector.tensor_tensor(qk[u][:, 0:2 * H, :].rearrange("p (t h) d -> p t (h d)", t=2), q_bank[:, :, :],
                                        bqkv[:, 0:C].unsqueeze(1).broadcast_to([P, 2, C]), ALU.add).then_inc(qk_done.sem, 1)

            def centre(b, u):
                dve.wait_ge(qk_done.sem, qk_done.after(b, 2))
                nc.vector.tensor_reduce(head_sum[:, :], qk[u][:, :, :], AX.X, ALU.add).then_inc(sum_done.sem, 1)
                dve.wait_ge(sum_done.sem, sum_done.after(b, 1))
                nc.vector.scalar_tensor_tensor(qk[u][:, :, :], head_sum[:, :].unsqueeze(2).broadcast_to([P, 3 * H, DH]), -1.0 / DH,
                                               qk[u][:, :, :], ALU.mult, ALU.add).then_inc(centred.sem, 1)

            def sum_squares(b):
                dve.wait_ge(sq_done.sem, sq_done.after(b, 1))
                nc.vector.tensor_reduce(head_ss[:, :], qk_sq[:, :, :], AX.X, ALU.add).then_inc(ss_done.sem, 1)

            def head_norm(b, u):
                dve.wait_ge(head_rs_done.sem, head_rs_done.after(b, 1))
                nc.vector.tensor_tensor(qk[u][:, :, :], qk[u][:, :, :], head_rs[:, :].unsqueeze(2).broadcast_to([P, 3 * H, DH]), ALU.mult)\
                    .then_inc(scaled.sem, 1)
                qk_t = qk[u][:, :, :].rearrange("p (t h) d -> p t h d", t=3)
                for before, op, what, after in ((scaled, ALU.mult, gain, gained), (gained, ALU.add, offset, normed)):
                    dve.wait_ge(before.sem, before.after(b, 1))
                    nc.vector.tensor_tensor(qk_t, qk_t, what[:, :, :].unsqueeze(2).broadcast_to([P, 3, H, DH]), op).then_inc(after.sem, 1)

            def middle(b):
                for n in range(2):
                    dve.wait_ge(rest_done.sem, rest_done.after(b, n + 1))
                    first, step = ((3, 2), (0, 5))[n]
                    heads = (2 * H, H)[n]
                    nc.vector.tensor_copy(parts[n][:, :, first:6:step, :], rest[:, HEADS_OF[n]].unsqueeze(2).broadcast_to([P, heads, 2, DH]))\
                        .then_inc(middle_done.sem, 1)

            def stack_q(b):
                dve.wait_ge(q_stack_in_psum.sem, q_stack_in_psum.after(b, 1))
                nc.vector.tensor_copy(q_stack[:, 0:8, :], ring[1][:, :, :].bitcast(bf16)[0:PARTS * DH].rearrange("p a (h s) -> p (a h) s", s=S))\
                    .then_inc(q_low_stack_done.sem, 1)

            def mask_scores(b, n):
                t, half = n % 2, n // 2
                heads = slice(8 * half, 8 * half + 8)
                dve.wait_ge(scores_in_psum.sem, scores_in_psum.after(b, n + 1))
                src = ring[n % 2][:, :, :].rearrange("p a (h s) -> p (a h) s", s=P)[:, :, 0:SK]
                nc.vector.scalar_tensor_tensor(masked_scores[:, t, heads, :], src, SCALE, mask[:, t, :].unsqueeze(1).broadcast_to([P, 8, SK]),
                                               ALU.mult, ALU.add).then_inc(masked_done.sem, 1)
                dve.wait_ge(masked_done.sem, masked_done.after(b, n + 1))
                nc.vector.tensor_reduce(neg_max[:, t, heads], masked_scores[:, t, heads, :], AX.X, ALU.max, negate=True).then_inc(max_done.sem, 1)

            def divide(b, pair):
                dve.wait_ge(recip_done.sem, recip_done.after(b, pair + 1))
                nc.vector.tensor_tensor(attn[:, pair], work_bank[pair][:, :, :], den[:, pair], ALU.mult).then_inc(attn_done.sem, 1)

            def denominator(b, pair):
                dve.wait_ge(attn_in_psum.sem, attn_in_psum.after(b, 2 * pair + 2))
                wait_apart(dve)
                nc.vector.stream_shuffle(den[:, pair], work_bank[pair][:, :, :], [DH] * 32).then_inc(den_done.sem, 1)

            def residual(b):
                dve.wait_ge(out_in_psum.sem, out_in_psum.after(b, 1))
                xb = x[:, at(2 * b, 2), :]
                nc.vector.tensor_tensor(xb, work_bank[0][:, :, :], xb, ALU.add).then_inc(x_done.sem, 1)

            def batch(b, u, left=4):
                if masked:
                    for n in range(4):
                        mask_scores(b, n)
                    if left >= 4:
                        moments(b + 4)
                    if left >= 3:
                        projected(b + 3, 1 - u)
                    if left >= 4:
                        normalise(b + 4)
                    for pair in range(2):
                        denominator(b, pair)
                    for pair in range(2):
                        divide(b, pair)
                else:
                    if left >= 2:
                        head_norm(b + 2, u)
                    if left >= 4:
                        moments(b + 4)
                    if left >= 3:
                        centre(b + 3, 1 - u)
                    if left >= 4:
                        normalise(b + 4)
                    if left >= 3:
                        sum_squares(b + 3)
                if left >= 1:
                    stack_q(b + 1)
                if left >= 2:
                    values(b + 2, u)
                residual(b)
                if left >= 2:
                    middle(b + 2)

            def front(b):
                if masked:
                    projected(b, b % 2)
                if b < 2:
                    values(b, b % 2)
                moments(b + 1)
                normalise(b + 1)
                if not masked:
                    centre(b, b % 2)
                    sum_squares(b)
                    if b < 2:
                        head_norm(b, b % 2)

            dve.wait_ge(zeros_done.sem, 4)
            moments(0)
            normalise(0)
            front(0)
            middle(0)
            front(1)
            stack_q(0)
            middle(1)
            front(2)
            with dve.Fori(0, (B - 4) // 2) as pair:
                for u in range(2):
                    batch(pair * 2 + u, u)
            for b in range(B - 4, B):
                batch(b, b % 2, B - 1 - b)


def shared_and_routed_experts(nc, shared, name, centroids, bias, wr, ws, wb):
    x = shared.x
    with ExitStack() as ctx:
        def sb(n, shape, dt=fp32):
            return ctx.enter_context(nc.sbuf_tensor(f"{name}_{n}", shape, dt))

        def ps(n, shape, dt=fp32):
            return ctx.enter_context(nc.psum_tensor(f"{name}_{n}", shape, dt))

        signals = []

        def signal(n, per_batch, opening=0):
            signals.append(nc.alloc_semaphore(f"{name}_{n}"))
            return Signal(signals[-1], per_batch, opening)

        stats = sb("stats", [P, 2, 6])
        mean_var = sb("mean_var", [P, 2, 2])
        var_eps = sb("var_eps", [P, 2])
        rstd = sb("rstd", [P, 2])
        un = [sb(f"un{u}", [P, 2, C]) for u in range(2)]
        u_t = [sb(f"u_t{u}", [P, 2, S]) for u in range(2)]
        logits = sb("logits", [P, 2, N_ROUTED])
        top_logits = sb("top_logits", [P, 2, 8])
        neg_top = sb("neg_top", [P, 2])
        exps = sb("exps", [P, 2, N_ROUTED])
        total = sb("total", [P, 2])
        recip = sb("recip", [P, 2])
        softmax = sb("softmax", [P, 2, N_ROUTED + 6])
        top = sb("top", [P, 2, 8])
        best_two = sb("best_two", [P, 2, 8])
        others = sb("others", [P, 2, N_ROUTED + 6])
        gates = [sb(f"gates{u}", [P, 2, 32]) for u in range(2)]
        gates_t = [sb(f"gates_t{u}", [32, S]) for u in range(2)]
        acc = sb("acc", [P, 2, C])

        expert_bank = [ps(f"expert_bank{n}", [P, 2, C]) for n in range(4)]
        u_t_bank = ps("u_t_bank", [P, 2, S])
        logits_bank = ps("logits_bank", [P, 2, N_ROUTED])
        gates_bank = ps("gates_bank", [32, S])
        shared_bank = ps("shared_bank", [P, 2, C])

        constants_done = signal("constants_done", 4)
        stats_done = signal("stats_done", 2)
        moments_done = signal("moments_done", 2)
        var_done = signal("var_done", 1)
        rstd_done = signal("rstd_done", 1)
        u_done = signal("u_done", 2)
        u_t_in_psum = signal("u_t_in_psum", 1)
        u_t_done = signal("u_t_done", 1)
        logits_in_psum = signal("logits_in_psum", 1)
        logits_done = signal("logits_done", 1)
        top_logits_done = signal("top_logits_done", 2)
        neg_top_done = signal("neg_top_done", 1)
        exps_done = signal("exps_done", 2)
        recip_done = signal("recip_done", 1)
        softmax_done = signal("softmax_done", 2)
        top_done = signal("top_done", 2)
        best_two_done = signal("best_two_done", 1)
        others_done = signal("others_done", 2)
        gates_done = signal("gates_done", 1)
        gates_t_in_psum = signal("gates_t_in_psum", 1)
        gates_t_done = signal("gates_t_done", 1)
        shared_in_psum = signal("shared_in_psum", 1)
        expert_in_psum = signal("expert_in_psum", N_ROUTED)
        acc_done = signal("acc_done", 2 * (N_ROUTED + 1), opening=1)
        x_done = signal("x_done", 1, opening=1)

        block = layer_block(ctx, nc, signals)

        @block.gpsimd
        def _(pool):
            nc.gpsimd.memset(softmax[:, :, N_ROUTED:], -1.0).then_inc(constants_done.sem, 1)
            pool.wait_ge(constants_done.sem, 1)
            nc.gpsimd.memset(best_two[:, :, 2:8], -1.0).then_inc(constants_done.sem, 1)
            for u in range(2):
                pool.wait_ge(constants_done.sem, 2 + 3 * u)
                nc.gpsimd.memset(gates[u][:, :, :], 0.0).then_inc(constants_done.sem, 1)
                pool.wait_ge(constants_done.sem, 3 + 3 * u)
                nc.gpsimd.memset(gates[u][:, :, N_ROUTED:N_ROUTED + 2], 0.5).then_inc(constants_done.sem, 1)
                pool.wait_ge(constants_done.sem, 4 + 3 * u)
                nc.gpsimd.memset(gates[u][:, :, N_ROUTED + 2:], 0.0).then_inc(constants_done.sem, 1)

            def normalise(b):
                pool.wait_ge(moments_done.sem, moments_done.after(b, 2))
                wait_apart(pool)
                nc.gpsimd.tensor_scalar(var_eps[:, :], mean_var[:, :, 1], LN_EPS, None, ALU.add).then_inc(var_done.sem, 1)
                pool.wait_ge(var_done.sem, var_done.after(b, 1))
                nc.gpsimd.tensor_tensor(rstd[:, :], var_eps[:, :], shared.neg_half[:, 0:2], ALU.pow).then_inc(rstd_done.sem, 1)

            with pool.Fori(0, B) as b:
                normalise(b)

        @block.tensor
        def _(pe):
            def route(b, u):
                pe.wait_ge(u_done.sem, u_done.after(b, 2))
                pe.wait_ge(logits_done.sem, logits_done.after(b, 0))
                for t in range(2):
                    for c in range(2):
                        last = nc.tensor.transpose(u_t_bank[:, c, t * P:(t + 1) * P], un[u][:, t, c * P:(c + 1) * P], shared.ident[:, :])
                last.then_inc(u_t_in_psum.sem, 1)
                pe.wait_ge(u_t_done.sem, u_t_done.after(b, 1))
                for t in range(2):
                    for c in range(2):
                        last = nc.tensor.matmul(logits_bank[:, t, :], u_t[u][:, c, t * P:(t + 1) * P], centroids[:, c, :],
                                                start=(c == 0), stop=(c == 1))
                last.then_inc(logits_in_psum.sem, 1)

            def transpose_gates(b, u):
                pe.wait_ge(gates_done.sem, gates_done.after(b, 1))
                for t in range(2):
                    last = nc.tensor.transpose(gates_bank[:, t * P:(t + 1) * P], gates[u][:, t, :], shared.ident[:, :])
                last.then_inc(gates_t_in_psum.sem, 1)

            def shared_experts(b, u):
                pe.wait_ge(gates_t_done.sem, gates_t_done.after(b, 1))
                pe.wait_ge(acc_done.sem, acc_done.after(b, 0))
                for t in range(2):
                    for c in range(2):
                        nc.tensor.matmul(shared_bank[:, t, :], u_t[u][:, c, t * P:(t + 1) * P], ws[:, c, :], start=(c == 0), stop=False)
                    last = nc.tensor.matmul(shared_bank[:, t, :], gates_t[u][0:N_ROUTED + 2, t * P:(t + 1) * P], wb[:, :],
                                            start=False, stop=True)
                last.then_inc(shared_in_psum.sem, 1)

            def experts(b, u, n):
                e, t = 2 * (n // 2), n % 2
                if n >= 4:
                    pe.wait_ge(acc_done.sem, acc_done.after(b, 2 + 2 * (n - 3)))
                for c in range(2):
                    last = nc.tensor.matmul(expert_bank[n % 4][:, :, :].rearrange("p a c -> p (a c)"), u_t[u][:, c, t * P:(t + 1) * P],
                                            wr[:, c, e:e + 2, :].rearrange("p a c -> p (a c)"), start=(c == 0), stop=(c == 1))
                last.then_inc(expert_in_psum.sem, 1)

            def batch(b, u, left=1):
                shared_experts(b, u)
                for n in range(N_ROUTED):
                    experts(b, u, n)
                    if left and n == 3:
                        route(b + 1, 1 - u)
                    if left and n == 12:
                        transpose_gates(b + 1, 1 - u)

            for opened in (acc_done, x_done):
                pe.sem_inc(opened.sem, 1)
            pe.wait_ge(constants_done.sem, 8)
            route(0, 0)
            transpose_gates(0, 0)
            with pe.Fori(0, (B - 2) // 2) as pair:
                for u in range(2):
                    batch(pair * 2 + u, u)
            batch(B - 2, 0)
            batch(B - 1, 1, 0)

        @block.scalar
        def _(act):
            def front(b, u):
                act.wait_ge(u_t_in_psum.sem, u_t_in_psum.after(b, 1))
                nc.scalar.activation(u_t[u][:, :, :], u_t_bank[:, :, :], ACT.Copy).then_inc(u_t_done.sem, 1)
                act.wait_ge(neg_top_done.sem, neg_top_done.after(b, 1))
                for t in range(2):
                    nc.scalar.activation(exps[:, t, :], logits[:, t, :], ACT.Exp, bias=neg_top[:, t:t + 1],
                                         accum_out=total[:, t:t + 1]).then_inc(exps_done.sem, 1)
                act.wait_ge(gates_t_in_psum.sem, gates_t_in_psum.after(b, 1))
                nc.scalar.activation(gates_t[u][:, :], gates_bank[:, :], ACT.Copy).then_inc(gates_t_done.sem, 1)

            with act.Fori(0, B // 2) as pair:
                for u in range(2):
                    front(pair * 2 + u, u)

        @block.vector
        def _(dve):
            def moments(b):
                for t in range(2):
                    nc.vector.bn_stats(stats[:, t], x[:, at(2 * b + t), :]).then_inc(stats_done.sem, 1)
                for t in range(2):
                    dve.wait_ge(stats_done.sem, stats_done.after(b, t + 1))
                    wait_apart(dve)
                    nc.vector.bn_aggr(mean_var[:, t], stats[:, t]).then_inc(moments_done.sem, 1)

            def normalise(b, u):
                dve.wait_ge(rstd_done.sem, rstd_done.after(b, 1))
                dve.wait_ge(moments_done.sem, moments_done.after(b, 2))
                for t in range(2):
                    nc.vector.tensor_scalar(un[u][:, t], x[:, at(2 * b + t), :], mean_var[:, t, 0:1], rstd[:, t:t + 1],
                                            ALU.subtract, ALU.mult).then_inc(u_done.sem, 1)

            def route(b):
                dve.wait_ge(logits_in_psum.sem, logits_in_psum.after(b, 1))
                nc.vector.tensor_tensor(logits[:, :, :], logits_bank[:, :, :], bias[:, :].unsqueeze(1).broadcast_to([P, 2, N_ROUTED]), ALU.add)\
                    .then_inc(logits_done.sem, 1)
                dve.wait_ge(logits_done.sem, logits_done.after(b, 1))
                nc.vector.tensor_reduce(neg_top[:, :], logits[:, :, :], AX.X, ALU.max, negate=True).then_inc(neg_top_done.sem, 1)

            def gate(b, u):
                dve.wait_ge(exps_done.sem, exps_done.after(b, 2))
                nc.vector.reciprocal(recip[:, :], total[:, :]).then_inc(recip_done.sem, 1)
                dve.wait_ge(recip_done.sem, recip_done.after(b, 1))
                for t in range(2):
                    nc.vector.tensor_scalar(softmax[:, t, 0:N_ROUTED], exps[:, t, :], recip[:, t:t + 1], None, ALU.mult)\
                        .then_inc(softmax_done.sem, 1)
                for t in range(2):
                    dve.wait_ge(softmax_done.sem, softmax_done.after(b, t + 1))
                    wait_apart(dve)
                    nc.vector.max(top[:, t, :], softmax[:, t, :]).then_inc(top_done.sem, 1)
                dve.wait_ge(top_done.sem, top_done.after(b, 2))
                nc.vector.tensor_copy(best_two[:, :, 0:2], top[:, :, 0:2]).then_inc(best_two_done.sem, 1)
                dve.wait_ge(best_two_done.sem, best_two_done.after(b, 1))
                wait_apart(dve)
                for t in range(2):
                    nc.vector.match_replace(others[:, t, :], best_two[:, t, :], softmax[:, t, :], 0.0).then_inc(others_done.sem, 1)
                dve.wait_ge(others_done.sem, others_done.after(b, 2))
                nc.vector.tensor_tensor(gates[u][:, :, 0:N_ROUTED], softmax[:, :, 0:N_ROUTED], others[:, :, 0:N_ROUTED], ALU.subtract)\
                    .then_inc(gates_done.sem, 1)

            def start_acc(b, u):
                dve.wait_ge(shared_in_psum.sem, shared_in_psum.after(b, 1))
                dve.wait_ge(x_done.sem, x_done.after(b, 0))
                for t in range(2):
                    nc.vector.tensor_tensor(acc[:, t, :], shared_bank[:, t, :], un[u][:, t, :], ALU.add).then_inc(acc_done.sem, 1)

            def add_experts(b, u, n):
                e, t = 2 * (n // 2), n % 2
                dve.wait_ge(expert_in_psum.sem, expert_in_psum.after(b, n + 1))
                for k in range(2):
                    sums = 2 + 2 * n + 1 if k else (t + 1 if n < 2 else 2 + 2 * (n - 1))
                    dve.wait_ge(acc_done.sem, acc_done.after(b, sums))
                    nc.vector.scalar_tensor_tensor(acc[:, t, :], expert_bank[n % 4][:, k, :], gates[u][:, t, e + k:e + k + 1],
                                                          acc[:, t, :], ALU.mult, ALU.add).then_inc(acc_done.sem, 1)

            def residual(b):
                dve.wait_ge(acc_done.sem, acc_done.after(b + 1, 0))
                xb = x[:, at(2 * b, 2), :]
                nc.vector.tensor_tensor(xb, xb, acc[:, :, :], ALU.add).then_inc(x_done.sem, 1)

            def batch(b, u, left=1):
                if left:
                    moments(b + 1)
                start_acc(b, u)
                if left:
                    normalise(b + 1, 1 - u)
                for n in range(N_ROUTED):
                    add_experts(b, u, n)
                    if left and n == 4:
                        route(b + 1)
                    if left and n == 7:
                        gate(b + 1, 1 - u)
                residual(b)

            dve.wait_ge(constants_done.sem, 8)
            moments(0)
            normalise(0, 0)
            route(0)
            gate(0, 0)
            with dve.Fori(0, (B - 2) // 2) as pair:
                for u in range(2):
                    batch(pair * 2 + u, u)
            batch(B - 2, 0)
            batch(B - 1, 1, 0)


def attention_of_experts(nc, shared, name, sim, gate, wq, wk, wv, wo, causal):
    x = shared.x
    with ExitStack() as ctx:
        def sb(n, shape, dt=fp32):
            return ctx.enter_context(nc.sbuf_tensor(f"{name}_{n}", shape, dt))

        def ps(n, shape, dt=fp32):
            return ctx.enter_context(nc.psum_tensor(f"{name}_{n}", shape, dt))

        signals = []

        def signal(n, per_batch, opening=0):
            signals.append(nc.alloc_semaphore(f"{name}_{n}"))
            return Signal(signals[-1], per_batch, opening)

        stats = sb("stats", [P, 2, 6])
        mean_var = sb("mean_var", [P, 2, 2])
        var_eps = sb("var_eps", [P, 2])
        rstd = sb("rstd", [P, 2])
        un = sb("un", [P, 2, C])
        un_sq = sb("un_sq", [P, 2, C])
        norm_sq = sb("norm_sq", [P, 2])
        norm_sq_eps = sb("norm_sq_eps", [P, 2])
        norm_recip = sb("norm_recip", [P, 2])
        u_t = sb("u_t", [P, 2, S])
        logits = sb("logits", [P, 2, N_ATTN + 6])
        active = sb("active", [P, 2, N_ATTN])
        n_active = sb("n_active", [P, 2])
        inactive = sb("inactive", [P, 2])
        top = sb("top", [P, 2, 8])
        best_two = sb("best_two", [P, 2, 8])
        others = sb("others", [P, 2, N_ATTN + 6])
        fallback = sb("fallback", [P, 2, N_ATTN])
        experts = sb("experts", [P, 2, N_ATTN])
        gated = sb("gated", [P, 2, N_ATTN])
        absent = sb("absent", [P, 2, N_ATTN])
        gated_used = sb("gated_used", [P, 2, N_ATTN])
        masked_logits = sb("masked_logits", [P, 2, N_ATTN])
        neg_top = sb("neg_top", [P, 2])
        route_exps = sb("route_exps", [P, 2, N_ATTN])
        route_total = sb("route_total", [P, 2])
        route_recip = sb("route_recip", [P, 2])
        route_softmax = sb("route_softmax", [P, 2, N_ATTN])
        weights = [sb(f"weights{u}", [P, 2, N_ATTN]) for u in range(2)]
        experts_t = sb("experts_t", [N_ATTN, S], bf16)
        select = sb("select", [N_ATTN, N_ATTN, P], bf16)
        masked_u_t = [sb(f"masked_u_t{u}", [P, N_ATTN, 2, S]) for u in range(2)]
        sim_sq = sb("sim_sq", [P, 2, N_ATTN])
        sim_norm = sb("sim_norm", [P, N_ATTN])
        q_t = sb("q_t", [P, S])
        k_t = sb("k_t", [P, S])
        v = sb("v", [P, 2, P])
        scores = sb("scores", [P, 3, P])
        neg_max = sb("neg_max", [P, 2])
        exps = sb("exps", [P, 3, P])
        total = sb("total", [P, 2])
        recip = sb("recip", [P, 2])
        probs = sb("probs", [P, 3, P])
        probs_t = sb("probs_t", [P, 3, P])
        attn_t = sb("attn_t", [P, S])
        acc = sb("acc", [P, 2, C])

        qkv_bank = [ps(f"{n}_bank", [P, S]) for n in "qkv"]
        attn_bank = ps("attn_bank", [P, 3, P])
        out_bank = [ps(f"out_bank{n}", [P, 2, C]) for n in range(2)]
        route_bank = [ps(f"route_bank{n}", [P, 2, S]) for n in range(2)]
        u_t_bank = route_bank[0]
        logits_bank = route_bank[1]
        experts_bank = route_bank[1][0:N_ATTN, 0, :]

        constants_done = signal("constants_done", 4)
        sim_sq_done = signal("sim_sq_done", 1)
        sim_sq_in_psum = signal("sim_sq_in_psum", 1)
        sim_norm_sq_done = signal("sim_norm_sq_done", 1)
        sim_norm_done = signal("sim_norm_done", 1)
        sim_done = signal("sim_done", 1)
        gate_done = signal("gate_done", 3)
        stats_done = signal("stats_done", 2)
        moments_done = signal("moments_done", 2)
        var_done = signal("var_done", 1)
        rstd_done = signal("rstd_done", 1)
        u_done = signal("u_done", 2)
        sq_done = signal("sq_done", 2)
        norm_eps_done = signal("norm_eps_done", 1)
        norm_done = signal("norm_done", 1)
        u_t_in_psum = signal("u_t_in_psum", 1)
        u_t_done = signal("u_t_done", 1)
        experts_t_in_psum = signal("experts_t_in_psum", 1)
        experts_t_done = signal("experts_t_done", 1)
        mask_in_psum = signal("mask_in_psum", N_ATTN // 2)
        logits_in_psum = signal("logits_in_psum", 1)
        logits_done = signal("logits_done", 2)
        active_done = signal("active_done", 1)
        n_active_done = signal("n_active_done", 1)
        inactive_done = signal("inactive_done", 1)
        top_done = signal("top_done", 2)
        best_two_done = signal("best_two_done", 1)
        others_done = signal("others_done", 2)
        fallback_done = signal("fallback_done", 1)
        experts_done = signal("experts_done", 2)
        gated_done = signal("gated_done", 1)
        absent_done = signal("absent_done", 1)
        gated_used_done = signal("gated_used_done", 1)
        masked_logits_done = signal("masked_logits_done", 1)
        neg_top_done = signal("neg_top_done", 1)
        route_exps_done = signal("route_exps_done", 2)
        route_recip_done = signal("route_recip_done", 1)
        route_softmax_done = signal("route_softmax_done", 2)
        weights_done = signal("weights_done", 1)
        masked_u_done = signal("masked_u_done", N_ATTN // 2)
        q_in_psum = signal("q_in_psum", 1)
        k_in_psum = signal("k_in_psum", 1)
        v_in_psum = signal("v_in_psum", 1)
        q_done = signal("q_done", 1)
        k_done = signal("k_done", 1)
        v_done = signal("v_done", 1)
        scores_in_psum = signal("scores_in_psum", 1)
        scores_done = signal("scores_done", 1)
        max_done = signal("max_done", 2)
        exps_done = signal("exps_done", 2)
        recip_done = signal("recip_done", 1)
        probs_done = signal("probs_done", 2)
        probs_t_in_psum = signal("probs_t_in_psum", 1)
        probs_t_done = signal("probs_t_done", 1)
        attn_in_psum = signal("attn_in_psum", 1)
        attn_done = signal("attn_done", 1, opening=1)
        out_in_psum = signal("out_in_psum", N_ATTN)
        acc_done = signal("acc_done", 2 * N_ATTN, opening=1)

        block = layer_block(ctx, nc, signals)

        @block.gpsimd
        def _(pool):
            nc.gpsimd.memset(logits[:, :, N_ATTN:], -4.0).then_inc(constants_done.sem, 1)
            pool.wait_ge(constants_done.sem, 1)
            nc.gpsimd.memset(best_two[:, :, 2:8], -4.0).then_inc(constants_done.sem, 1)
            nc.gpsimd.memset(select[:, :, :], 0.0).then_inc(constants_done.sem, 1)
            pool.wait_ge(constants_done.sem, 3)
            nc.gpsimd.affine_select(out=select[:, :, :], in_=select[:, :, :], compare_op=ALU.not_equal, fill=1.0,
                                    base=0, pattern=[[-1, N_ATTN], [0, P]], channel_multiplier=1).then_inc(constants_done.sem, 1)

            def unit_columns():
                pool.wait_ge(sim_norm_sq_done.sem, 1)
                nc.gpsimd.tensor_tensor(sim_norm[:, :], sim_norm[:, :], shared.neg_half[:, 0:N_ATTN], ALU.pow).then_inc(sim_norm_done.sem, 1)
                pool.wait_ge(sim_norm_done.sem, 1)
                nc.gpsimd.tensor_tensor(sim[:, :, :], sim[:, :, :], sim_norm[:, :].unsqueeze(1).broadcast_to([P, 2, N_ATTN]), ALU.mult)\
                    .then_inc(sim_done.sem, 1)

            def normalise(b):
                pool.wait_ge(moments_done.sem, moments_done.after(b, 2))
                wait_apart(pool)
                nc.gpsimd.tensor_scalar(var_eps[:, :], mean_var[:, :, 1], LN_EPS, None, ALU.add).then_inc(var_done.sem, 1)
                pool.wait_ge(var_done.sem, var_done.after(b, 1))
                nc.gpsimd.tensor_tensor(rstd[:, :], var_eps[:, :], shared.neg_half[:, 0:2], ALU.pow).then_inc(rstd_done.sem, 1)

            def token_norms(b):
                pool.wait_ge(sq_done.sem, sq_done.after(b, 2))
                wait_apart(pool)
                nc.gpsimd.tensor_scalar(norm_sq_eps[:, :], norm_sq[:, :], NORM_EPS ** 2, None, ALU.max).then_inc(norm_eps_done.sem, 1)
                pool.wait_ge(norm_eps_done.sem, norm_eps_done.after(b, 1))
                nc.gpsimd.tensor_tensor(norm_recip[:, :], norm_sq_eps[:, :], shared.neg_half[:, 0:2], ALU.pow).then_inc(norm_done.sem, 1)

            normalise(0)
            unit_columns()
            token_norms(0)
            normalise(1)
            token_norms(1)
            with pool.Fori(2, B) as b:
                normalise(b)
                token_norms(b)

        @block.tensor
        def _(pe):
            def transpose_u(b):
                pe.wait_ge(u_done.sem, u_done.after(b, 2))
                pe.wait_ge(masked_u_done.sem, masked_u_done.after(b, 0))
                for t in range(2):
                    for c in range(2):
                        last = nc.tensor.transpose(u_t_bank[:, c, t * P:(t + 1) * P], un[:, t, c * P:(c + 1) * P], shared.ident[:, :])
                last.then_inc(u_t_in_psum.sem, 1)

            def route(b):
                pe.wait_ge(u_t_done.sem, u_t_done.after(b, 1))
                for t in range(2):
                    for c in range(2):
                        last = nc.tensor.matmul(logits_bank[:, t, 0:N_ATTN], u_t[:, c, t * P:(t + 1) * P], sim[:, c, :],
                                                start=(c == 0), stop=(c == 1))
                last.then_inc(logits_in_psum.sem, 1)

            def transpose_experts(b):
                pe.wait_ge(experts_done.sem, experts_done.after(b, 2))
                for t in range(2):
                    last = nc.tensor.transpose(experts_bank[:, t * P:(t + 1) * P], experts[:, t, :], shared.ident[:, :])
                last.then_inc(experts_t_in_psum.sem, 1)

            def spread(b, n):
                if n == 0:
                    pe.wait_ge(experts_t_done.sem, experts_t_done.after(b, 1))
                if n >= 2:
                    pe.wait_ge(masked_u_done.sem, masked_u_done.after(b, n - 1))
                for k in range(2):
                    last = nc.tensor.matmul(route_bank[n % 2][:, k, :], select[:, 2 * n + k, :], experts_t[:, :], start=True, stop=True)
                last.then_inc(mask_in_psum.sem, 1)

            def project_qk(b, u, which):
                bank, w, in_psum, done = ((qkv_bank[0], wq, q_in_psum, q_done), (qkv_bank[1], wk, k_in_psum, k_done))[which]
                if which == 0:
                    pe.wait_ge(masked_u_done.sem, masked_u_done.after(b, N_ATTN // 2))
                pe.wait_ge(done.sem, done.after(b, 0))
                for e in range(N_ATTN):
                    for c in range(2):
                        last = nc.tensor.matmul(bank[:, :], w[:, c, e, :], masked_u_t[u][:, e, c, :],
                                                start=(e == 0 and c == 0), stop=(e == N_ATTN - 1 and c == 1))
                last.then_inc(in_psum.sem, 1)

            def project_v(b, u):
                pe.wait_ge(v_done.sem, v_done.after(b, 0))
                for t in range(2):
                    for e in range(N_ATTN):
                        for c in range(2):
                            last = nc.tensor.matmul(qkv_bank[2][:, t * P:(t + 1) * P], masked_u_t[u][:, e, c, t * P:(t + 1) * P], wv[:, c, e, :],
                                                    start=(e == 0 and c == 0), stop=(e == N_ATTN - 1 and c == 1))
                last.then_inc(v_in_psum.sem, 1)

            def attend(b):
                pe.wait_ge(q_done.sem, q_done.after(b, 1))
                pe.wait_ge(k_done.sem, k_done.after(b, 1))
                pe.wait_ge(attn_done.sem, attn_done.after(b, 0))
                nc.tensor.matmul(attn_bank[:, 0, :], q_t[:, 0:P], k_t[:, 0:P], start=True, stop=True)
                nc.tensor.matmul(attn_bank[:, 1:3, :].rearrange("p a k -> p (a k)"), q_t[:, P:S], k_t[:, :],
                                 start=True, stop=True).then_inc(scores_in_psum.sem, 1)

            def transpose_probs(b):
                pe.wait_ge(probs_done.sem, probs_done.after(b, 2))
                for n, (q_tile, k_tile) in enumerate(((0, 0), (1, 0), (1, 1))):
                    last = nc.tensor.transpose(attn_bank[:, n, :], probs[:, n, :], shared.ident[:, :])
                last.then_inc(probs_t_in_psum.sem, 1)

            def weigh(b):
                pe.wait_ge(probs_t_done.sem, probs_t_done.after(b, 1))
                pe.wait_ge(v_done.sem, v_done.after(b, 1))
                out = attn_bank[:, 0:2, :].rearrange("p a k -> p (a k)")
                nc.tensor.matmul(out, v[:, 0, :], probs_t[:, 0:2, :].rearrange("p a k -> p (a k)"), start=True, stop=False)
                nc.tensor.matmul(out[:, P:S], v[:, 1, :], probs_t[:, 2, :], start=False, stop=True).then_inc(attn_in_psum.sem, 1)

            def output(b, n):
                e, t = 2 * (n // 2), n % 2
                if n == 0:
                    pe.wait_ge(attn_done.sem, attn_done.after(b, 1))
                if n < 2:
                    pe.wait_ge(acc_done.sem, acc_done.after(b, 0))
                else:
                    pe.wait_ge(acc_done.sem, acc_done.after(b, 2 * (n - 1)))
                nc.tensor.matmul(out_bank[n % 2][:, :, :].rearrange("p a c -> p (a c)"), attn_t[:, t * P:(t + 1) * P],
                                 wo[:, e:e + 2, :].rearrange("p a c -> p (a c)"), start=True, stop=True).then_inc(out_in_psum.sem, 1)

            def front(b):
                transpose_u(b)
                route(b)
                transpose_experts(b)
                for n in range(N_ATTN // 2):
                    spread(b, n)

            def batch(b, u, left=2):
                attend(b)
                if left >= 1:
                    project_qk(b + 1, 1 - u, 0)
                if left >= 2:
                    transpose_u(b + 2)
                transpose_probs(b)
                if left >= 1:
                    project_qk(b + 1, 1 - u, 1)
                if left >= 2:
                    route(b + 2)
                weigh(b)
                if left >= 1:
                    project_v(b + 1, 1 - u)
                if left >= 2:
                    transpose_experts(b + 2)
                for n in range(N_ATTN):
                    output(b, n)
                    if left >= 2 and n % 2 == 1:
                        spread(b + 2, n // 2)

            for opened in (attn_done, acc_done):
                pe.sem_inc(opened.sem, 1)
            pe.wait_ge(constants_done.sem, 4)
            pe.wait_ge(sim_sq_done.sem, 1)
            for c in range(2):
                last = nc.tensor.matmul(logits_bank[:, 0, 0:N_ATTN], shared.ones[:, :], sim_sq[:, c, :], start=(c == 0), stop=(c == 1))
            last.then_inc(sim_sq_in_psum.sem, 1)
            pe.wait_ge(sim_done.sem, 1)
            front(0)
            project_qk(0, 0, 0)
            project_qk(0, 0, 1)
            project_v(0, 0)
            front(1)
            with pe.Fori(0, (B - 2) // 2) as pair:
                for u in range(2):
                    batch(pair * 2 + u, u)
            batch(B - 2, 0, 1)
            batch(B - 1, 1, 0)

        @block.scalar
        def _(act):
            def square(b):
                for t in range(2):
                    act.wait_ge(u_done.sem, u_done.after(b, t + 1))
                    nc.scalar.activation(un_sq[:, t, :], un[:, t, :], ACT.Square, accum_out=norm_sq[:, t:t + 1]).then_inc(sq_done.sem, 1)

            def copy_u_t(b):
                act.wait_ge(u_t_in_psum.sem, u_t_in_psum.after(b, 1))
                act.wait_ge(masked_u_done.sem, masked_u_done.after(b, 0))
                nc.scalar.activation(u_t[:, :, :], u_t_bank[:, :, :], ACT.Copy).then_inc(u_t_done.sem, 1)

            def copy_experts_t(b):
                act.wait_ge(experts_t_in_psum.sem, experts_t_in_psum.after(b, 1))
                nc.scalar.activation(experts_t[:, :], experts_bank, ACT.Copy).then_inc(experts_t_done.sem, 1)

            def route_softmax_exps(b):
                act.wait_ge(neg_top_done.sem, neg_top_done.after(b, 1))
                for t in range(2):
                    nc.scalar.activation(route_exps[:, t, :], masked_logits[:, t, :], ACT.Exp, bias=neg_top[:, t:t + 1],
                                         accum_out=route_total[:, t:t + 1]).then_inc(route_exps_done.sem, 1)

            def exponentials(b):
                for t, tiles in enumerate(TILES_OF):
                    act.wait_ge(max_done.sem, max_done.after(b, t + 1))
                    nc.scalar.activation(exps[:, tiles, :], scores[:, tiles, :], ACT.Exp, bias=neg_max[:, t:t + 1],
                                         accum_out=total[:, t:t + 1]).then_inc(exps_done.sem, 1)

            def copy_q(b):
                act.wait_ge(q_in_psum.sem, q_in_psum.after(b, 1))
                nc.scalar.activation(q_t[:, :], qkv_bank[0][:, :], ACT.Copy).then_inc(q_done.sem, 1)

            def copy_k(b):
                act.wait_ge(k_in_psum.sem, k_in_psum.after(b, 1))
                nc.scalar.activation(k_t[:, :], qkv_bank[1][:, :], ACT.Copy).then_inc(k_done.sem, 1)

            def copy_v(b):
                act.wait_ge(v_in_psum.sem, v_in_psum.after(b, 1))
                nc.scalar.activation(v[:, :, :], qkv_bank[2][:, :].rearrange("p (t c) -> p t c", t=2), ACT.Copy).then_inc(v_done.sem, 1)

            def copy_probs_t(b):
                act.wait_ge(probs_t_in_psum.sem, probs_t_in_psum.after(b, 1))
                nc.scalar.activation(probs_t[:, :, :], attn_bank[:, :, :], ACT.Copy).then_inc(probs_t_done.sem, 1)

            def copy_attn(b):
                act.wait_ge(attn_in_psum.sem, attn_in_psum.after(b, 1))
                nc.scalar.activation(attn_t[:, :].rearrange("p (a k) -> p a k", a=2), attn_bank[:, 0:2, :], ACT.Copy).then_inc(attn_done.sem, 1)

            def front(b):
                square(b)
                copy_u_t(b)
                copy_experts_t(b)
                route_softmax_exps(b)

            def batch(b, left=2):
                exponentials(b)
                if left >= 2:
                    square(b + 2)
                if left >= 1:
                    copy_q(b + 1)
                if left >= 2:
                    copy_u_t(b + 2)
                copy_probs_t(b)
                if left >= 1:
                    copy_k(b + 1)
                copy_attn(b)
                if left >= 1:
                    copy_v(b + 1)
                if left >= 2:
                    copy_experts_t(b + 2)
                    route_softmax_exps(b + 2)

            nc.scalar.activation(sim_sq[:, :, :], sim[:, :, :], ACT.Square).then_inc(sim_sq_done.sem, 1)
            nc.scalar.activation(gate[:, :], gate[:, :], ACT.Exp, scale=-1.0).then_inc(gate_done.sem, 1)
            front(0)
            copy_q(0)
            copy_k(0)
            copy_v(0)
            front(1)
            with act.Fori(0, B - 2) as b:
                batch(b)
            batch(B - 2, 1)
            batch(B - 1, 0)

        @block.vector
        def _(dve):
            def moments(b):
                dve.wait_ge(u_done.sem, u_done.after(b, 0))
                for t in range(2):
                    nc.vector.bn_stats(stats[:, t], x[:, at(2 * b + t), :]).then_inc(stats_done.sem, 1)
                for t in range(2):
                    dve.wait_ge(stats_done.sem, stats_done.after(b, t + 1))
                    wait_apart(dve)
                    nc.vector.bn_aggr(mean_var[:, t], stats[:, t]).then_inc(moments_done.sem, 1)

            def normalise(b):
                dve.wait_ge(rstd_done.sem, rstd_done.after(b, 1))
                dve.wait_ge(moments_done.sem, moments_done.after(b, 2))
                dve.wait_ge(sq_done.sem, sq_done.after(b, 0))
                dve.wait_ge(u_t_in_psum.sem, u_t_in_psum.after(b, 0))
                for t in range(2):
                    nc.vector.tensor_scalar(un[:, t], x[:, at(2 * b + t), :], mean_var[:, t, 0:1], rstd[:, t:t + 1],
                                            ALU.subtract, ALU.mult).then_inc(u_done.sem, 1)

            def route(b):
                dve.wait_ge(logits_in_psum.sem, logits_in_psum.after(b, 1))
                dve.wait_ge(norm_done.sem, norm_done.after(b, 1))
                for t in range(2):
                    nc.vector.scalar_tensor_tensor(logits[:, t, 0:N_ATTN], logits_bank[:, t, 0:N_ATTN], norm_recip[:, t:t + 1],
                                                   gate[:, :], ALU.mult, ALU.subtract).then_inc(logits_done.sem, 1)
                dve.wait_ge(logits_done.sem, logits_done.after(b, 2))
                real = logits[:, :, 0:N_ATTN]
                nc.vector.tensor_scalar(active[:, :, :], real, 0.0, None, ALU.is_gt).then_inc(active_done.sem, 1)
                nc.vector.tensor_scalar(gated[:, :, :], real, 0.0, None, ALU.max).then_inc(gated_done.sem, 1)
                for t in range(2):
                    nc.vector.max(top[:, t, :], logits[:, t, :]).then_inc(top_done.sem, 1)
                dve.wait_ge(active_done.sem, active_done.after(b, 1))
                nc.vector.tensor_reduce(n_active[:, :], active[:, :, :], AX.X, ALU.add).then_inc(n_active_done.sem, 1)
                dve.wait_ge(top_done.sem, top_done.after(b, 2))
                nc.vector.tensor_copy(best_two[:, :, 0:2], top[:, :, 0:2]).then_inc(best_two_done.sem, 1)
                dve.wait_ge(n_active_done.sem, n_active_done.after(b, 1))
                nc.vector.tensor_scalar(inactive[:, :], n_active[:, :], 0.0, None, ALU.is_equal).then_inc(inactive_done.sem, 1)
                dve.wait_ge(best_two_done.sem, best_two_done.after(b, 1))
                wait_apart(dve)
                for t in range(2):
                    nc.vector.match_replace(others[:, t, :], best_two[:, t, :], logits[:, t, :], 4.0).then_inc(others_done.sem, 1)
                dve.wait_ge(others_done.sem, others_done.after(b, 2))
                nc.vector.tensor_tensor(fallback[:, :, :], others[:, :, 0:N_ATTN], real, ALU.not_equal).then_inc(fallback_done.sem, 1)
                dve.wait_ge(fallback_done.sem, fallback_done.after(b, 1))
                dve.wait_ge(inactive_done.sem, inactive_done.after(b, 1))
                for t in range(2):
                    nc.vector.scalar_tensor_tensor(experts[:, t, :], fallback[:, t, :], inactive[:, t:t + 1], active[:, t, :],
                                                   ALU.mult, ALU.add).then_inc(experts_done.sem, 1)
                dve.wait_ge(experts_done.sem, experts_done.after(b, 2))
                dve.wait_ge(gated_done.sem, gated_done.after(b, 1))
                nc.vector.tensor_scalar(absent[:, :, :], experts[:, :, :], 1.0, 1e9, ALU.subtract, ALU.mult).then_inc(absent_done.sem, 1)
                nc.vector.tensor_tensor(gated_used[:, :, :], gated[:, :, :], experts[:, :, :], ALU.mult).then_inc(gated_used_done.sem, 1)
                dve.wait_ge(absent_done.sem, absent_done.after(b, 1))
                dve.wait_ge(gated_used_done.sem, gated_used_done.after(b, 1))
                nc.vector.tensor_tensor(masked_logits[:, :, :], absent[:, :, :], gated_used[:, :, :], ALU.add).then_inc(masked_logits_done.sem, 1)
                dve.wait_ge(masked_logits_done.sem, masked_logits_done.after(b, 1))
                nc.vector.tensor_reduce(neg_top[:, :], masked_logits[:, :, :], AX.X, ALU.max, negate=True).then_inc(neg_top_done.sem, 1)

            def mask_inputs(b, u, n):
                dve.wait_ge(mask_in_psum.sem, mask_in_psum.after(b, n + 1))
                if n == 0 and not (isinstance(b, int) and b < 2):
                    dve.wait_ge(v_in_psum.sem, v_in_psum.after(b - 1, 0))
                nc.vector.tensor_tensor(masked_u_t[u][:, 2 * n:2 * n + 2, :, :], route_bank[n % 2][:, :, :].unsqueeze(2).broadcast_to([P, 2, 2, S]),
                                        u_t[:, :, :].unsqueeze(1).broadcast_to([P, 2, 2, S]), ALU.mult).then_inc(masked_u_done.sem, 1)

            def route_weights(b, u):
                dve.wait_ge(route_exps_done.sem, route_exps_done.after(b, 2))
                nc.vector.reciprocal(route_recip[:, :], route_total[:, :]).then_inc(route_recip_done.sem, 1)
                dve.wait_ge(route_recip_done.sem, route_recip_done.after(b, 1))
                for t in range(2):
                    nc.vector.tensor_scalar(route_softmax[:, t, :], route_exps[:, t, :], route_recip[:, t:t + 1], None, ALU.mult)\
                        .then_inc(route_softmax_done.sem, 1)
                dve.wait_ge(route_softmax_done.sem, route_softmax_done.after(b, 2))
                nc.vector.tensor_tensor(weights[u][:, :, :], route_softmax[:, :, :], experts[:, :, :], ALU.mult).then_inc(weights_done.sem, 1)

            def score_maxima(b):
                dve.wait_ge(scores_in_psum.sem, scores_in_psum.after(b, 1))
                nc.vector.scalar_tensor_tensor(scores[:, :, :], attn_bank[:, :, :], P ** -0.5, causal[:, :, :], ALU.mult, ALU.add)\
                    .then_inc(scores_done.sem, 1)
                dve.wait_ge(scores_done.sem, scores_done.after(b, 1))
                for t, tiles in enumerate(TILES_OF):
                    nc.vector.tensor_reduce(neg_max[:, t:t + 1], scores[:, tiles, :], AX.XY, ALU.max, negate=True).then_inc(max_done.sem, 1)

            def probabilities(b):
                dve.wait_ge(exps_done.sem, exps_done.after(b, 2))
                nc.vector.reciprocal(recip[:, :], total[:, :]).then_inc(recip_done.sem, 1)
                dve.wait_ge(recip_done.sem, recip_done.after(b, 1))
                for t, tiles in enumerate(TILES_OF):
                    nc.vector.tensor_scalar(probs[:, tiles, :], exps[:, tiles, :], recip[:, t:t + 1], None, ALU.mult).then_inc(probs_done.sem, 1)

            def add_output(b, u, n):
                e, t = 2 * (n // 2), n % 2
                dve.wait_ge(out_in_psum.sem, out_in_psum.after(b, n + 1))
                for k in range(2):
                    if k == 1:
                        dve.wait_ge(acc_done.sem, acc_done.after(b, 2 * n + 1))
                    elif n >= 2:
                        dve.wait_ge(acc_done.sem, acc_done.after(b, 2 * (n - 1)))
                    xb = x[:, at(2 * b + t), :]
                    src = xb if n < 2 and k == 0 else acc[:, t, :]
                    dst = xb if n >= N_ATTN - 2 and k == 1 else acc[:, t, :]
                    nc.vector.scalar_tensor_tensor(dst, out_bank[n % 2][:, k, :], weights[u][:, t, e + k:e + k + 1], src,
                                                   ALU.mult, ALU.add).then_inc(acc_done.sem, 1)

            def front(b, u):
                moments(b)
                normalise(b)
                route(b)
                for n in range(N_ATTN // 2):
                    mask_inputs(b, u, n)
                route_weights(b, u)

            def batch(b, u, left=2):
                score_maxima(b)
                if left >= 2:
                    normalise(b + 2)
                probabilities(b)
                if left >= 2:
                    route(b + 2)
                for n in range(N_ATTN):
                    add_output(b, u, n)
                    if left >= 2 and n % 2 == 1:
                        mask_inputs(b + 2, u, n // 2)
                if left >= 2:
                    route_weights(b + 2, u)
                if left >= 3:
                    moments(b + 3)

            dve.wait_ge(constants_done.sem, 4)
            moments(0)
            dve.wait_ge(gate_done.sem, 1)
            nc.vector.tensor_scalar(gate[:, :], gate[:, :], 1.0, None, ALU.add).then_inc(gate_done.sem, 1)
            dve.wait_ge(sim_sq_in_psum.sem, 1)
            nc.vector.tensor_scalar(sim_norm[:, :], logits_bank[:, 0, 0:N_ATTN], NORM_EPS ** 2, None, ALU.max).then_inc(sim_norm_sq_done.sem, 1)
            dve.wait_ge(gate_done.sem, 2)
            nc.vector.reciprocal(gate[:, :], gate[:, :]).then_inc(gate_done.sem, 1)
            dve.wait_ge(gate_done.sem, 3)
            normalise(0)
            route(0)
            for n in range(N_ATTN // 2):
                mask_inputs(0, 0, n)
            route_weights(0, 0)
            front(1, 1)
            moments(2)
            with dve.Fori(0, (B - 4) // 2) as pair:
                for u in range(2):
                    batch(pair * 2 + u, u, 3)
            for b in range(B - 4, B):
                batch(b, b % 2, min(3, B - 1 - b))


LEAST = float(np.finfo(np.float32).min)


def decoder(nc, w, out, first=1, last=6):
    with ExitStack() as ctx:
        def sb(n, shape, dt=fp32):
            return ctx.enter_context(nc.sbuf_tensor(n, shape, dt))

        class Shared:
            pass

        shared = Shared()
        shared.x = sb("x_res", [P, T, C])
        shared.ident = sb("ident", [P, P])
        shared.ident_bf = sb("ident_bf", [P, P], bf16)
        shared.neg_half = sb("neg_half", [P, 64])
        shared.rms_eps = sb("rms_eps", [P, 1])
        shared.ln_eps = sb("ln_eps", [P, 1])
        shared.bias_row = sb("bias_row", [P, 1])
        x0 = dict(wq=sb("x0_wq", [P, 2, C]), wkv=sb("x0_wkv", [P, 2, 2 * C]), wo=sb("x0_wo", [P, 4, C]),
                  gain=sb("x0_gain", [P, 3, DH]), offset=sb("x0_offset", [P, 3, DH]))
        big = sb("big", [P, 2 * (N_ROUTED + 1) * C])
        f0_wr = big[:, 0:2 * N_ROUTED * C].rearrange("p (a e c) -> p a e c", a=2, e=N_ROUTED)
        f0_ws = big[:, 2 * N_ROUTED * C:].rearrange("p (a c) -> p a c", a=2)
        ws_pair = sb("f0_ws_pair", [P, 2, 2, C])
        f0 = dict(centroids=sb("f0_centroids", [P, 2, N_ROUTED]), bias=sb("f0_bias", [P, N_ROUTED]),
                  wr=f0_wr, ws=f0_ws, wb=sb("f0_wb", [N_ROUTED + 2, C]))
        size = 2 * N_ATTN * P
        f1_wq, f1_wk, f1_wv = (big[:, n * size:(n + 1) * size].rearrange("p (a e d) -> p a e d", a=2, e=N_ATTN) for n in range(3))
        f1_wo = big[:, 3 * size:3 * size + N_ATTN * C].rearrange("p (e c) -> p e c", e=N_ATTN)
        f1 = dict(sim=sb("f1_sim", [P, 2, N_ATTN]), gate=sb("f1_gate", [P, N_ATTN]), wq=f1_wq, wk=f1_wk, wv=f1_wv, wo=f1_wo,
                  causal=sb("f1_causal", [P, 3, P]))
        ones = shared.ones = sb("ones", [P, P])
        x1 = dict(wq=sb("x1_wq", [P, 2, C]), wkv=sb("x1_wkv", [P, 2, 2 * C]), wo=sb("x1_wo", [P, 4, C]),
                  bqkv=sb("x1_bqkv", [P, 3 * C]), mask=sb("x1_mask", [P, 2, SK]))
        a0 = dict(wqkv=sb("a0_wqkv", [P, 2, 3 * C]), bqkv=sb("a0_bqkv", [P, 3 * C]), wo=sb("a0_wo", [P, 4, C]))
        a1 = dict(wqkv=sb("a1_wqkv", [P, 2, 3 * C]), bqkv=sb("a1_bqkv", [P, 3 * C]), wo=sb("a1_wo", [P, 4, C]))
        gain = sb("a0_gain", [P, 2, DH])
        qk_gain = sb("a0_qk_gain", [P, DH])
        head_mask = sb("a1_head_mask", [P, 4])

        prepared = nc.alloc_semaphore("prepared")
        routed_ready = nc.alloc_semaphore("routed_ready")
        masks_done = nc.alloc_semaphore("masks_done")

        loads = {
            "a0": [
                (shared.x[:, 0:4, :], w["x"][0:2].rearrange("b (t p) c -> p (b t) c", p=P)),
                (a0["wqkv"][:, :, :], w["a0_wqkv"]),
                (a0["bqkv"][:, :], w["a0_bqkv"].partition_broadcast(P)),
                (gain[:, :, :], w["a0_gain"].partition_broadcast(P)),
                (shared.bias_row[:, :], w["bias_row"]),
                (a0["wo"][:, :, :], w["a0_wo"]),
                (shared.x[:, 4:T, :], w["x"][2:B].rearrange("b (t p) c -> p (b t) c", p=P)),
            ],
            "x0": [
                (x0["wq"][:, :, :], w["x0_wq"]),
                (x0["wkv"][:, :, :], w["x0_wkv"]),
                (x0["wo"][:, :, :], w["x0_wo"]),
                (x0["gain"][:, :, :], w["x0_gain"].partition_broadcast(P)),
                (x0["offset"][:, :, :], w["x0_offset"].partition_broadcast(P)),
            ],
            "f0": [
                (f0_wr, w["f0_wr"]),
                (ws_pair[:, :, :, :], w["f0_ws"]),
                (f0["centroids"][:, :, :], w["f0_centroids"]),
                (f0["bias"][:, :], w["f0_bias"].partition_broadcast(P)),
                (f0["wb"][:, :], w["f0_wb"]),
            ],
            "rest": [
                (a1["wqkv"][:, :, :], w["a1_wqkv"]),
                (a1["bqkv"][:, :], w["a1_bqkv"].partition_broadcast(P)),
                (a1["wo"][:, :, :], w["a1_wo"]),
                (head_mask[:, :], w["a1_head_mask"]),
                (x1["wq"][:, :, :], w["x1_wq"]),
                (x1["wkv"][:, :, :], w["x1_wkv"]),
                (x1["wo"][:, :, :], w["x1_wo"]),
                (x1["bqkv"][:, :], w["x1_bqkv"].partition_broadcast(P)),
                (x1["mask"][:, :, :], w["x1_mask"].rearrange("(t p) s -> p t s", p=P)),
                (f1["sim"][:, :, :], w["f1_sim"]),
                (f1["gate"][:, :], w["f1_gates"].partition_broadcast(P)),
            ],
            "f1": [(dst, w[src]) for dst, src in zip((f1_wq, f1_wk, f1_wv, f1_wo), ("f1_wq", "f1_wk", "f1_wv", "f1_wo"))],
        }
        loaded = {layer: nc.alloc_semaphore(f"loaded_{layer}") for layer in loads}

        def start_loads(sp, *layers):
            for layer in layers:
                for dst, src in loads[layer]:
                    sp.dma_start(dst, src).then_inc(loaded[layer], 16)

        def wait_loaded(engine, layer):
            engine.wait_ge(loaded[layer], 16 * len(loads[layer]))

        with nc.Block() as block:
            @block.sync
            def _(sp):
                start_loads(sp, "a0", "x0", "f0", "rest")
                wait_loaded(sp, "a0")

            @block.gpsimd
            def _(pool):
                nc.gpsimd.memset(shared.ln_eps[:, :], LN_EPS).then_inc(prepared, 1)
                nc.gpsimd.memset(shared.ident[:, :], 0.0).then_inc(prepared, 1)
                nc.gpsimd.memset(shared.neg_half[:, :], -0.5).then_inc(prepared, 1)
                nc.gpsimd.memset(shared.rms_eps[:, :], RMS_EPS).then_inc(prepared, 1)
                pool.wait_ge(prepared, 4)
                nc.gpsimd.affine_select(out=shared.ident[:, :], in_=shared.ident[:, :], compare_op=ALU.not_equal, fill=1.0,
                                        base=0, pattern=[[-1, P]], channel_multiplier=1).then_inc(prepared, 1)
                pool.wait_ge(prepared, 5)
                nc.gpsimd.tensor_copy(shared.ident_bf[:, :], shared.ident[:, :]).then_inc(prepared, 1)
                nc.gpsimd.memset(f1["causal"][:, :, :], 0.0).then_inc(prepared, 1)
                nc.gpsimd.memset(ones[:, :], 1.0).then_inc(prepared, 1)
                for n, tile in enumerate((0, 2)):
                    pool.wait_ge(prepared, 8 + n)
                    nc.gpsimd.affine_select(out=f1["causal"][:, tile, :], in_=f1["causal"][:, tile, :], compare_op=ALU.is_ge,
                                            fill=LEAST, base=0, pattern=[[-1, P]], channel_multiplier=1).then_inc(prepared, 1)
                wait_loaded(pool, "a0")
                nc.gpsimd.tensor_tensor(qk_gain[:, :], gain[:, 0], gain[:, 1], ALU.mult).then_inc(prepared, 1)
                pool.wait_ge(prepared, 11)

            @block.scalar
            def _(act):
                nc.scalar.preload_act_table_set(LN_EXP_TABLES)

        def prepare_routed(pool):
            wait_loaded(pool, "f0")
            nc.gpsimd.tensor_tensor(f0_ws, ws_pair[:, :, 0, :], ws_pair[:, :, 1, :], ALU.add).then_inc(routed_ready, 1)
            pool.wait_ge(routed_ready, 1)
            nc.gpsimd.tensor_scalar(f0_ws, f0_ws, 0.5, None, ALU.mult).then_inc(routed_ready, 1)
            pool.wait_ge(routed_ready, 2)

        def prepare_masks(pool):
            wait_loaded(pool, "rest")
            nc.gpsimd.tensor_tensor(a1["wo"][:, :, :], a1["wo"][:, :, :], head_mask[:, :].unsqueeze(2).broadcast_to([P, 4, C]), ALU.mult)\
                .then_inc(masks_done, 1)
            nc.gpsimd.tensor_scalar(x1["mask"][:, :, :], x1["mask"][:, :, :], -1e9, None, ALU.mult).then_inc(masks_done, 1)
            pool.wait_ge(masks_done, 2)

        if first <= 1 <= last:
            self_attention(nc, shared, "a0", qk_gain=qk_gain, at_end=prepare_routed, **a0)
        if first <= 2 <= last:
            with nc.Block() as block:
                @block.sync
                def _(sp):
                    wait_loaded(sp, "x0")
            cross_attention(nc, shared, "x0", w["ctx"], at_end=prepare_masks, **x0)
        if first <= 3 <= last:
            with nc.Block() as block:
                @block.sync
                def _(sp):
                    wait_loaded(sp, "f0")

                @block.scalar
                def _(act):
                    nc.scalar.preload_act_table_set(LN_EXP_TABLES)
            shared_and_routed_experts(nc, shared, "f0", **f0)
        with nc.Block() as block:
            @block.sync
            def _(sp):
                wait_loaded(sp, "rest")
                start_loads(sp, "f1")
        if first <= 4 <= last:
            self_attention(nc, shared, "a1", qk_gain=None, **a1)
        if first <= 5 <= last:
            cross_attention(nc, shared, "x1", w["ctx"], **x1)
        with nc.Block() as block:
            @block.sync
            def _(sp):
                wait_loaded(sp, "f1")
        if first <= 6 <= last:
            attention_of_experts(nc, shared, "f1", **f1)
        stored = nc.alloc_semaphore("stored")
        with nc.Block() as block:
            @block.sync
            def _(sp):
                sp.dma_start(out.rearrange("b (t p) c -> p (b t) c", p=P), shared.x[:, :, :]).then_inc(stored, 16)
                sp.wait_ge(stored, 16)
                for layer in loads:
                    wait_loaded(sp, layer)


def laid_out(inputs):
    f = {k: np.asarray(v) for k, v in inputs.items()}

    def rows(w):
        return np.ascontiguousarray(w.reshape(-1, P, w.shape[1]).transpose(1, 0, 2))

    def per_head(w, bias):
        o = np.zeros((4, 2 * DH, 4, w.shape[0]), w.dtype)
        o[:, 0:DH] = w.T.reshape(4, 4, DH, w.shape[0]).transpose(1, 2, 0, 3)
        if bias is not None:
            o[0, DH, 0] = bias
        return o.reshape(P, 4, w.shape[0])

    mask = np.ones((4, 2 * DH, 4), f["L1_attn_head_mask"].dtype)
    mask[:, 0:DH] = f["L1_attn_head_mask"].reshape(4, 4).T[:, None, :]
    a = {
        "x": f["x"],
        "a0_wqkv": rows(f["L0_attn_w_qkv"].T),
        "a0_bqkv": f["L0_attn_b_qkv"],
        "a0_wo": per_head(f["L0_attn_w_proj"], f["L0_attn_b_proj"]),
        "a0_gain": np.stack([f["L0_attn_qn_w"], f["L0_attn_kn_w"]]),
        "a1_wqkv": rows(np.concatenate([f["L1_attn_Wq"], f["L1_attn_Wk"], f["L1_attn_Wv"]]).T),
        "a1_bqkv": np.concatenate([f["L1_attn_bq"], f["L1_attn_bk"], f["L1_attn_bv"]]),
        "a1_wo": per_head(f["L1_attn_Wo"], f["L1_attn_bo"]),
        "a1_head_mask": mask.reshape(P, 4),
        "bias_row": (np.arange(P) == DH).astype(np.float32).reshape(P, 1),
        "ctx": np.ascontiguousarray(f["ctx_1024"].reshape(B, SK, 2, P).transpose(3, 0, 2, 1)),
        "f0_wr": np.ascontiguousarray(f["L0_ffn_Wr"].reshape(N_ROUTED, C, 2, P).transpose(3, 2, 0, 1)),
        "f0_ws": np.ascontiguousarray(f["L0_ffn_Ws"].reshape(2, C, 2, P).transpose(3, 2, 0, 1)),
        "f0_centroids": rows(f["L0_ffn_centroids"].T),
        "f0_bias": f["L0_ffn_expert_biases"],
        "f0_wb": np.concatenate([f["L0_ffn_br"], f["L0_ffn_bs"]]),
        "f1_sim": rows(f["L1_ffn_sim_matrix"]),
        "f1_gates": f["L1_ffn_gates"],
        "f1_wo": np.ascontiguousarray(f["L1_ffn_o_proj"].transpose(1, 0, 2)),
        "x0_wq": rows(f["L0_xattn_Wq"].T),
        "x0_wkv": rows(np.concatenate([f["L0_xattn_Wk"], f["L0_xattn_Wv"]]).T),
        "x0_wo": per_head(f["L0_xattn_Wo"], f["L0_xattn_bo"]),
        "x0_gain": np.stack([f["L0_xattn_gq"], f["L0_xattn_gq"], f["L0_xattn_gk"]]),
        "x0_offset": np.stack([f["L0_xattn_bq"], f["L0_xattn_bq"], f["L0_xattn_bk"]]),
        "x1_wq": rows(f["L1_xattn_wq_w"].T),
        "x1_wkv": rows(np.concatenate([f["L1_xattn_wk_w"], f["L1_xattn_wv_w"]]).T),
        "x1_wo": per_head(f["L1_xattn_dense_w"], f["L1_xattn_dense_b"]),
        "x1_bqkv": np.concatenate([f["L1_xattn_wq_b"], f["L1_xattn_wk_b"], f["L1_xattn_wv_b"]]),
        "x1_mask": f["mask_1x1xSxS2_fk1"].reshape(S, SK),
    }
    for n in "qkv":
        a[f"f1_w{n}"] = np.ascontiguousarray(f[f"L1_ffn_{n}_proj"].reshape(N_ATTN, 2, P, P).transpose(2, 1, 0, 3))
    return a


def kernel(**inputs):
    import concourse.bacc as bacc
    from concourse.bass_utils import run_bass_kernel_spmd

    arrays = laid_out(inputs)
    nc = bacc.Bacc("TRN2", target_bir_lowering=False, num_devices=1)
    w = {n: nc.dram_tensor(f"in_{n}", a.shape, mybir.dt.from_np(a.dtype), kind="ExternalInput").ap() for n, a in arrays.items()}
    out = nc.dram_tensor("out_x", (B, S, C), fp32, kind="ExternalOutput").ap()
    decoder(nc, w, out)
    r = run_bass_kernel_spmd(nc, [{f"in_{n}": a for n, a in arrays.items()}], core_ids=[0])
    return r.results[0]["out_x"]
```

```python
import numpy as np
from contextlib import ExitStack, contextmanager

import concourse.bass as bass
from concourse import mybir

fp32 = mybir.dt.float32
bf16 = mybir.dt.bfloat16
ALU = mybir.AluOpType
ACT = mybir.ActivationFunctionType
AX = mybir.AxisListType

B, S, C = 8, 256, 256
SK = 77
H, DH = 16, 16
P = 128
T = B * S // P
PARTS = 6
LN_EPS = 1e-5
RMS_EPS = 1e-6
SCALE = DH ** -0.5
N_ROUTED = 16
N_ATTN = 8
TILES_OF = (slice(0, 1), slice(1, 3))
NORM_EPS = 1e-12
SK_PAD = 128
HEADS_OF = (slice(0, 2 * H), slice(2 * H, 3 * H))
FIRST_STEPS, LATER_STEPS = range(2), range(2, H // 2)
SPLIT_STEP = 9
LN_EXP_TABLES = "natural_log_exp_and_others"


class Signal:

    def __init__(self, sem, per_batch, opening=0):
        self.sem = sem
        self.per_batch = per_batch
        self.opening = opening

    def after(self, b, n):
        value = b * self.per_batch + n + self.opening
        assert isinstance(value, int) or value.min_val > 0
        return value


def wait_apart(engine):
    engine.nop(nofuse=True)


@contextmanager
def layer_block_of(nc, signals):
    with nc.Block() as block:
        yield block
    nc.clear_and_free_semaphores(signals)
    nc.all_engine_barrier()


def layer_block(ctx, nc, signals):
    return ctx.enter_context(layer_block_of(nc, signals))


def at(i, n=1):
    if isinstance(i, int):
        return slice(i, i + n)
    return bass.ds(i, n)




def tokens(b, t, n=1):
    return at(2 * (0 if isinstance(b, int) and b == B else b) + t, n)


def self_attention(nc, shared, name, wqkv, bqkv, wo, qk_gain, wait_late=None, start_others=None, at_end=None):
    x = shared.x
    with ExitStack() as ctx:
        def sb(n, shape, dt=fp32):
            return ctx.enter_context(nc.sbuf_tensor(f"{name}_{n}", shape, dt))

        def ps(n, shape, dt=fp32):
            return ctx.enter_context(nc.psum_tensor(f"{name}_{n}", shape, dt))

        signals = []

        def signal(n, per_batch, opening=0):
            signals.append(nc.alloc_semaphore(f"{name}_{n}"))
            return Signal(signals[-1], per_batch, opening)

        stats = sb("stats", [P, 2, 6])
        mean_var = sb("mean_var", [P, 2, 2])
        var_eps = sb("var_eps", [P, 2])
        rstd = sb("rstd", [P, 2])
        xn = shared.xn
        xn_t = sb("xn_t", [P, 2, S])
        qk = sb("qk", [P, 2, 2 * H, DH])
        qk_sq = sb("qk_sq", [P, 2, 2 * H, DH])
        head_ms = sb("head_ms", [P, 4 * H])
        head_ln = sb("head_ln", [P, 4 * H])
        head_rs = sb("head_rs", [P, 4 * H])
        rest = sb("rest", [P, 2, 2 * H, DH])
        parts = [sb(f"parts_{n}", [P, 2 * H, PARTS, DH], bf16) for n in "qk"]
        stacks = [[sb(f"stack_{n}{u}", [P, H, S], bf16) for n in "qk"] for u in range(2)]
        v = [sb(f"v{u}", [P, 2, H, 2 * DH]) for u in range(2)]
        neg_max = sb("neg_max", [P, 2, H])
        neg_max_parts = sb("neg_max_parts", [P, 2, 2, H], bf16)
        neg_max_t = sb("neg_max_t", [2 * H, S], bf16)
        probs = sb("probs", [P, 4, 2, 2, S])
        den = sb("den", [P, 2, 2, S])
        log_den = sb("log_den", [P, 2, 2, S])
        attn = sb("attn", [P, 2, 2, S])

        max_bank = [ps(f"max_bank{n}", [P, 2, S]) for n in range(2)]
        prob_bank = [ps(f"prob_bank{n}", [P, 2, 2, S]) for n in range(2)]
        work_bank = [ps(f"work_bank{n}", [P, 2, S]) for n in range(2)]

        def stack_bank(n):
            return prob_bank[(n // 2 + 1) % 2][:, n % 2].rearrange("p a s -> p (a s)").bitcast(bf16)\
                .rearrange("p (h s) -> p h s", h=4)

        def stack_rows(u, n):
            return stacks[u][1 - n // 4][0:PARTS * DH, 4 * (n % 4):4 * (n % 4) + 4, :]

        xn_bank = max_bank[0]
        v_bank = max_bank[1]
        neg_max_bank = max_bank[1][:, 0, 0:S // 2].bitcast(bf16)

        stats_done = signal("stats_done", 2)
        moments_done = signal("moments_done", 2)
        var_done = signal("var_done", 1)
        rstd_done = signal("rstd_done", 1)
        xn_done = signal("xn_done", 2)
        xn_t_in_psum = signal("xn_t_in_psum", 1)
        xn_t_done = signal("xn_t_done", 1)
        qk_in_psum = signal("qk_in_psum", 2)
        v_in_psum = signal("v_in_psum", 1)
        qk_done = signal("qk_done", 2)
        v_done = signal("v_done", 1)
        sq_done = signal("sq_done", 1)
        ms_done = signal("ms_done", 1)
        ln_ms_done = signal("ln_ms_done", 1)
        head_rs_done = signal("head_rs_done", 1)
        qk_scaled = signal("qk_scaled", 1)
        q_gained = signal("q_gained", 1)
        high_done = signal("high_done", 2)
        rest_done = signal("rest_done", 2)
        middle_done = signal("middle_done", 2)
        low_done = signal("low_done", 2)
        stack_in_psum = signal("stack_in_psum", 8)
        even_stack_done = signal("even_stack_done", 4)
        odd_stack_done = signal("odd_stack_done", 4)
        max_in_psum = signal("max_in_psum", H)
        max_done = signal("max_done", H)
        max_high_done = signal("max_high_done", 1)
        max_parts_done = signal("max_parts_done", 1)
        max_t_in_psum = signal("max_t_in_psum", 1)
        max_t_done = signal("max_t_done", 1)
        max_row_done = signal("max_row_done", 32)
        scores_in_psum = signal("scores_in_psum", H // 2)
        probs_done = signal("probs_done", H // 2, opening=1)
        attn_in_psum = signal("attn_in_psum", 4)
        den_done = signal("den_done", 2)
        log_done = signal("log_done", 2)
        recip_done = signal("recip_done", 2)
        attn_done = signal("attn_done", 2)
        out_in_psum = signal("out_in_psum", 1)
        x_done = signal("x_done", 1, opening=1)
        ones_done = signal("ones_done", 4)

        block = layer_block(ctx, nc, signals)

        @block.gpsimd
        def _(pool):
            def normalise(b):
                pool.wait_ge(moments_done.sem, moments_done.after(b, 2))
                wait_apart(pool)
                nc.gpsimd.tensor_scalar(var_eps[:, :], mean_var[:, :, 1], LN_EPS, None, ALU.add).then_inc(var_done.sem, 1)
                pool.wait_ge(var_done.sem, var_done.after(b, 1))
                nc.gpsimd.tensor_tensor(rstd[:, :], var_eps[:, :], shared.neg_half[:, 0:2], ALU.pow).then_inc(rstd_done.sem, 1)

            def split(b):
                for n in range(2):
                    pool.wait_ge(high_done.sem, high_done.after(b, n + 1))
                    high = parts[n][:, :, (0, 2)[n], :]
                    nc.gpsimd.tensor_tensor(rest[:, n], qk[:, n], high, ALU.subtract).then_inc(rest_done.sem, 1)
                for n in range(2):
                    pool.wait_ge(middle_done.sem, middle_done.after(b, n + 1))
                    nc.gpsimd.tensor_tensor(parts[n][:, :, (4, 1)[n], :], rest[:, n], parts[n][:, :, (3, 0)[n], :],
                                            ALU.subtract).then_inc(low_done.sem, 1)

            for done in (var_done, rstd_done):
                pool.sem_inc(done.sem, 1)
            normalise(1)
            pool.wait_ge(rstd_done.sem, rstd_done.after(1, 1))
            for u in range(2):
                nc.gpsimd.memset(stacks[u][1][PARTS * DH:P], 1.0).then_inc(ones_done.sem, 1)
                pool.wait_ge(ones_done.sem, 2 * u + 1)
                nc.gpsimd.memset(v[u][:, :, :, DH:2 * DH], 1.0).then_inc(ones_done.sem, 1)
                pool.wait_ge(ones_done.sem, 2 * u + 2)
            split(0)
            normalise(2)
            split(1)
            with pool.Fori(0, B - 3) as b:
                normalise(b + 3)
                split(b + 2)
            normalise(B)
            split(B - 1)
            if at_end:
                at_end(pool)

        @block.sync
        def _(sp):
            def max_row(b, u):
                sp.wait_ge(max_t_done.sem, max_t_done.after(b, 1))
                for part in range(2):
                    row = PARTS * DH + part
                    sp.dma_start(stacks[u][0][row:row + 1], neg_max_t[part * H:(part + 1) * H, :]).then_inc(max_row_done.sem, 16)

            if start_others:
                start_others(sp)
            with sp.Fori(0, B // 2) as pair:
                for u in range(2):
                    max_row(pair * 2 + u, u)
            sp.wait_ge(max_row_done.sem, max_row_done.after(B - 1, 32))

        @block.tensor
        def _(pe):
            def stacked(b, n):
                pe.wait_ge(even_stack_done.sem, even_stack_done.after(b, n))
                pe.wait_ge(odd_stack_done.sem, odd_stack_done.after(b, n))

            def transpose_xn(b):
                pe.wait_ge(xn_done.sem, xn_done.after(b, 2))
                for t in range(2):
                    for c in range(2):
                        last = nc.tensor.transpose(xn_bank[:, c, t * P:(t + 1) * P], xn[:, t, c * P:(c + 1) * P], shared.ident[:, :])
                last.then_inc(xn_t_in_psum.sem, 1)

            def project(b):
                pe.wait_ge(xn_t_done.sem, xn_t_done.after(b, 1))
                if isinstance(b, int) and b == 1:
                    pe.wait_ge(qk_done.sem, qk_done.after(b, 0))
                for t in range(2):
                    for c in range(2):
                        last = nc.tensor.matmul(prob_bank[1][:, t].rearrange("p a s -> p (a s)"), xn_t[:, c, t * P:(t + 1) * P],
                                                wqkv[:, c, 0:2 * C], start=(c == 0), stop=(c == 1))
                    last.then_inc(qk_in_psum.sem, 1)

            def values(b):
                for t in range(2):
                    for c in range(2):
                        last = nc.tensor.matmul(v_bank[:, t, :], xn_t[:, c, t * P:(t + 1) * P],
                                                wqkv[:, c, 2 * C:3 * C], start=(c == 0), stop=(c == 1))
                last.then_inc(v_in_psum.sem, 1)

            def stack(b, u):
                for n in range(8):
                    which = 1 - n // 4
                    pe.wait_ge(low_done.sem, low_done.after(b, 2))
                    if n >= 4:
                        done = (even_stack_done, odd_stack_done)[n % 2]
                        pe.wait_ge(done.sem, done.after(b, n // 2 - 1))
                    for h in range(4):
                        for t in range(2):
                            src = parts[which][:, t * H + 4 * (n % 4) + h].rearrange("p a d -> p (a d)")
                            last = nc.tensor.transpose(stack_bank(n)[0:PARTS * DH, h, t * P:(t + 1) * P], src, shared.ident_bf[:, :])
                    last.then_inc(stack_in_psum.sem, 1)

            def maxima(b, u, h):
                q, k = stacks[u]
                if h == 0:
                    stacked(b, 4)
                if h == 1:
                    pe.wait_ge(max_t_done.sem, max_t_done.after(b, 0))
                    pe.wait_ge(v_done.sem, v_done.after(b, 1))
                if h >= 2:
                    pe.wait_ge(max_done.sem, max_done.after(b, h - 1))
                for t in range(2):
                    last = nc.tensor.matmul(max_bank[h % 2][:, t, :], q[0:PARTS * DH, h, t * P:(t + 1) * P],
                                            k[0:PARTS * DH, h, :], start=True, stop=True)
                last.then_inc(max_in_psum.sem, 1)

            def max_transposed(b):
                pe.wait_ge(max_parts_done.sem, max_parts_done.after(b, 1))
                for t in range(2):
                    last = nc.tensor.transpose(neg_max_bank[0:2 * H, t * P:(t + 1) * P],
                                               neg_max_parts[:, t].rearrange("p a h -> p (a h)"), shared.ident_bf[:, :])
                last.then_inc(max_t_in_psum.sem, 1)

            def scores(b, u, p, left):
                q, k = stacks[u]
                if p == 0:
                    pe.wait_ge(max_row_done.sem, max_row_done.after(b, 32))
                    stacked(b, 4 * (1 + min(left, 1)))
                    pe.wait_ge(probs_done.sem, probs_done.after(b, 0))
                if p == 1:
                    pe.wait_ge(qk_done.sem, qk_done.after(b, 2 * (1 + min(left, 2))))
                if p >= 2:
                    pe.wait_ge(probs_done.sem, probs_done.after(b, p - 1))
                rows = PARTS * DH + 2
                for h in range(2):
                    for kt in range(2):
                        last = nc.tensor.matmul(prob_bank[p % 2][:, h, kt, :], k[0:rows, 2 * p + h, kt * P:(kt + 1) * P],
                                                q[0:rows, 2 * p + h, :], start=True, stop=True)
                last.then_inc(scores_in_psum.sem, 1)

            def weigh(b, u, g):
                if g % 2 == 0 and g == 0:
                    pe.wait_ge(v_done.sem, v_done.after(b, 1))
                pe.wait_ge(probs_done.sem, probs_done.after(b, 2 * g + 2))
                for kt in range(2):
                    for j in range(4):
                        h = 4 * g + j
                        last = nc.tensor.matmul(work_bank[g // 2][32 * j:32 * j + 32, g % 2, :], v[u][:, kt, h, :],
                                                probs[:, (h // 2) % 4, h % 2, kt, :], start=(kt == 0), stop=(kt == 1))
                last.then_inc(attn_in_psum.sem, 1)

            def output(b):
                pe.wait_ge(attn_done.sem, attn_done.after(b, 2))
                for t in range(2):
                    for g in range(4):
                        last = nc.tensor.matmul(work_bank[0][:, t, :], attn[:, g // 2, g % 2, t * P:(t + 1) * P], wo[:, g, :],
                                                start=(g == 0), stop=(g == 3))
                last.then_inc(out_in_psum.sem, 1)

            def main(b, u, steps, left=3):
                for p in steps:
                    scores(b, u, p, left)
                    if left >= 1:
                        maxima(b + 1, 1 - u, 2 * p)
                        maxima(b + 1, 1 - u, 2 * p + 1)
                    if p == 0 and not (isinstance(b, int) and b == 0):
                        output(b - 1)
                    if p == 2:
                        pe.wait_ge(x_done.sem, x_done.after(b, 0))
                    if p % 2 == 0 and p >= 2:
                        weigh(b, u, p // 2 - 1)

            def batch(b, u, left=3):
                main(b, u, LATER_STEPS, left)
                weigh(b, u, 3)
                if left >= 1:
                    pe.wait_ge(max_done.sem, max_done.after(b + 1, H))
                if left >= 2:
                    pe.wait_ge(probs_done.sem, probs_done.after(b, H // 2))
                    values(b + 2)
                    if left >= 3:
                        transpose_xn(b + 3)
                    stack(b + 2, u)
                    pe.wait_ge(v_done.sem, v_done.after(b + 2, 1))
                if left >= 1:
                    max_transposed(b + 1)
                if left >= 3:
                    stacked(b + 2, 3)
                    project(b + 3)
                if left >= 1:
                    main(b + 1, 1 - u, FIRST_STEPS, min(3, B - 2 - b) if isinstance(b, int) else 3)

            for opened in (probs_done, x_done):
                pe.sem_inc(opened.sem, 1)
            transpose_xn(0)
            project(0)
            values(0)
            transpose_xn(1)
            project(1)
            pe.wait_ge(qk_done.sem, qk_done.after(1, 2))
            stack(0, 0)
            pe.wait_ge(v_done.sem, v_done.after(0, 1))
            values(1)
            pe.wait_ge(v_done.sem, v_done.after(1, 1))
            for h in range(H):
                maxima(0, 0, h)
                if h == SPLIT_STEP:
                    stack(1, 1)
            pe.wait_ge(max_done.sem, max_done.after(0, H))
            transpose_xn(2)
            max_transposed(0)
            stacked(1, 3)
            project(2)
            pe.wait_ge(ones_done.sem, 4)
            if wait_late:
                wait_late(pe)
            main(0, 0, FIRST_STEPS)
            with pe.Fori(0, (B - 4) // 2) as pair:
                for u in range(2):
                    batch(pair * 2 + u, u)
            for b in range(B - 4, B):
                batch(b, b % 2, min(3, B - 1 - b))
            output(B - 1)

        @block.scalar
        def _(act):
            def xn_transposed(b):
                act.wait_ge(xn_t_in_psum.sem, xn_t_in_psum.after(b, 1))
                nc.scalar.activation(xn_t[:, :, :], xn_bank[:, :, :], ACT.Copy).then_inc(xn_t_done.sem, 1)

            def square(b):
                act.wait_ge(qk_done.sem, qk_done.after(b, 2))
                nc.scalar.activation(qk_sq[:, :], qk[:, :], ACT.Square).then_inc(sq_done.sem, 1)

            def head_rms(b):
                act.wait_ge(ms_done.sem, ms_done.after(b, 1))
                nc.scalar.activation(head_ln[:, :], head_ms[:, :], ACT.Ln, bias=shared.rms_eps[:, :], scale=1.0 / DH).then_inc(ln_ms_done.sem, 1)
                act.wait_ge(ln_ms_done.sem, ln_ms_done.after(b, 1))
                nc.scalar.activation(head_rs[:, :], head_ln[:, :], ACT.Exp, scale=-0.5).then_inc(head_rs_done.sem, 1)

            def high(b, which=(0, 1)):
                if qk_gain is not None:
                    act.wait_ge(qk_scaled.sem, qk_scaled.after(b, 1))
                    act.wait_ge(q_gained.sem, q_gained.after(b, 1))
                else:
                    act.wait_ge(qk_done.sem, qk_done.after(b, 2))
                for n in which:
                    first = (0, 2)[n]
                    nc.scalar.activation(parts[n][:, :, first:first + 3, :], qk[:, n].unsqueeze(2).broadcast_to([P, 2 * H, 3, DH]),
                                         ACT.Copy).then_inc(high_done.sem, 1)

            def even_stacks(b, u):
                for n in range(0, 8, 2):
                    act.wait_ge(stack_in_psum.sem, stack_in_psum.after(b, n + 1))
                    nc.scalar.activation(stack_rows(u, n), stack_bank(n)[0:PARTS * DH], ACT.Copy).then_inc(even_stack_done.sem, 1)

            def max_transposed(b):
                act.wait_ge(max_t_in_psum.sem, max_t_in_psum.after(b, 1))
                nc.scalar.activation(neg_max_t[:, :], neg_max_bank[0:2 * H, :], ACT.Copy).then_inc(max_t_done.sem, 1)

            def reciprocal(b, pair):
                act.wait_ge(den_done.sem, den_done.after(b, pair + 1))
                nc.scalar.activation(log_den[:, pair], den[:, pair], ACT.Ln).then_inc(log_done.sem, 1)
                act.wait_ge(log_done.sem, log_done.after(b, pair + 1))
                nc.scalar.activation(den[:, pair], log_den[:, pair], ACT.Exp, scale=-1.0).then_inc(recip_done.sem, 1)

            def batch(b, u, left=3):
                if left >= 2 and qk_gain is not None:
                    square(b + 2)
                for p in range(H // 2):
                    act.wait_ge(scores_in_psum.sem, scores_in_psum.after(b, p + 1))
                    if p >= 4:
                        act.wait_ge(attn_in_psum.sem, attn_in_psum.after(b, p // 2 - 1))
                    nc.scalar.activation(probs[:, p % 4], prob_bank[p % 2][:, :], ACT.Exp, scale=SCALE).then_inc(probs_done.sem, 1)
                    if left >= 2 and p == 1 and qk_gain is not None:
                        head_rms(b + 2)
                    if left >= 2 and p in (3, 4):
                        high(b + 2, (p - 3,))
                    if p == 6:
                        reciprocal(b, 0)
                reciprocal(b, 1)
                if left >= 3:
                    xn_transposed(b + 3)
                if left >= 2:
                    even_stacks(b + 2, u)
                if left >= 1:
                    max_transposed(b + 1)

            xn_transposed(0)
            if qk_gain is not None:
                square(0)
            xn_transposed(1)
            if qk_gain is not None:
                head_rms(0)
            high(0)
            if qk_gain is not None:
                square(1)
            even_stacks(0, 0)
            if qk_gain is not None:
                head_rms(1)
            act.wait_ge(stack_in_psum.sem, stack_in_psum.after(0, 8))
            high(1)
            even_stacks(1, 1)
            xn_transposed(2)
            max_transposed(0)
            with act.Fori(0, (B - 4) // 2) as pair:
                for u in range(2):
                    batch(pair * 2 + u, u)
            for b in range(B - 4, B):
                batch(b, b % 2, min(3, B - 1 - b))

        @block.vector
        def _(dve):
            def moments(b):
                for t in range(2):
                    nc.vector.bn_stats(stats[:, t], x[:, tokens(b, t), :]).then_inc(stats_done.sem, 1)
                for t in range(2):
                    dve.wait_ge(stats_done.sem, stats_done.after(b, t + 1))
                    wait_apart(dve)
                    nc.vector.bn_aggr(mean_var[:, t], stats[:, t]).then_inc(moments_done.sem, 1)

            def normalise(b):
                dve.wait_ge(rstd_done.sem, rstd_done.after(b, 1))
                dve.wait_ge(moments_done.sem, moments_done.after(b, 2))
                dve.wait_ge(xn_t_in_psum.sem, xn_t_in_psum.after(b, 0))
                for t in range(2):
                    nc.vector.tensor_scalar(xn[:, t], x[:, tokens(b, t), :], mean_var[:, t, 0:1], rstd[:, t:t + 1],
                                            ALU.subtract, ALU.mult).then_inc(xn_done.sem, 1)

            def projected(b):
                for t in range(2):
                    dve.wait_ge(qk_in_psum.sem, qk_in_psum.after(b, t + 1))
                    nc.vector.tensor_tensor(qk[:, :, t * H:(t + 1) * H, :],
                                            prob_bank[1][:, t].rearrange("p a (h d) -> p a h d", d=DH),
                                            bqkv[:, 0:2 * C].rearrange("p (a h d) -> p a h d", a=2, d=DH), ALU.add).then_inc(qk_done.sem, 1)

            def values(b, u):
                dve.wait_ge(v_in_psum.sem, v_in_psum.after(b, 1))
                bias = bqkv[:, 2 * C:3 * C].rearrange("p (h d) -> p h d", d=DH).unsqueeze(1).broadcast_to([P, 2, H, DH])
                nc.vector.tensor_tensor(v[u][:, :, :, 0:DH], v_bank[:, :, :].rearrange("p t (h d) -> p t h d", d=DH), bias, ALU.add)\
                    .then_inc(v_done.sem, 1)

            def head_ms_sum(b):
                dve.wait_ge(sq_done.sem, sq_done.after(b, 1))
                nc.vector.tensor_reduce(head_ms[:, :], qk_sq[:, :].rearrange("p a h d -> p (a h) d"), AX.X, ALU.add).then_inc(ms_done.sem, 1)

            def head_rms(b):
                dve.wait_ge(head_rs_done.sem, head_rs_done.after(b, 1))
                qk_all = qk[:, :].rearrange("p a h d -> p (a h) d")
                nc.vector.tensor_tensor(qk_all, qk_all, head_rs[:, :].unsqueeze(2).broadcast_to([P, 4 * H, DH]), ALU.mult)\
                    .then_inc(qk_scaled.sem, 1)

            def gain_q(b):
                dve.wait_ge(qk_scaled.sem, qk_scaled.after(b, 1))
                nc.vector.tensor_tensor(qk[:, 0], qk[:, 0], qk_gain[:, :].unsqueeze(1).broadcast_to([P, 2 * H, DH]), ALU.mult)\
                    .then_inc(q_gained.sem, 1)

            def middle(b, which=(0, 1)):
                for n in which:
                    dve.wait_ge(rest_done.sem, rest_done.after(b, n + 1))
                    first, step = ((3, 2), (0, 5))[n]
                    nc.vector.tensor_copy(parts[n][:, :, first:6:step, :], rest[:, n].unsqueeze(2).broadcast_to([P, 2 * H, 2, DH]))\
                        .then_inc(middle_done.sem, 1)

            def odd_stacks(b, u):
                for n in range(1, 8, 2):
                    dve.wait_ge(stack_in_psum.sem, stack_in_psum.after(b, n + 1))
                    nc.vector.tensor_copy(stack_rows(u, n), stack_bank(n)[0:PARTS * DH]).then_inc(odd_stack_done.sem, 1)

            def maximum(b, h):
                dve.wait_ge(max_in_psum.sem, max_in_psum.after(b, h + 1))
                nc.vector.tensor_reduce(neg_max[:, :, h], max_bank[h % 2][:, :, :], AX.X, ALU.max, negate=True).then_inc(max_done.sem, 1)

            def max_parts(b):
                dve.wait_ge(max_done.sem, max_done.after(b, H))
                nc.vector.tensor_copy(neg_max_parts[:, :, 0, :], neg_max[:, :, :]).then_inc(max_high_done.sem, 1)
                dve.wait_ge(max_high_done.sem, max_high_done.after(b, 1))
                nc.vector.tensor_tensor(neg_max_parts[:, :, 1, :], neg_max[:, :, :], neg_max_parts[:, :, 0, :], ALU.subtract)\
                    .then_inc(max_parts_done.sem, 1)

            def denominator(b, pair):
                dve.wait_ge(attn_in_psum.sem, attn_in_psum.after(b, 2 * pair + 2))
                wait_apart(dve)
                nc.vector.stream_shuffle(den[:, pair], work_bank[pair][:, :, :], [DH] * 32).then_inc(den_done.sem, 1)

            def divide(b, pair):
                dve.wait_ge(recip_done.sem, recip_done.after(b, pair + 1))
                nc.vector.tensor_tensor(attn[:, pair], work_bank[pair][:, :, :], den[:, pair], ALU.mult).then_inc(attn_done.sem, 1)

            def residual(b):
                dve.wait_ge(out_in_psum.sem, out_in_psum.after(b, 1))
                xb = x[:, at(2 * b, 2), :]
                nc.vector.tensor_tensor(xb, work_bank[0][:, :, :], xb, ALU.add).then_inc(x_done.sem, 1)

            def main(b, u, steps, left=3):
                for p in steps:
                    if p == 0 and (left >= 3 or b + 3 == B):
                        moments(b + 3)
                    if left >= 1:
                        maximum(b + 1, 2 * p)
                        maximum(b + 1, 2 * p + 1)
                    if left >= 2 and qk_gain is not None:
                        if p == 0:
                            head_ms_sum(b + 2)
                        if p == 1:
                            head_rms(b + 2)
                        if p == 2:
                            gain_q(b + 2)
                    if p == 0 and not (isinstance(b, int) and b == 0):
                        residual(b - 1)
                    if p == 3 and (left >= 3 or b + 3 == B):
                        normalise(b + 3)
                    if left >= 2 and p in (6, 7):
                        middle(b + 2, (p - 6,))
                    if p == 5:
                        denominator(b, 0)
                    if p == 7:
                        divide(b, 0)

            def batch(b, u, left=3):
                main(b, u, LATER_STEPS, left)
                if left >= 1:
                    max_parts(b + 1)
                denominator(b, 1)
                if left >= 2:
                    values(b + 2, u)
                divide(b, 1)
                if left >= 2:
                    odd_stacks(b + 2, u)
                if left >= 3:
                    projected(b + 3)
                if left >= 1:
                    main(b + 1, 1 - u, FIRST_STEPS, min(3, B - 2 - b) if isinstance(b, int) else 3)

            for done in (stats_done, moments_done, xn_done):
                dve.sem_inc(done.sem, 2)
            moments(1)
            normalise(1)
            projected(0)
            values(0, 0)
            if qk_gain is not None:
                head_ms_sum(0)
                head_rms(0)
                gain_q(0)
            middle(0)
            projected(1)
            if qk_gain is not None:
                head_ms_sum(1)
            odd_stacks(0, 0)
            if wait_late:
                wait_late(dve)
            moments(2)
            values(1, 1)
            if qk_gain is not None:
                head_rms(1)
                gain_q(1)
            normalise(2)
            for h in range(H):
                maximum(0, h)
                if h == SPLIT_STEP - 3:
                    middle(1)
                if h == SPLIT_STEP:
                    odd_stacks(1, 1)
            max_parts(0)
            projected(2)
            main(0, 0, FIRST_STEPS)
            with dve.Fori(0, (B - 4) // 2) as pair:
                for u in range(2):
                    batch(pair * 2 + u, u)
            for b in range(B - 4, B):
                batch(b, b % 2, min(3, B - 1 - b))
            residual(B - 1)


def cross_attention(nc, shared, name, ctx_dram, wq, wkv, wo, bqkv=None, mask=None, gain=None, offset=None, at_end=None):
    x = shared.x
    masked = mask is not None
    with ExitStack() as ctx:
        def sb(n, shape, dt=fp32):
            return ctx.enter_context(nc.sbuf_tensor(f"{name}_{n}", shape, dt))

        def ps(n, shape, dt=fp32):
            return ctx.enter_context(nc.psum_tensor(f"{name}_{n}", shape, dt))

        signals = []

        def signal(n, per_batch, opening=0):
            signals.append(nc.alloc_semaphore(f"{name}_{n}"))
            return Signal(signals[-1], per_batch, opening)

        stats = sb("stats", [P, 2, 6])
        mean_var = sb("mean_var", [P, 2, 2])
        var_eps = sb("var_eps", [P, 2])
        rstd = sb("rstd", [P, 2])
        xn = shared.xn
        xn_t = sb("xn_t", [P, 2, S])
        ctx_t = [sb(f"ctx_t{u}", [P, 2, SK]) for u in range(2)]
        qk = [sb(f"qk{u}", [P, 3 * H, DH]) for u in range(2)]
        qk_sq = sb("qk_sq", [P, 3 * H, DH])
        head_sum = sb("head_sum", [P, 3 * H])
        head_ss = sb("head_ss", [P, 3 * H])
        head_ln = sb("head_ln", [P, 3 * H])
        head_rs = sb("head_rs", [P, 3 * H])
        rest = sb("rest", [P, 3 * H, DH])
        parts = [sb("parts_q", [P, 2 * H, PARTS, DH], bf16), sb("parts_k", [P, H, PARTS, DH], bf16)]
        q_stack = sb("q_stack", [PARTS * DH, H, S], bf16)
        k_stack = sb("k_stack", [PARTS * DH, H, SK], bf16)
        v = [sb(f"v{u}", [SK, H, 2 * DH]) for u in range(2)]
        masked_scores = sb("masked_scores", [P, 2, H, SK])
        neg_max = sb("neg_max", [P, 2, H])
        shifted = sb("shifted", [P, 2, H, SK])
        exps = sb("exps", [P, 2, H, SK])
        probs = sb("probs", [SK, H, S])
        den = sb("den", [P, 2, 2, S])
        log_den = sb("log_den", [P, 2, 2, S])
        attn = sb("attn", [P, 2, 2, S])

        ring = [ps(f"ring{n}", [P, 2, 2 * S]) for n in range(2)]
        work_bank = [ps(f"work_bank{n}", [P, 2, S]) for n in range(2)]
        q_bank = ps("q_bank", [P, 2, S])
        kv_bank = ps("kv_bank", [P, 2 * C])

        loaded = [signal(f"ctx_loaded{u}", 16) for u in range(2)]
        zeros_done = signal("zeros_done", 4)
        stats_done = signal("stats_done", 2)
        moments_done = signal("moments_done", 2)
        var_done = signal("var_done", 1)
        rstd_done = signal("rstd_done", 1)
        xn_done = signal("xn_done", 2)
        xn_t_in_psum = signal("xn_t_in_psum", 1)
        xn_t_done = signal("xn_t_done", 1)
        k_in_psum = signal("k_in_psum", 1)
        v_in_psum = signal("v_in_psum", 1)
        q_in_psum = signal("q_in_psum", 1)
        qk_done = signal("qk_done", 2)
        v_done = signal("v_done", 1)
        sum_done = signal("sum_done", 1)
        centred = signal("centred", 1)
        sq_done = signal("sq_done", 1)
        ss_done = signal("ss_done", 1)
        ln_done = signal("ln_done", 1)
        head_rs_done = signal("head_rs_done", 1)
        scaled = signal("scaled", 1)
        gained = signal("gained", 1)
        normed = signal("normed", 1)
        high_done = signal("high_done", 2)
        rest_done = signal("rest_done", 2)
        middle_done = signal("middle_done", 2)
        low_done = signal("low_done", 2)
        k_stack_in_psum = signal("k_stack_in_psum", 1)
        q_stack_in_psum = signal("q_stack_in_psum", 2)
        k_stack_done = signal("k_stack_done", 1)
        q_low_stack_done = signal("q_low_stack_done", 1)
        q_high_stack_done = signal("q_high_stack_done", 1)
        scores_in_psum = signal("scores_in_psum", 4)
        masked_done = signal("masked_done", 4)
        max_done = signal("max_done", 4)
        shifted_done = signal("shifted_done", 4)
        exps_done = signal("exps_done", 4)
        probs_in_psum = signal("probs_in_psum", 4)
        probs_done = signal("probs_done", 4, opening=1)
        attn_in_psum = signal("attn_in_psum", 4)
        den_done = signal("den_done", 2)
        log_done = signal("log_done", 2)
        recip_done = signal("recip_done", 2)
        attn_done = signal("attn_done", 2)
        out_in_psum = signal("out_in_psum", 1)
        x_done = signal("x_done", 1, opening=1)

        qk_ready = qk_done if masked else normed
        n_qk_ready = 2 if masked else 1

        block = layer_block(ctx, nc, signals)

        @block.sync
        def _(sp):
            for u in range(2):
                sp.dma_start(ctx_t[u][:, :, :], ctx_dram[:, u]).then_inc(loaded[u].sem, 16)
            with sp.Fori(0, (B - 2) // 2) as pair:
                for u in range(2):
                    b = pair * 2 + u
                    sp.wait_ge(v_in_psum.sem, v_in_psum.after(b, 1))
                    sp.dma_start(ctx_t[u][:, :, :], ctx_dram[:, at(b + 2), :, :].rearrange("p o a s -> p (o a) s"))\
                        .then_inc(loaded[u].sem, 16)
            for u in range(2):
                sp.wait_ge(loaded[u].sem, 16 * B // 2)

        @block.gpsimd
        def _(pool):
            def normalise(b):
                pool.wait_ge(moments_done.sem, moments_done.after(b, 2))
                wait_apart(pool)
                nc.gpsimd.tensor_scalar(var_eps[:, :], mean_var[:, :, 1], LN_EPS, None, ALU.add).then_inc(var_done.sem, 1)
                pool.wait_ge(var_done.sem, var_done.after(b, 1))
                nc.gpsimd.tensor_tensor(rstd[:, :], var_eps[:, :], shared.neg_half[:, 0:2], ALU.pow).then_inc(rstd_done.sem, 1)

            def split_rest(b, u):
                for n in range(2):
                    pool.wait_ge(high_done.sem, high_done.after(b, n + 1))
                    nc.gpsimd.tensor_tensor(rest[:, HEADS_OF[n]], qk[u][:, HEADS_OF[n]], parts[n][:, :, (0, 2)[n], :], ALU.subtract)\
                        .then_inc(rest_done.sem, 1)

            def split_low(b):
                for n in range(2):
                    pool.wait_ge(middle_done.sem, middle_done.after(b, n + 1))
                    nc.gpsimd.tensor_tensor(parts[n][:, :, (4, 1)[n], :], rest[:, HEADS_OF[n]], parts[n][:, :, (3, 0)[n], :],
                                            ALU.subtract).then_inc(low_done.sem, 1)

            def shift(b):
                for n in range(4):
                    t, half = n % 2, n // 2
                    heads = slice(8 * half, 8 * half + 8)
                    pool.wait_ge(max_done.sem, max_done.after(b, n + 1))
                    nc.gpsimd.tensor_tensor(shifted[:, t, heads, :], masked_scores[:, t, heads, :],
                                            neg_max[:, t, heads].unsqueeze(2).broadcast_to([P, 8, SK]), ALU.add)\
                        .then_inc(shifted_done.sem, 1)

            def batch(b, u, left=4):
                if masked:
                    shift(b)
                    if left >= 1:
                        split_low(b + 1)
                if left >= 4 or b + 4 == B:
                    normalise(b + 4)
                if left >= 2:
                    split_rest(b + 2, u)
                    if not masked:
                        split_low(b + 2)

            for u in range(2):
                nc.gpsimd.memset(qk[u][:, 2 * H:3 * H, :], 0.0).then_inc(zeros_done.sem, 1)
                pool.wait_ge(zeros_done.sem, 2 * u + 1)
                nc.gpsimd.memset(v[u][:, :, DH:2 * DH], 1.0 if masked else 0.0).then_inc(zeros_done.sem, 1)
                pool.wait_ge(zeros_done.sem, 2 * u + 2)
            for done in (var_done, rstd_done):
                pool.sem_inc(done.sem, 1)
            normalise(1)
            split_rest(0, 0)
            split_low(0)
            normalise(2)
            split_rest(1, 1)
            if not masked:
                split_low(1)
            normalise(3)
            with pool.Fori(0, (B - 4) // 2) as pair:
                for u in range(2):
                    batch(pair * 2 + u, u)
            for b in range(B - 4, B):
                batch(b, b % 2, B - 1 - b)
            if at_end:
                at_end(pool)

        @block.tensor
        def _(pe):
            def keys(b, u, values_before):
                pe.wait_ge(loaded[u].sem, 8 * (b - u) + 16)
                pe.wait_ge(v_done.sem, v_done.after(values_before, 0))
                pe.wait_ge(qk_done.sem, qk_done.after(b, 0))
                for c in range(2):
                    last = nc.tensor.matmul(kv_bank[0:SK, 0:C], ctx_t[u][:, c, :], wkv[:, c, 0:C], start=(c == 0), stop=(c == 1))
                last.then_inc(k_in_psum.sem, 1)

            def values(b, u, keys_before):
                pe.wait_ge(qk_done.sem, qk_done.after(keys_before, 2))
                for c in range(2):
                    last = nc.tensor.matmul(kv_bank[0:SK, C:2 * C], ctx_t[u][:, c, :], wkv[:, c, C:2 * C], start=(c == 0), stop=(c == 1))
                last.then_inc(v_in_psum.sem, 1)

            def transpose_xn(b):
                pe.wait_ge(xn_done.sem, xn_done.after(b, 2))
                pe.wait_ge(qk_done.sem, qk_done.after(b, 0))
                for t in range(2):
                    for c in range(2):
                        last = nc.tensor.transpose(q_bank[:, c, t * P:(t + 1) * P], xn[:, t, c * P:(c + 1) * P], shared.ident[:, :])
                last.then_inc(xn_t_in_psum.sem, 1)

            def queries(b):
                pe.wait_ge(xn_t_done.sem, xn_t_done.after(b, 1))
                for t in range(2):
                    for c in range(2):
                        last = nc.tensor.matmul(q_bank[:, t, :], xn_t[:, c, t * P:(t + 1) * P], wq[:, c, :], start=(c == 0), stop=(c == 1))
                last.then_inc(q_in_psum.sem, 1)

            def stack(b):
                pe.wait_ge(low_done.sem, low_done.after(b, 2))
                out = ring[0][:, :, :].bitcast(bf16)
                for h in range(H):
                    last = nc.tensor.transpose(out[0:PARTS * DH, h // 8, SK_PAD * (h % 8):SK_PAD * (h % 8) + SK],
                                               parts[1][0:SK, h].rearrange("p a d -> p (a d)"), shared.ident_bf[0:SK, 0:SK])
                last.then_inc(k_stack_in_psum.sem, 1)
                for half in range(2):
                    if half == 1:
                        pe.wait_ge(k_stack_done.sem, k_stack_done.after(b, 1))
                    out = ring[1 - half][:, :, :].bitcast(bf16)
                    for h in range(8):
                        for t in range(2):
                            last = nc.tensor.transpose(out[0:PARTS * DH, h // 4, S * (h % 4) + t * P:S * (h % 4) + (t + 1) * P],
                                                       parts[0][:, t * H + 8 * half + h].rearrange("p a d -> p (a d)"), shared.ident_bf[:, :])
                    last.then_inc(q_stack_in_psum.sem, 1)

            def stacks_ready(b):
                pe.wait_ge(k_stack_done.sem, k_stack_done.after(b, 1))
                pe.wait_ge(q_low_stack_done.sem, q_low_stack_done.after(b, 1))
                pe.wait_ge(q_high_stack_done.sem, q_high_stack_done.after(b, 1))

            def sigmoid_scores(b, n):
                if n >= 2:
                    pe.wait_ge(probs_done.sem, probs_done.after(b, n - 1))
                for h in range(4):
                    last = nc.tensor.matmul(ring[n % 2][0:SK, h // 2, S * (h % 2):S * (h % 2) + S], k_stack[:, 4 * n + h, :],
                                            q_stack[:, 4 * n + h, :], start=True, stop=True)
                last.then_inc(scores_in_psum.sem, 1)

            def softmax_scores(b, n):
                t, half = n % 2, n // 2
                if n == 0:
                    pe.wait_ge(probs_done.sem, probs_done.after(b, 0))
                if n >= 2:
                    pe.wait_ge(masked_done.sem, masked_done.after(b, n - 1))
                for h in range(8):
                    last = nc.tensor.matmul(ring[n % 2][:, h // 4, P * (h % 4):P * (h % 4) + SK],
                                            q_stack[:, 8 * half + h, t * P:(t + 1) * P], k_stack[:, 8 * half + h, :],
                                            start=True, stop=True)
                last.then_inc(scores_in_psum.sem, 1)

            def transpose_probs(b, n):
                pe.wait_ge(exps_done.sem, exps_done.after(b, 2 * (n // 2) + 2))
                if n == 0:
                    pe.wait_ge(masked_done.sem, masked_done.after(b, 4))
                if n == 1:
                    pe.wait_ge(masked_done.sem, masked_done.after(b, 4))
                if n >= 2:
                    pe.wait_ge(probs_done.sem, probs_done.after(b, n - 1))
                for h in range(4):
                    for t in range(2):
                        last = nc.tensor.transpose(ring[1 - n % 2][0:SK, h // 2, S * (h % 2) + t * P:S * (h % 2) + (t + 1) * P],
                                                   exps[:, t, 4 * n + h, :], shared.ident[:, :])
                last.then_inc(probs_in_psum.sem, 1)

            def weigh(b, u, g):
                if g == 0:
                    pe.wait_ge(x_done.sem, x_done.after(b, 0))
                    pe.wait_ge(v_done.sem, v_done.after(b, 1))
                pe.wait_ge(probs_done.sem, probs_done.after(b, g + 1))
                for j in range(4):
                    last = nc.tensor.matmul(work_bank[g // 2][32 * j:32 * j + 32, g % 2, :], v[u][:, 4 * g + j, :],
                                            probs[:, 4 * g + j, :], start=True, stop=True)
                last.then_inc(attn_in_psum.sem, 1)

            def output(b):
                pe.wait_ge(attn_done.sem, attn_done.after(b, 2))
                for t in range(2):
                    for g in range(4):
                        last = nc.tensor.matmul(work_bank[0][:, t, :], attn[:, g // 2, g % 2, t * P:(t + 1) * P], wo[:, g, :],
                                                start=(g == 0), stop=(g == 3))
                last.then_inc(out_in_psum.sem, 1)

            scores = softmax_scores if masked else sigmoid_scores

            def first_scores(b):
                stacks_ready(b)
                scores(b, 0)
                scores(b, 1)

            def batch(b, u, left=4):
                if left >= 3:
                    transpose_xn(b + 3)
                scores(b, 2)
                if not masked:
                    weigh(b, u, 0)
                scores(b, 3)
                if not masked:
                    weigh(b, u, 1)
                if left >= 3:
                    keys(b + 3, 1 - u, b + 2)
                    queries(b + 3)
                if masked:
                    for n in range(4):
                        transpose_probs(b, n)
                        if n >= 1:
                            weigh(b, u, n - 1)
                    weigh(b, u, 3)
                else:
                    weigh(b, u, 2)
                    weigh(b, u, 3)
                if left >= 1:
                    pe.wait_ge(probs_done.sem, probs_done.after(b, 4))
                    stack(b + 1)
                if left >= 2:
                    values(b + 2, u, b + 2 + min(left - 2, 1))
                if left >= 1:
                    first_scores(b + 1)
                output(b)

            for opened in (probs_done, x_done):
                pe.sem_inc(opened.sem, 1)
            keys(0, 0, 0)
            for b in range(2):
                transpose_xn(b)
                queries(b)
            values(0, 0, 0)
            keys(1, 1, 1)
            values(1, 1, 1)
            stack(0)
            if masked:
                first_scores(0)
            keys(2, 0, 2)
            transpose_xn(2)
            queries(2)
            pe.wait_ge(zeros_done.sem, 4)
            if not masked:
                first_scores(0)
            with pe.Fori(0, (B - 4) // 2) as pair:
                for u in range(2):
                    batch(pair * 2 + u, u)
            for b in range(B - 4, B):
                batch(b, b % 2, B - 1 - b)

        @block.scalar
        def _(act):
            def xn_transposed(b):
                act.wait_ge(xn_t_in_psum.sem, xn_t_in_psum.after(b, 1))
                nc.scalar.activation(xn_t[:, :, :], q_bank[:, :, :], ACT.Copy).then_inc(xn_t_done.sem, 1)

            def projected(b, u):
                act.wait_ge(q_in_psum.sem, q_in_psum.after(b, 1))
                if not (isinstance(b, int) and b < 2):
                    act.wait_ge(rest_done.sem, rest_done.after(b - 1, 0))
                nc.scalar.activation(qk[u][:, 0:2 * H, :], q_bank[:, :, :].rearrange("p t (h d) -> p (t h) d", d=DH), ACT.Copy)\
                    .then_inc(qk_done.sem, 1)
                act.wait_ge(k_in_psum.sem, k_in_psum.after(b, 1))
                nc.scalar.activation(qk[u][0:SK, 2 * H:3 * H, :], kv_bank[0:SK, 0:C].rearrange("p (h d) -> p h d", d=DH), ACT.Copy)\
                    .then_inc(qk_done.sem, 1)

            def square(b, u):
                act.wait_ge(centred.sem, centred.after(b, 1))
                nc.scalar.activation(qk_sq[:, :, :], qk[u][:, :, :], ACT.Square).then_inc(sq_done.sem, 1)

            def head_rs_of(b):
                act.wait_ge(ss_done.sem, ss_done.after(b, 1))
                act.wait_ge(scaled.sem, scaled.after(b, 0))
                wait_apart(act)
                nc.scalar.preload_act_table_set(LN_EXP_TABLES)
                nc.scalar.activation(head_ln[:, :], head_ss[:, :], ACT.Ln, bias=shared.ln_eps[:, :], scale=1.0 / DH).then_inc(ln_done.sem, 1)
                act.wait_ge(ln_done.sem, ln_done.after(b, 1))
                nc.scalar.activation(head_rs[:, :], head_ln[:, :], ACT.Exp, scale=-0.5).then_inc(head_rs_done.sem, 1)

            def high(b, u):
                act.wait_ge(qk_ready.sem, qk_ready.after(b, n_qk_ready))
                if not (isinstance(b, int) and b == 0):
                    act.wait_ge(q_stack_in_psum.sem, q_stack_in_psum.after(b - 1, 2))
                for n in range(2):
                    first = (0, 2)[n]
                    heads = (2 * H, H)[n]
                    nc.scalar.activation(parts[n][:, :, first:first + 3, :], qk[u][:, HEADS_OF[n]].unsqueeze(2).broadcast_to([P, heads, 3, DH]),
                                         ACT.Copy).then_inc(high_done.sem, 1)

            def stack_k(b):
                act.wait_ge(k_stack_in_psum.sem, k_stack_in_psum.after(b, 1))
                src = ring[0][:, :, :].bitcast(bf16)[0:PARTS * DH].rearrange("p a (h s) -> p (a h) s", s=SK_PAD)
                nc.scalar.activation(k_stack[:, :, :], src[:, :, 0:SK], ACT.Copy).then_inc(k_stack_done.sem, 1)

            def sigmoids(b, which):
                for n in which:
                    act.wait_ge(scores_in_psum.sem, scores_in_psum.after(b, n + 1))
                    nc.scalar.activation(probs[:, 4 * n:4 * n + 4, :], ring[n % 2][0:SK].rearrange("p a (h s) -> p (a h) s", s=S),
                                         ACT.Sigmoid, scale=SCALE).then_inc(probs_done.sem, 1)

            def copy_attn(b):
                for pair in range(2):
                    act.wait_ge(attn_in_psum.sem, attn_in_psum.after(b, 2 * pair + 2))
                    nc.scalar.activation(attn[:, pair], work_bank[pair][:, :, :], ACT.Identity, bias=shared.bias_row[:, :]).then_inc(attn_done.sem, 1)

            def exponentials(b, n):
                t, half = n % 2, n // 2
                heads = slice(8 * half, 8 * half + 8)
                act.wait_ge(shifted_done.sem, shifted_done.after(b, n + 1))
                nc.scalar.activation(exps[:, t, heads, :], shifted[:, t, heads, :], ACT.Exp).then_inc(exps_done.sem, 1)

            def copy_probs(b, n):
                act.wait_ge(probs_in_psum.sem, probs_in_psum.after(b, n + 1))
                nc.scalar.activation(probs[:, 4 * n:4 * n + 4, :], ring[1 - n % 2][0:SK].rearrange("p a (h s) -> p (a h) s", s=S),
                                     ACT.Copy).then_inc(probs_done.sem, 1)

            def reciprocal(b, pair):
                act.wait_ge(den_done.sem, den_done.after(b, pair + 1))
                nc.scalar.activation(log_den[:, pair], den[:, pair], ACT.Ln).then_inc(log_done.sem, 1)
                act.wait_ge(log_done.sem, log_done.after(b, pair + 1))
                nc.scalar.activation(den[:, pair], log_den[:, pair], ACT.Exp, scale=-1.0).then_inc(recip_done.sem, 1)

            def batch(b, u, left=4):
                if masked:
                    if left >= 3:
                        xn_transposed(b + 3)
                    for n in range(3):
                        exponentials(b, n)
                    copy_probs(b, 0)
                    exponentials(b, 3)
                    for n in range(1, 4):
                        copy_probs(b, n)
                    reciprocal(b, 0)
                    if left >= 1:
                        stack_k(b + 1)
                    reciprocal(b, 1)
                else:
                    sigmoids(b, (0, 1))
                    if left >= 2:
                        square(b + 2, u)
                    if left >= 3:
                        xn_transposed(b + 3)
                    sigmoids(b, (2, 3))
                    if left >= 2:
                        head_rs_of(b + 2)
                    if left >= 3:
                        projected(b + 3, 1 - u)
                    copy_attn(b)
                    if left >= 1:
                        stack_k(b + 1)
                if left >= 2:
                    high(b + 2, u)

            act.wait_ge(zeros_done.sem, 4)
            xn_transposed(0)
            if masked:
                high(0, 0)
                xn_transposed(1)
            else:
                projected(0, 0)
                xn_transposed(1)
                square(0, 0)
                head_rs_of(0)
                projected(1, 1)
                high(0, 0)
                square(1, 1)
                head_rs_of(1)
            stack_k(0)
            if masked:
                xn_transposed(2)
            high(1, 1)
            if not masked:
                xn_transposed(2)
                projected(2, 0)
            with act.Fori(0, (B - 4) // 2) as pair:
                for u in range(2):
                    batch(pair * 2 + u, u)
            for b in range(B - 4, B):
                batch(b, b % 2, B - 1 - b)

        @block.vector
        def _(dve):
            def moments(b):
                for t in range(2):
                    nc.vector.bn_stats(stats[:, t], x[:, tokens(b, t), :]).then_inc(stats_done.sem, 1)
                for t in range(2):
                    dve.wait_ge(stats_done.sem, stats_done.after(b, t + 1))
                    wait_apart(dve)
                    nc.vector.bn_aggr(mean_var[:, t], stats[:, t]).then_inc(moments_done.sem, 1)

            def normalise(b):
                dve.wait_ge(rstd_done.sem, rstd_done.after(b, 1))
                dve.wait_ge(moments_done.sem, moments_done.after(b, 2))
                dve.wait_ge(xn_t_in_psum.sem, xn_t_in_psum.after(b, 0))
                for t in range(2):
                    nc.vector.tensor_scalar(xn[:, t], x[:, tokens(b, t), :], mean_var[:, t, 0:1], rstd[:, t:t + 1],
                                            ALU.subtract, ALU.mult).then_inc(xn_done.sem, 1)

            def values(b, u):
                dve.wait_ge(v_in_psum.sem, v_in_psum.after(b, 1))
                v_src = kv_bank[0:SK, C:2 * C].rearrange("p (h d) -> p h d", d=DH)
                if masked:
                    nc.vector.tensor_tensor(v[u][:, :, 0:DH], v_src, bqkv[0:SK, 2 * C:3 * C].rearrange("p (h d) -> p h d", d=DH), ALU.add)\
                        .then_inc(v_done.sem, 1)
                else:
                    nc.vector.tensor_copy(v[u][:, :, 0:DH], v_src).then_inc(v_done.sem, 1)

            def projected(b, u):
                dve.wait_ge(k_in_psum.sem, k_in_psum.after(b, 1))
                if not (isinstance(b, int) and b < 2):
                    dve.wait_ge(rest_done.sem, rest_done.after(b - 1, 0))
                nc.vector.tensor_tensor(qk[u][0:SK, 2 * H:3 * H, :], kv_bank[0:SK, 0:C].rearrange("p (h d) -> p h d", d=DH),
                                        bqkv[0:SK, C:2 * C].rearrange("p (h d) -> p h d", d=DH), ALU.add).then_inc(qk_done.sem, 1)
                dve.wait_ge(q_in_psum.sem, q_in_psum.after(b, 1))
                nc.vector.tensor_tensor(qk[u][:, 0:2 * H, :].rearrange("p (t h) d -> p t (h d)", t=2), q_bank[:, :, :],
                                        bqkv[:, 0:C].unsqueeze(1).broadcast_to([P, 2, C]), ALU.add).then_inc(qk_done.sem, 1)

            def centre(b, u):
                dve.wait_ge(qk_done.sem, qk_done.after(b, 2))
                nc.vector.tensor_reduce(head_sum[:, :], qk[u][:, :, :], AX.X, ALU.add).then_inc(sum_done.sem, 1)
                dve.wait_ge(sum_done.sem, sum_done.after(b, 1))
                nc.vector.scalar_tensor_tensor(qk[u][:, :, :], head_sum[:, :].unsqueeze(2).broadcast_to([P, 3 * H, DH]), -1.0 / DH,
                                               qk[u][:, :, :], ALU.mult, ALU.add).then_inc(centred.sem, 1)

            def sum_squares(b):
                dve.wait_ge(sq_done.sem, sq_done.after(b, 1))
                nc.vector.tensor_reduce(head_ss[:, :], qk_sq[:, :, :], AX.X, ALU.add).then_inc(ss_done.sem, 1)

            def head_norm(b, u):
                dve.wait_ge(head_rs_done.sem, head_rs_done.after(b, 1))
                nc.vector.tensor_tensor(qk[u][:, :, :], qk[u][:, :, :], head_rs[:, :].unsqueeze(2).broadcast_to([P, 3 * H, DH]), ALU.mult)\
                    .then_inc(scaled.sem, 1)
                qk_t = qk[u][:, :, :].rearrange("p (t h) d -> p t h d", t=3)
                for before, op, what, after in ((scaled, ALU.mult, gain, gained), (gained, ALU.add, offset, normed)):
                    dve.wait_ge(before.sem, before.after(b, 1))
                    nc.vector.tensor_tensor(qk_t, qk_t, what[:, :, :].unsqueeze(2).broadcast_to([P, 3, H, DH]), op).then_inc(after.sem, 1)

            def middle(b):
                for n in range(2):
                    dve.wait_ge(rest_done.sem, rest_done.after(b, n + 1))
                    first, step = ((3, 2), (0, 5))[n]
                    heads = (2 * H, H)[n]
                    nc.vector.tensor_copy(parts[n][:, :, first:6:step, :], rest[:, HEADS_OF[n]].unsqueeze(2).broadcast_to([P, heads, 2, DH]))\
                        .then_inc(middle_done.sem, 1)

            def stack_q(b):
                dve.wait_ge(q_stack_in_psum.sem, q_stack_in_psum.after(b, 1))
                nc.vector.tensor_copy(q_stack[:, 0:8, :], ring[1][:, :, :].bitcast(bf16)[0:PARTS * DH].rearrange("p a (h s) -> p (a h) s", s=S))\
                    .then_inc(q_low_stack_done.sem, 1)
                dve.wait_ge(q_stack_in_psum.sem, q_stack_in_psum.after(b, 2))
                nc.vector.tensor_copy(q_stack[:, 8:16, :], ring[0][:, :, :].bitcast(bf16)[0:PARTS * DH].rearrange("p a (h s) -> p (a h) s", s=S))\
                    .then_inc(q_high_stack_done.sem, 1)

            def mask_scores(b, n):
                t, half = n % 2, n // 2
                heads = slice(8 * half, 8 * half + 8)
                dve.wait_ge(scores_in_psum.sem, scores_in_psum.after(b, n + 1))
                src = ring[n % 2][:, :, :].rearrange("p a (h s) -> p (a h) s", s=P)[:, :, 0:SK]
                nc.vector.scalar_tensor_tensor(masked_scores[:, t, heads, :], src, SCALE, mask[:, t, :].unsqueeze(1).broadcast_to([P, 8, SK]),
                                               ALU.mult, ALU.add).then_inc(masked_done.sem, 1)
                dve.wait_ge(masked_done.sem, masked_done.after(b, n + 1))
                nc.vector.tensor_reduce(neg_max[:, t, heads], masked_scores[:, t, heads, :], AX.X, ALU.max, negate=True).then_inc(max_done.sem, 1)

            def divide(b, pair):
                dve.wait_ge(recip_done.sem, recip_done.after(b, pair + 1))
                nc.vector.tensor_tensor(attn[:, pair], work_bank[pair][:, :, :], den[:, pair], ALU.mult).then_inc(attn_done.sem, 1)

            def denominator(b, pair):
                dve.wait_ge(attn_in_psum.sem, attn_in_psum.after(b, 2 * pair + 2))
                wait_apart(dve)
                nc.vector.stream_shuffle(den[:, pair], work_bank[pair][:, :, :], [DH] * 32).then_inc(den_done.sem, 1)

            def residual(b):
                dve.wait_ge(out_in_psum.sem, out_in_psum.after(b, 1))
                xb = x[:, at(2 * b, 2), :]
                nc.vector.tensor_tensor(xb, work_bank[0][:, :, :], xb, ALU.add).then_inc(x_done.sem, 1)

            def batch(b, u, left=4):
                if masked:
                    mask_scores(b, 2)
                    mask_scores(b, 3)
                    if left >= 1:
                        middle(b + 1)
                    if left >= 4 or b + 4 == B:
                        moments(b + 4)
                    if left >= 3:
                        projected(b + 3, 1 - u)
                    if left >= 4 or b + 4 == B:
                        normalise(b + 4)
                    denominator(b, 0)
                    denominator(b, 1)
                    divide(b, 0)
                else:
                    if left >= 4 or b + 4 == B:
                        moments(b + 4)
                    if left >= 2:
                        sum_squares(b + 2)
                        head_norm(b + 2, u)
                    if left >= 1:
                        stack_q(b + 1)
                    if left >= 3:
                        centre(b + 3, 1 - u)
                    if left >= 4 or b + 4 == B:
                        normalise(b + 4)
                if masked and left >= 1:
                    stack_q(b + 1)
                if masked:
                    divide(b, 1)
                if left >= 2:
                    values(b + 2, u)
                if masked and left >= 1:
                    mask_scores(b + 1, 0)
                    mask_scores(b + 1, 1)
                if not masked and left >= 2:
                    middle(b + 2)
                residual(b)

            for done in (stats_done, moments_done, xn_done):
                dve.sem_inc(done.sem, 2)
            moments(1)
            normalise(1)
            dve.wait_ge(zeros_done.sem, 4)
            if masked:
                projected(0, 0)
                middle(0)
                values(0, 0)
                projected(1, 1)
                values(1, 1)
            else:
                centre(0, 0)
                sum_squares(0)
                values(0, 0)
                head_norm(0, 0)
                centre(1, 1)
                middle(0)
                values(1, 1)
                sum_squares(1)
            moments(2)
            if not masked:
                head_norm(1, 1)
            normalise(2)
            stack_q(0)
            if masked:
                mask_scores(0, 0)
                mask_scores(0, 1)
                projected(2, 0)
            else:
                middle(1)
                centre(2, 0)
            moments(3)
            normalise(3)
            with dve.Fori(0, (B - 4) // 2) as pair:
                for u in range(2):
                    batch(pair * 2 + u, u)
            for b in range(B - 4, B):
                batch(b, b % 2, B - 1 - b)


def shared_and_routed_experts(nc, shared, name, centroids, bias, wr, ws, wb):
    x = shared.x
    with ExitStack() as ctx:
        def sb(n, shape, dt=fp32):
            return ctx.enter_context(nc.sbuf_tensor(f"{name}_{n}", shape, dt))

        def ps(n, shape, dt=fp32):
            return ctx.enter_context(nc.psum_tensor(f"{name}_{n}", shape, dt))

        signals = []

        def signal(n, per_batch, opening=0):
            signals.append(nc.alloc_semaphore(f"{name}_{n}"))
            return Signal(signals[-1], per_batch, opening)

        stats = sb("stats", [P, 2, 6])
        mean_var = sb("mean_var", [P, 2, 2])
        var_eps = sb("var_eps", [P, 2])
        rstd = sb("rstd", [P, 2])
        un = [shared.xn, sb("un1", [P, 2, C])]
        u_t = [sb(f"u_t{u}", [P, 2, S]) for u in range(2)]
        logits = sb("logits", [P, 2, N_ROUTED])
        top_logits = sb("top_logits", [P, 2, 8])
        neg_top = sb("neg_top", [P, 2])
        exps = sb("exps", [P, 2, N_ROUTED])
        total = sb("total", [P, 2])
        recip = sb("recip", [P, 2])
        softmax = sb("softmax", [P, 2, N_ROUTED + 6])
        top = sb("top", [P, 2, 8])
        best_two = sb("best_two", [P, 2, 8])
        others = sb("others", [P, 2, N_ROUTED + 6])
        gates = [sb(f"gates{u}", [P, 2, 32]) for u in range(2)]
        gates_t = [sb(f"gates_t{u}", [32, S]) for u in range(2)]
        acc = sb("acc", [P, 2, C])

        expert_bank = [ps(f"expert_bank{n}", [P, 2, C]) for n in range(4)]
        u_t_bank = ps("u_t_bank", [P, 2, S])
        logits_bank = ps("logits_bank", [P, 2, N_ROUTED])
        gates_bank = ps("gates_bank", [32, S])
        shared_bank = ps("shared_bank", [P, 2, C])

        constants_done = signal("constants_done", 4)
        stats_done = signal("stats_done", 2)
        moments_done = signal("moments_done", 2)
        var_done = signal("var_done", 1)
        rstd_done = signal("rstd_done", 1)
        u_done = signal("u_done", 2)
        u_t_in_psum = signal("u_t_in_psum", 1)
        u_t_done = signal("u_t_done", 1)
        logits_in_psum = signal("logits_in_psum", 1)
        logits_done = signal("logits_done", 1)
        top_logits_done = signal("top_logits_done", 2)
        neg_top_done = signal("neg_top_done", 1)
        exps_done = signal("exps_done", 2)
        recip_done = signal("recip_done", 1)
        softmax_done = signal("softmax_done", 2)
        top_done = signal("top_done", 2)
        best_two_done = signal("best_two_done", 1)
        others_done = signal("others_done", 2)
        gates_done = signal("gates_done", 1)
        gates_t_in_psum = signal("gates_t_in_psum", 1)
        gates_t_done = signal("gates_t_done", 1)
        shared_in_psum = signal("shared_in_psum", 1)
        expert_in_psum = signal("expert_in_psum", N_ROUTED)
        acc_done = signal("acc_done", 2 * (N_ROUTED + 1))
        x_done = signal("x_done", 1, opening=1)

        block = layer_block(ctx, nc, signals)

        @block.gpsimd
        def _(pool):
            nc.gpsimd.memset(softmax[:, :, N_ROUTED:], -1.0).then_inc(constants_done.sem, 1)
            pool.wait_ge(constants_done.sem, 1)
            nc.gpsimd.memset(best_two[:, :, 2:8], -1.0).then_inc(constants_done.sem, 1)
            for u in range(2):
                pool.wait_ge(constants_done.sem, 2 + 3 * u)
                nc.gpsimd.memset(gates[u][:, :, :], 0.0).then_inc(constants_done.sem, 1)
                pool.wait_ge(constants_done.sem, 3 + 3 * u)
                nc.gpsimd.memset(gates[u][:, :, N_ROUTED:N_ROUTED + 2], 0.5).then_inc(constants_done.sem, 1)
                pool.wait_ge(constants_done.sem, 4 + 3 * u)
                nc.gpsimd.memset(gates[u][:, :, N_ROUTED + 2:], 0.0).then_inc(constants_done.sem, 1)

            def normalise(b):
                pool.wait_ge(moments_done.sem, moments_done.after(b, 2))
                wait_apart(pool)
                nc.gpsimd.tensor_scalar(var_eps[:, :], mean_var[:, :, 1], LN_EPS, None, ALU.add).then_inc(var_done.sem, 1)
                pool.wait_ge(var_done.sem, var_done.after(b, 1))
                nc.gpsimd.tensor_tensor(rstd[:, :], var_eps[:, :], shared.neg_half[:, 0:2], ALU.pow).then_inc(rstd_done.sem, 1)

            for done in (var_done, rstd_done):
                pool.sem_inc(done.sem, 1)
            with pool.Fori(1, B) as b:
                normalise(b)
            normalise(B)

        @block.tensor
        def _(pe):
            def transpose_u(b, u):
                pe.wait_ge(u_done.sem, u_done.after(b, 2))
                for t in range(2):
                    for c in range(2):
                        last = nc.tensor.transpose(u_t_bank[:, c, t * P:(t + 1) * P], un[u][:, t, c * P:(c + 1) * P], shared.ident[:, :])
                last.then_inc(u_t_in_psum.sem, 1)

            def route(b, u):
                pe.wait_ge(logits_done.sem, logits_done.after(b, 0))
                pe.wait_ge(u_t_done.sem, u_t_done.after(b, 1))
                for t in range(2):
                    for c in range(2):
                        last = nc.tensor.matmul(logits_bank[:, t, :], u_t[u][:, c, t * P:(t + 1) * P], centroids[:, c, :],
                                                start=(c == 0), stop=(c == 1))
                last.then_inc(logits_in_psum.sem, 1)

            def transpose_gates(b, u):
                pe.wait_ge(gates_done.sem, gates_done.after(b, 1))
                for t in range(2):
                    last = nc.tensor.transpose(gates_bank[:, t * P:(t + 1) * P], gates[u][:, t, :], shared.ident[:, :])
                last.then_inc(gates_t_in_psum.sem, 1)

            def shared_experts(b, u):
                pe.wait_ge(gates_t_done.sem, gates_t_done.after(b, 1))
                for t in range(2):
                    for c in range(2):
                        nc.tensor.matmul(shared_bank[:, t, :], u_t[u][:, c, t * P:(t + 1) * P], ws[:, c, :], start=(c == 0), stop=False)
                    last = nc.tensor.matmul(shared_bank[:, t, :], gates_t[u][0:N_ROUTED + 2, t * P:(t + 1) * P], wb[:, :],
                                            start=False, stop=True)
                last.then_inc(shared_in_psum.sem, 1)

            def experts(b, u, n):
                e, t = 2 * (n // 2), n % 2
                if n >= 4:
                    pe.wait_ge(acc_done.sem, acc_done.after(b, 2 + 2 * (n - 3)))
                elif not (isinstance(b, int) and b == 0):
                    pe.wait_ge(acc_done.sem, acc_done.after(b - 1, 2 + 2 * (n + N_ROUTED - 3)))
                for c in range(2):
                    last = nc.tensor.matmul(expert_bank[n % 4][:, :, :].rearrange("p a c -> p (a c)"), u_t[u][:, c, t * P:(t + 1) * P],
                                            wr[:, c, e:e + 2, :].rearrange("p a c -> p (a c)"), start=(c == 0), stop=(c == 1))
                last.then_inc(expert_in_psum.sem, 1)

            def batch(b, u, left=1):
                for n in range(4, N_ROUTED):
                    experts(b, u, n)
                    if left and n == 4:
                        transpose_u(b + 1, 1 - u)
                    if left and n == 5:
                        route(b + 1, 1 - u)
                    if left and n == 12:
                        transpose_gates(b + 1, 1 - u)
                if left:
                    for n in range(4):
                        if n == 2:
                            shared_experts(b + 1, 1 - u)
                        experts(b + 1, 1 - u, n)

            pe.sem_inc(x_done.sem, 1)
            transpose_u(0, 0)
            route(0, 0)
            for n in range(4):
                if n == 1:
                    pe.wait_ge(constants_done.sem, 8)
                    transpose_gates(0, 0)
                if n == 2:
                    shared_experts(0, 0)
                experts(0, 0, n)
            with pe.Fori(0, (B - 2) // 2) as pair:
                for u in range(2):
                    batch(pair * 2 + u, u)
            batch(B - 2, 0)
            batch(B - 1, 1, 0)

        @block.scalar
        def _(act):
            def front(b, u):
                act.wait_ge(u_t_in_psum.sem, u_t_in_psum.after(b, 1))
                nc.scalar.activation(u_t[u][:, :, :], u_t_bank[:, :, :], ACT.Copy).then_inc(u_t_done.sem, 1)
                act.wait_ge(neg_top_done.sem, neg_top_done.after(b, 1))
                for t in range(2):
                    nc.scalar.activation(exps[:, t, :], logits[:, t, :], ACT.Exp, bias=neg_top[:, t:t + 1],
                                         accum_out=total[:, t:t + 1]).then_inc(exps_done.sem, 1)
                act.wait_ge(gates_t_in_psum.sem, gates_t_in_psum.after(b, 1))
                nc.scalar.activation(gates_t[u][:, :], gates_bank[:, :], ACT.Copy).then_inc(gates_t_done.sem, 1)

            with act.Fori(0, B // 2) as pair:
                for u in range(2):
                    front(pair * 2 + u, u)

        @block.vector
        def _(dve):
            def moments(b):
                for t in range(2):
                    nc.vector.bn_stats(stats[:, t], x[:, tokens(b, t), :]).then_inc(stats_done.sem, 1)
                for t in range(2):
                    dve.wait_ge(stats_done.sem, stats_done.after(b, t + 1))
                    wait_apart(dve)
                    nc.vector.bn_aggr(mean_var[:, t], stats[:, t]).then_inc(moments_done.sem, 1)

            def normalise(b, u):
                dve.wait_ge(rstd_done.sem, rstd_done.after(b, 1))
                dve.wait_ge(moments_done.sem, moments_done.after(b, 2))
                for t in range(2):
                    nc.vector.tensor_scalar(un[u][:, t], x[:, tokens(b, t), :], mean_var[:, t, 0:1], rstd[:, t:t + 1],
                                            ALU.subtract, ALU.mult).then_inc(u_done.sem, 1)

            def route(b):
                dve.wait_ge(logits_in_psum.sem, logits_in_psum.after(b, 1))
                nc.vector.tensor_tensor(logits[:, :, :], logits_bank[:, :, :], bias[:, :].unsqueeze(1).broadcast_to([P, 2, N_ROUTED]), ALU.add)\
                    .then_inc(logits_done.sem, 1)
                dve.wait_ge(logits_done.sem, logits_done.after(b, 1))
                nc.vector.tensor_reduce(neg_top[:, :], logits[:, :, :], AX.X, ALU.max, negate=True).then_inc(neg_top_done.sem, 1)

            def gate(b, u):
                dve.wait_ge(exps_done.sem, exps_done.after(b, 2))
                nc.vector.reciprocal(recip[:, :], total[:, :]).then_inc(recip_done.sem, 1)
                dve.wait_ge(recip_done.sem, recip_done.after(b, 1))
                for t in range(2):
                    nc.vector.tensor_scalar(softmax[:, t, 0:N_ROUTED], exps[:, t, :], recip[:, t:t + 1], None, ALU.mult)\
                        .then_inc(softmax_done.sem, 1)
                for t in range(2):
                    dve.wait_ge(softmax_done.sem, softmax_done.after(b, t + 1))
                    wait_apart(dve)
                    nc.vector.max(top[:, t, :], softmax[:, t, :]).then_inc(top_done.sem, 1)
                dve.wait_ge(top_done.sem, top_done.after(b, 2))
                nc.vector.tensor_copy(best_two[:, :, 0:2], top[:, :, 0:2]).then_inc(best_two_done.sem, 1)
                dve.wait_ge(best_two_done.sem, best_two_done.after(b, 1))
                wait_apart(dve)
                for t in range(2):
                    nc.vector.match_replace(others[:, t, :], best_two[:, t, :], softmax[:, t, :], 0.0).then_inc(others_done.sem, 1)
                dve.wait_ge(others_done.sem, others_done.after(b, 2))
                nc.vector.tensor_tensor(gates[u][:, :, 0:N_ROUTED], softmax[:, :, 0:N_ROUTED], others[:, :, 0:N_ROUTED], ALU.subtract)\
                    .then_inc(gates_done.sem, 1)

            def start_acc(b, u):
                dve.wait_ge(shared_in_psum.sem, shared_in_psum.after(b, 1))
                dve.wait_ge(x_done.sem, x_done.after(b, 0))
                for t in range(2):
                    nc.vector.tensor_tensor(acc[:, t, :], shared_bank[:, t, :], un[u][:, t, :], ALU.add).then_inc(acc_done.sem, 1)

            def add_experts(b, u, n):
                e, t = 2 * (n // 2), n % 2
                dve.wait_ge(expert_in_psum.sem, expert_in_psum.after(b, n + 1))
                for k in range(2):
                    sums = 2 + 2 * n + 1 if k else (t + 1 if n < 2 else 2 + 2 * (n - 1))
                    dve.wait_ge(acc_done.sem, acc_done.after(b, sums))
                    nc.vector.scalar_tensor_tensor(acc[:, t, :], expert_bank[n % 4][:, k, :], gates[u][:, t, e + k:e + k + 1],
                                                          acc[:, t, :], ALU.mult, ALU.add).then_inc(acc_done.sem, 1)

            def residual(b):
                dve.wait_ge(acc_done.sem, acc_done.after(b + 1, 0))
                xb = x[:, at(2 * b, 2), :]
                nc.vector.tensor_tensor(xb, xb, acc[:, :, :], ALU.add).then_inc(x_done.sem, 1)

            def batch(b, u, left=1):
                moments(b + 1)
                start_acc(b, u)
                normalise(b + 1, 1 - u)
                for n in range(N_ROUTED):
                    add_experts(b, u, n)
                    if left and n == 5:
                        route(b + 1)
                    if left and n == 7:
                        gate(b + 1, 1 - u)
                residual(b)

            for done in (stats_done, moments_done, u_done):
                dve.sem_inc(done.sem, 2)
            route(0)
            dve.wait_ge(constants_done.sem, 8)
            gate(0, 0)
            with dve.Fori(0, (B - 2) // 2) as pair:
                for u in range(2):
                    batch(pair * 2 + u, u)
            batch(B - 2, 0)
            batch(B - 1, 1, 0)


def attention_of_experts(nc, shared, name, sim, gate, wq, wk, wv, wo, causal):
    x = shared.x
    with ExitStack() as ctx:
        def sb(n, shape, dt=fp32):
            return ctx.enter_context(nc.sbuf_tensor(f"{name}_{n}", shape, dt))

        def ps(n, shape, dt=fp32):
            return ctx.enter_context(nc.psum_tensor(f"{name}_{n}", shape, dt))

        signals = []

        def signal(n, per_batch, opening=0):
            signals.append(nc.alloc_semaphore(f"{name}_{n}"))
            return Signal(signals[-1], per_batch, opening)

        stats = sb("stats", [P, 2, 6])
        mean_var = sb("mean_var", [P, 2, 2])
        var_eps = sb("var_eps", [P, 2])
        rstd = sb("rstd", [P, 2])
        un = shared.xn
        un_sq = sb("un_sq", [P, 2, C])
        norm_sq = sb("norm_sq", [P, 2])
        norm_sq_eps = sb("norm_sq_eps", [P, 2])
        norm_recip = sb("norm_recip", [P, 2])
        u_t = sb("u_t", [P, 2, S])
        logits = sb("logits", [P, 2, N_ATTN + 6])
        active = sb("active", [P, 2, N_ATTN])
        n_active = sb("n_active", [P, 2])
        inactive = sb("inactive", [P, 2])
        top = sb("top", [P, 2, 8])
        best_two = sb("best_two", [P, 2, 8])
        others = sb("others", [P, 2, N_ATTN + 6])
        fallback = sb("fallback", [P, 2, N_ATTN])
        experts = sb("experts", [P, 2, N_ATTN])
        gated = sb("gated", [P, 2, N_ATTN])
        absent = sb("absent", [P, 2, N_ATTN])
        gated_used = sb("gated_used", [P, 2, N_ATTN])
        masked_logits = sb("masked_logits", [P, 2, N_ATTN])
        neg_top = sb("neg_top", [P, 2])
        route_exps = sb("route_exps", [P, 2, N_ATTN])
        route_total = sb("route_total", [P, 2])
        route_recip = sb("route_recip", [P, 2])
        route_softmax = sb("route_softmax", [P, 2, N_ATTN])
        weights = [sb(f"weights{u}", [P, 2, N_ATTN]) for u in range(2)]
        experts_t = sb("experts_t", [N_ATTN, S], bf16)
        select = sb("select", [N_ATTN, N_ATTN, P], bf16)
        masked_u_t = [sb(f"masked_u_t{u}", [P, N_ATTN, 2, S]) for u in range(2)]
        sim_sq = sb("sim_sq", [P, 2, N_ATTN])
        sim_norm = sb("sim_norm", [P, N_ATTN])
        q_t = sb("q_t", [P, S])
        k_t = sb("k_t", [P, S])
        v = sb("v", [P, 2, P])
        scores = sb("scores", [P, 3, P])
        neg_max = sb("neg_max", [P, 2])
        exps = sb("exps", [P, 3, P])
        total = sb("total", [P, 2])
        recip = sb("recip", [P, 2])
        probs = sb("probs", [P, 3, P])
        probs_t = sb("probs_t", [P, 3, P])
        attn_t = sb("attn_t", [P, S])
        acc = sb("acc", [P, 2, C])

        qkv_bank = [ps(f"{n}_bank", [P, S]) for n in "qkv"]
        attn_bank = ps("attn_bank", [P, 3, P])
        out_bank = [ps(f"out_bank{n}", [P, 2, C]) for n in range(2)]
        route_bank = [ps(f"route_bank{n}", [P, 2, S]) for n in range(2)]
        u_t_bank = route_bank[0]
        logits_bank = route_bank[1]
        experts_bank = route_bank[1][0:N_ATTN, 0, :]

        constants_done = signal("constants_done", 4)
        sim_sq_done = signal("sim_sq_done", 1)
        sim_sq_in_psum = signal("sim_sq_in_psum", 1)
        sim_norm_sq_done = signal("sim_norm_sq_done", 1)
        sim_norm_done = signal("sim_norm_done", 1)
        sim_done = signal("sim_done", 1)
        gate_done = signal("gate_done", 3)
        stats_done = signal("stats_done", 2)
        moments_done = signal("moments_done", 2)
        var_done = signal("var_done", 1)
        rstd_done = signal("rstd_done", 1)
        u_done = signal("u_done", 2)
        sq_done = signal("sq_done", 2)
        norm_eps_done = signal("norm_eps_done", 1)
        norm_done = signal("norm_done", 1)
        u_t_in_psum = signal("u_t_in_psum", 1)
        u_t_done = signal("u_t_done", 1)
        experts_t_in_psum = signal("experts_t_in_psum", 1)
        experts_t_done = signal("experts_t_done", 1)
        mask_in_psum = signal("mask_in_psum", N_ATTN // 2)
        logits_in_psum = signal("logits_in_psum", 1)
        logits_done = signal("logits_done", 2)
        active_done = signal("active_done", 1)
        n_active_done = signal("n_active_done", 1)
        inactive_done = signal("inactive_done", 1)
        top_done = signal("top_done", 2)
        best_two_done = signal("best_two_done", 1)
        others_done = signal("others_done", 2)
        fallback_done = signal("fallback_done", 1)
        experts_done = signal("experts_done", 2)
        gated_done = signal("gated_done", 1)
        absent_done = signal("absent_done", 1)
        gated_used_done = signal("gated_used_done", 1)
        masked_logits_done = signal("masked_logits_done", 1)
        neg_top_done = signal("neg_top_done", 1)
        route_exps_done = signal("route_exps_done", 2)
        route_recip_done = signal("route_recip_done", 1)
        route_softmax_done = signal("route_softmax_done", 2)
        weights_done = signal("weights_done", 1)
        masked_u_done = signal("masked_u_done", N_ATTN // 2)
        q_in_psum = signal("q_in_psum", 1)
        k_in_psum = signal("k_in_psum", 1)
        v_in_psum = signal("v_in_psum", 1)
        q_done = signal("q_done", 1)
        k_done = signal("k_done", 1)
        v_done = signal("v_done", 1)
        scores_in_psum = signal("scores_in_psum", 1)
        scores_done = signal("scores_done", 1)
        max_done = signal("max_done", 2)
        exps_done = signal("exps_done", 2)
        recip_done = signal("recip_done", 1)
        probs_done = signal("probs_done", 2)
        probs_t_in_psum = signal("probs_t_in_psum", 1)
        probs_t_done = signal("probs_t_done", 1)
        attn_in_psum = signal("attn_in_psum", 1)
        attn_done = signal("attn_done", 1, opening=1)
        out_in_psum = signal("out_in_psum", N_ATTN)
        acc_done = signal("acc_done", 2 * N_ATTN, opening=1)

        block = layer_block(ctx, nc, signals)

        @block.gpsimd
        def _(pool):
            nc.gpsimd.memset(logits[:, :, N_ATTN:], -4.0).then_inc(constants_done.sem, 1)
            pool.wait_ge(constants_done.sem, 1)
            nc.gpsimd.memset(best_two[:, :, 2:8], -4.0).then_inc(constants_done.sem, 1)
            pool.wait_ge(constants_done.sem, 2)

            def unit_columns():
                pool.wait_ge(sim_norm_sq_done.sem, 1)
                nc.gpsimd.tensor_tensor(sim_norm[:, :], sim_norm[:, :], shared.neg_half[:, 0:N_ATTN], ALU.pow).then_inc(sim_norm_done.sem, 1)
                pool.wait_ge(sim_norm_done.sem, 1)
                nc.gpsimd.tensor_tensor(sim[:, :, :], sim[:, :, :], sim_norm[:, :].unsqueeze(1).broadcast_to([P, 2, N_ATTN]), ALU.mult)\
                    .then_inc(sim_done.sem, 1)

            def normalise(b):
                pool.wait_ge(moments_done.sem, moments_done.after(b, 2))
                wait_apart(pool)
                nc.gpsimd.tensor_scalar(var_eps[:, :], mean_var[:, :, 1], LN_EPS, None, ALU.add).then_inc(var_done.sem, 1)
                pool.wait_ge(var_done.sem, var_done.after(b, 1))
                nc.gpsimd.tensor_tensor(rstd[:, :], var_eps[:, :], shared.neg_half[:, 0:2], ALU.pow).then_inc(rstd_done.sem, 1)

            def token_norms(b):
                pool.wait_ge(sq_done.sem, sq_done.after(b, 2))
                wait_apart(pool)
                nc.gpsimd.tensor_scalar(norm_sq_eps[:, :], norm_sq[:, :], NORM_EPS ** 2, None, ALU.max).then_inc(norm_eps_done.sem, 1)
                pool.wait_ge(norm_eps_done.sem, norm_eps_done.after(b, 1))
                nc.gpsimd.tensor_tensor(norm_recip[:, :], norm_sq_eps[:, :], shared.neg_half[:, 0:2], ALU.pow).then_inc(norm_done.sem, 1)

            for done in (var_done, rstd_done):
                pool.sem_inc(done.sem, 1)
            unit_columns()
            token_norms(0)
            pool.wait_ge(norm_done.sem, norm_done.after(0, 1))
            nc.gpsimd.memset(select[:, :, :], 0.0).then_inc(constants_done.sem, 1)
            pool.wait_ge(constants_done.sem, 3)
            nc.gpsimd.affine_select(out=select[:, :, :], in_=select[:, :, :], compare_op=ALU.not_equal, fill=1.0,
                                    base=0, pattern=[[-1, N_ATTN], [0, P]], channel_multiplier=1).then_inc(constants_done.sem, 1)
            pool.wait_ge(constants_done.sem, 4)
            normalise(1)
            token_norms(1)
            with pool.Fori(2, B) as b:
                normalise(b)
                token_norms(b)

        @block.tensor
        def _(pe):
            def transpose_u(b):
                pe.wait_ge(u_done.sem, u_done.after(b, 2))
                pe.wait_ge(masked_u_done.sem, masked_u_done.after(b, 0))
                for t in range(2):
                    for c in range(2):
                        last = nc.tensor.transpose(u_t_bank[:, c, t * P:(t + 1) * P], un[:, t, c * P:(c + 1) * P], shared.ident[:, :])
                last.then_inc(u_t_in_psum.sem, 1)

            def route(b):
                pe.wait_ge(u_t_done.sem, u_t_done.after(b, 1))
                for t in range(2):
                    for c in range(2):
                        last = nc.tensor.matmul(logits_bank[:, t, 0:N_ATTN], u_t[:, c, t * P:(t + 1) * P], sim[:, c, :],
                                                start=(c == 0), stop=(c == 1))
                last.then_inc(logits_in_psum.sem, 1)

            def transpose_experts(b):
                pe.wait_ge(experts_done.sem, experts_done.after(b, 2))
                for t in range(2):
                    last = nc.tensor.transpose(experts_bank[:, t * P:(t + 1) * P], experts[:, t, :], shared.ident[:, :])
                last.then_inc(experts_t_in_psum.sem, 1)

            def spread(b, n):
                if n == 0:
                    pe.wait_ge(experts_t_done.sem, experts_t_done.after(b, 1))
                if n >= 2:
                    pe.wait_ge(masked_u_done.sem, masked_u_done.after(b, n - 1))
                for k in range(2):
                    last = nc.tensor.matmul(route_bank[n % 2][:, k, :], select[:, 2 * n + k, :], experts_t[:, :], start=True, stop=True)
                last.then_inc(mask_in_psum.sem, 1)

            def project_qk(b, u, which):
                bank, w, in_psum, done = ((qkv_bank[0], wq, q_in_psum, q_done), (qkv_bank[1], wk, k_in_psum, k_done))[which]
                if which == 0:
                    pe.wait_ge(masked_u_done.sem, masked_u_done.after(b, N_ATTN // 2))
                pe.wait_ge(done.sem, done.after(b, 0))
                for e in range(N_ATTN):
                    for c in range(2):
                        last = nc.tensor.matmul(bank[:, :], w[:, c, e, :], masked_u_t[u][:, e, c, :],
                                                start=(e == 0 and c == 0), stop=(e == N_ATTN - 1 and c == 1))
                last.then_inc(in_psum.sem, 1)

            def project_v(b, u, t, e_from=0, e_to=N_ATTN):
                if t == 0 and e_from == 0:
                    pe.wait_ge(v_done.sem, v_done.after(b, 0))
                for e in range(e_from, e_to):
                    for c in range(2):
                        last = nc.tensor.matmul(qkv_bank[2][:, t * P:(t + 1) * P], masked_u_t[u][:, e, c, t * P:(t + 1) * P], wv[:, c, e, :],
                                                start=(e == 0 and c == 0), stop=(e == N_ATTN - 1 and c == 1))
                if t == 1 and e_to == N_ATTN:
                    last.then_inc(v_in_psum.sem, 1)

            def attend(b):
                pe.wait_ge(q_done.sem, q_done.after(b, 1))
                pe.wait_ge(k_done.sem, k_done.after(b, 1))
                pe.wait_ge(attn_done.sem, attn_done.after(b, 0))
                nc.tensor.matmul(attn_bank[:, 0, :], q_t[:, 0:P], k_t[:, 0:P], start=True, stop=True)
                nc.tensor.matmul(attn_bank[:, 1:3, :].rearrange("p a k -> p (a k)"), q_t[:, P:S], k_t[:, :],
                                 start=True, stop=True).then_inc(scores_in_psum.sem, 1)

            def transpose_probs(b):
                pe.wait_ge(probs_done.sem, probs_done.after(b, 2))
                for n, (q_tile, k_tile) in enumerate(((0, 0), (1, 0), (1, 1))):
                    last = nc.tensor.transpose(attn_bank[:, n, :], probs[:, n, :], shared.ident[:, :])
                last.then_inc(probs_t_in_psum.sem, 1)

            def weigh(b):
                pe.wait_ge(probs_t_done.sem, probs_t_done.after(b, 1))
                pe.wait_ge(v_done.sem, v_done.after(b, 1))
                out = attn_bank[:, 0:2, :].rearrange("p a k -> p (a k)")
                nc.tensor.matmul(out, v[:, 0, :], probs_t[:, 0:2, :].rearrange("p a k -> p (a k)"), start=True, stop=False)
                nc.tensor.matmul(out[:, P:S], v[:, 1, :], probs_t[:, 2, :], start=False, stop=True).then_inc(attn_in_psum.sem, 1)

            def output(b, n):
                e, t = 2 * (n // 2), n % 2
                if n == 0:
                    pe.wait_ge(attn_done.sem, attn_done.after(b, 1))
                if n < 2:
                    pe.wait_ge(acc_done.sem, acc_done.after(b, 0))
                else:
                    pe.wait_ge(acc_done.sem, acc_done.after(b, 2 * (n - 1)))
                nc.tensor.matmul(out_bank[n % 2][:, :, :].rearrange("p a c -> p (a c)"), attn_t[:, t * P:(t + 1) * P],
                                 wo[:, e:e + 2, :].rearrange("p a c -> p (a c)"), start=True, stop=True).then_inc(out_in_psum.sem, 1)

            def batch(b, u, left=2):
                attend(b)
                if left >= 1:
                    project_qk(b + 1, 1 - u, 0)
                if left >= 2:
                    transpose_u(b + 2)
                transpose_probs(b)
                if left >= 1:
                    project_qk(b + 1, 1 - u, 1)
                if left >= 2:
                    route(b + 2)
                weigh(b)
                if left >= 1:
                    project_v(b + 1, 1 - u, 0, 0, 4)
                output(b, 0)
                output(b, 1)
                if left >= 2:
                    transpose_experts(b + 2)
                if left >= 1:
                    project_v(b + 1, 1 - u, 0, 4, 6)
                if left >= 2:
                    spread(b + 2, 0)
                    spread(b + 2, 1)
                if left >= 1:
                    project_v(b + 1, 1 - u, 0, 6)
                output(b, 2)
                output(b, 3)
                if left >= 2:
                    spread(b + 2, 2)
                    spread(b + 2, 3)
                if left >= 1:
                    project_v(b + 1, 1 - u, 1, 0, 5)
                output(b, 4)
                output(b, 5)
                if left >= 1:
                    project_v(b + 1, 1 - u, 1, 5)
                output(b, 6)
                output(b, 7)

            for opened in (attn_done, acc_done):
                pe.sem_inc(opened.sem, 1)
            pe.wait_ge(sim_sq_done.sem, 1)
            for c in range(2):
                last = nc.tensor.matmul(logits_bank[:, 0, 0:N_ATTN], shared.ones[:, :], sim_sq[:, c, :], start=(c == 0), stop=(c == 1))
            last.then_inc(sim_sq_in_psum.sem, 1)
            transpose_u(0)
            pe.wait_ge(sim_done.sem, 1)
            route(0)
            transpose_experts(0)
            pe.wait_ge(constants_done.sem, 4)
            for n in range(N_ATTN // 2):
                spread(0, n)
            project_qk(0, 0, 0)
            transpose_u(1)
            project_qk(0, 0, 1)
            route(1)
            project_v(0, 0, 0)
            transpose_experts(1)
            project_v(0, 0, 1, 0, 2)
            spread(1, 0)
            spread(1, 1)
            project_v(0, 0, 1, 2)
            spread(1, 2)
            spread(1, 3)
            with pe.Fori(0, (B - 2) // 2) as pair:
                for u in range(2):
                    batch(pair * 2 + u, u)
            batch(B - 2, 0, 1)
            batch(B - 1, 1, 0)

        @block.scalar
        def _(act):
            def square(b):
                for t in range(2):
                    act.wait_ge(u_done.sem, u_done.after(b, t + 1))
                    nc.scalar.activation(un_sq[:, t, :], un[:, t, :], ACT.Square, accum_out=norm_sq[:, t:t + 1]).then_inc(sq_done.sem, 1)

            def copy_u_t(b):
                act.wait_ge(u_t_in_psum.sem, u_t_in_psum.after(b, 1))
                act.wait_ge(masked_u_done.sem, masked_u_done.after(b, 0))
                nc.scalar.activation(u_t[:, :, :], u_t_bank[:, :, :], ACT.Copy).then_inc(u_t_done.sem, 1)

            def copy_experts_t(b):
                act.wait_ge(experts_t_in_psum.sem, experts_t_in_psum.after(b, 1))
                nc.scalar.activation(experts_t[:, :], experts_bank, ACT.Copy).then_inc(experts_t_done.sem, 1)

            def route_softmax_exps(b):
                act.wait_ge(neg_top_done.sem, neg_top_done.after(b, 1))
                for t in range(2):
                    nc.scalar.activation(route_exps[:, t, :], masked_logits[:, t, :], ACT.Exp, bias=neg_top[:, t:t + 1],
                                         accum_out=route_total[:, t:t + 1]).then_inc(route_exps_done.sem, 1)

            def exponentials(b):
                for t, tiles in enumerate(TILES_OF):
                    act.wait_ge(max_done.sem, max_done.after(b, t + 1))
                    nc.scalar.activation(exps[:, tiles, :], scores[:, tiles, :], ACT.Exp, bias=neg_max[:, t:t + 1],
                                         accum_out=total[:, t:t + 1]).then_inc(exps_done.sem, 1)

            def copy_q(b):
                act.wait_ge(q_in_psum.sem, q_in_psum.after(b, 1))
                nc.scalar.activation(q_t[:, :], qkv_bank[0][:, :], ACT.Copy).then_inc(q_done.sem, 1)

            def copy_k(b):
                act.wait_ge(k_in_psum.sem, k_in_psum.after(b, 1))
                nc.scalar.activation(k_t[:, :], qkv_bank[1][:, :], ACT.Copy).then_inc(k_done.sem, 1)

            def copy_v(b):
                act.wait_ge(v_in_psum.sem, v_in_psum.after(b, 1))
                nc.scalar.activation(v[:, :, :], qkv_bank[2][:, :].rearrange("p (t c) -> p t c", t=2), ACT.Copy).then_inc(v_done.sem, 1)

            def copy_probs_t(b):
                act.wait_ge(probs_t_in_psum.sem, probs_t_in_psum.after(b, 1))
                nc.scalar.activation(probs_t[:, :, :], attn_bank[:, :, :], ACT.Copy).then_inc(probs_t_done.sem, 1)

            def copy_attn(b):
                act.wait_ge(attn_in_psum.sem, attn_in_psum.after(b, 1))
                nc.scalar.activation(attn_t[:, :].rearrange("p (a k) -> p a k", a=2), attn_bank[:, 0:2, :], ACT.Copy).then_inc(attn_done.sem, 1)

            def front(b):
                square(b)
                copy_u_t(b)
                copy_experts_t(b)
                route_softmax_exps(b)

            def batch(b, left=2):
                exponentials(b)
                if left >= 2:
                    square(b + 2)
                if left >= 1:
                    copy_q(b + 1)
                if left >= 2:
                    copy_u_t(b + 2)
                copy_probs_t(b)
                if left >= 1:
                    copy_k(b + 1)
                copy_attn(b)
                if left >= 2:
                    copy_experts_t(b + 2)
                    route_softmax_exps(b + 2)
                if left >= 1:
                    copy_v(b + 1)

            nc.scalar.activation(sim_sq[:, :, :], sim[:, :, :], ACT.Square).then_inc(sim_sq_done.sem, 1)
            nc.scalar.activation(gate[:, :], gate[:, :], ACT.Exp, scale=-1.0).then_inc(gate_done.sem, 1)
            front(0)
            square(1)
            copy_q(0)
            copy_u_t(1)
            copy_k(0)
            copy_experts_t(1)
            route_softmax_exps(1)
            copy_v(0)
            with act.Fori(0, B - 2) as b:
                batch(b)
            batch(B - 2, 1)
            batch(B - 1, 0)

        @block.vector
        def _(dve):
            def moments(b):
                dve.wait_ge(u_done.sem, u_done.after(b, 0))
                for t in range(2):
                    nc.vector.bn_stats(stats[:, t], x[:, at(2 * b + t), :]).then_inc(stats_done.sem, 1)
                for t in range(2):
                    dve.wait_ge(stats_done.sem, stats_done.after(b, t + 1))
                    wait_apart(dve)
                    nc.vector.bn_aggr(mean_var[:, t], stats[:, t]).then_inc(moments_done.sem, 1)

            def normalise(b):
                dve.wait_ge(rstd_done.sem, rstd_done.after(b, 1))
                dve.wait_ge(moments_done.sem, moments_done.after(b, 2))
                dve.wait_ge(sq_done.sem, sq_done.after(b, 0))
                dve.wait_ge(u_t_in_psum.sem, u_t_in_psum.after(b, 0))
                for t in range(2):
                    nc.vector.tensor_scalar(un[:, t], x[:, at(2 * b + t), :], mean_var[:, t, 0:1], rstd[:, t:t + 1],
                                            ALU.subtract, ALU.mult).then_inc(u_done.sem, 1)

            def route(b):
                dve.wait_ge(logits_in_psum.sem, logits_in_psum.after(b, 1))
                dve.wait_ge(norm_done.sem, norm_done.after(b, 1))
                for t in range(2):
                    nc.vector.scalar_tensor_tensor(logits[:, t, 0:N_ATTN], logits_bank[:, t, 0:N_ATTN], norm_recip[:, t:t + 1],
                                                   gate[:, :], ALU.mult, ALU.subtract).then_inc(logits_done.sem, 1)
                dve.wait_ge(logits_done.sem, logits_done.after(b, 2))
                real = logits[:, :, 0:N_ATTN]
                nc.vector.tensor_scalar(active[:, :, :], real, 0.0, None, ALU.is_gt).then_inc(active_done.sem, 1)
                nc.vector.tensor_scalar(gated[:, :, :], real, 0.0, None, ALU.max).then_inc(gated_done.sem, 1)
                for t in range(2):
                    nc.vector.max(top[:, t, :], logits[:, t, :]).then_inc(top_done.sem, 1)
                dve.wait_ge(active_done.sem, active_done.after(b, 1))
                nc.vector.tensor_reduce(n_active[:, :], active[:, :, :], AX.X, ALU.add).then_inc(n_active_done.sem, 1)
                dve.wait_ge(top_done.sem, top_done.after(b, 2))
                nc.vector.tensor_copy(best_two[:, :, 0:2], top[:, :, 0:2]).then_inc(best_two_done.sem, 1)
                dve.wait_ge(n_active_done.sem, n_active_done.after(b, 1))
                nc.vector.tensor_scalar(inactive[:, :], n_active[:, :], 0.0, None, ALU.is_equal).then_inc(inactive_done.sem, 1)
                dve.wait_ge(best_two_done.sem, best_two_done.after(b, 1))
                wait_apart(dve)
                for t in range(2):
                    nc.vector.match_replace(others[:, t, :], best_two[:, t, :], logits[:, t, :], 4.0).then_inc(others_done.sem, 1)
                dve.wait_ge(others_done.sem, others_done.after(b, 2))
                nc.vector.tensor_tensor(fallback[:, :, :], others[:, :, 0:N_ATTN], real, ALU.not_equal).then_inc(fallback_done.sem, 1)
                dve.wait_ge(fallback_done.sem, fallback_done.after(b, 1))
                dve.wait_ge(inactive_done.sem, inactive_done.after(b, 1))
                for t in range(2):
                    nc.vector.scalar_tensor_tensor(experts[:, t, :], fallback[:, t, :], inactive[:, t:t + 1], active[:, t, :],
                                                   ALU.mult, ALU.add).then_inc(experts_done.sem, 1)
                dve.wait_ge(experts_done.sem, experts_done.after(b, 2))
                dve.wait_ge(gated_done.sem, gated_done.after(b, 1))
                nc.vector.tensor_scalar(absent[:, :, :], experts[:, :, :], 1.0, 1e9, ALU.subtract, ALU.mult).then_inc(absent_done.sem, 1)
                nc.vector.tensor_tensor(gated_used[:, :, :], gated[:, :, :], experts[:, :, :], ALU.mult).then_inc(gated_used_done.sem, 1)
                dve.wait_ge(absent_done.sem, absent_done.after(b, 1))
                dve.wait_ge(gated_used_done.sem, gated_used_done.after(b, 1))
                nc.vector.tensor_tensor(masked_logits[:, :, :], absent[:, :, :], gated_used[:, :, :], ALU.add).then_inc(masked_logits_done.sem, 1)
                dve.wait_ge(masked_logits_done.sem, masked_logits_done.after(b, 1))
                nc.vector.tensor_reduce(neg_top[:, :], masked_logits[:, :, :], AX.X, ALU.max, negate=True).then_inc(neg_top_done.sem, 1)

            def mask_inputs(b, u, n):
                dve.wait_ge(mask_in_psum.sem, mask_in_psum.after(b, n + 1))
                if n == 0 and not (isinstance(b, int) and b < 2):
                    dve.wait_ge(v_in_psum.sem, v_in_psum.after(b - 1, 0))
                nc.vector.tensor_tensor(masked_u_t[u][:, 2 * n:2 * n + 2, :, :], route_bank[n % 2][:, :, :].unsqueeze(2).broadcast_to([P, 2, 2, S]),
                                        u_t[:, :, :].unsqueeze(1).broadcast_to([P, 2, 2, S]), ALU.mult).then_inc(masked_u_done.sem, 1)

            def route_weights(b, u):
                dve.wait_ge(route_exps_done.sem, route_exps_done.after(b, 2))
                nc.vector.reciprocal(route_recip[:, :], route_total[:, :]).then_inc(route_recip_done.sem, 1)
                dve.wait_ge(route_recip_done.sem, route_recip_done.after(b, 1))
                for t in range(2):
                    nc.vector.tensor_scalar(route_softmax[:, t, :], route_exps[:, t, :], route_recip[:, t:t + 1], None, ALU.mult)\
                        .then_inc(route_softmax_done.sem, 1)
                dve.wait_ge(route_softmax_done.sem, route_softmax_done.after(b, 2))
                nc.vector.tensor_tensor(weights[u][:, :, :], route_softmax[:, :, :], experts[:, :, :], ALU.mult).then_inc(weights_done.sem, 1)

            def score_maxima(b):
                dve.wait_ge(scores_in_psum.sem, scores_in_psum.after(b, 1))
                nc.vector.scalar_tensor_tensor(scores[:, :, :], attn_bank[:, :, :], P ** -0.5, causal[:, :, :], ALU.mult, ALU.add)\
                    .then_inc(scores_done.sem, 1)
                dve.wait_ge(scores_done.sem, scores_done.after(b, 1))
                for t, tiles in enumerate(TILES_OF):
                    nc.vector.tensor_reduce(neg_max[:, t:t + 1], scores[:, tiles, :], AX.XY, ALU.max, negate=True).then_inc(max_done.sem, 1)

            def probabilities(b):
                dve.wait_ge(exps_done.sem, exps_done.after(b, 2))
                nc.vector.reciprocal(recip[:, :], total[:, :]).then_inc(recip_done.sem, 1)
                dve.wait_ge(recip_done.sem, recip_done.after(b, 1))
                for t, tiles in enumerate(TILES_OF):
                    nc.vector.tensor_scalar(probs[:, tiles, :], exps[:, tiles, :], recip[:, t:t + 1], None, ALU.mult).then_inc(probs_done.sem, 1)

            def add_output(b, u, n):
                e, t = 2 * (n // 2), n % 2
                dve.wait_ge(out_in_psum.sem, out_in_psum.after(b, n + 1))
                for k in range(2):
                    if k == 1:
                        dve.wait_ge(acc_done.sem, acc_done.after(b, 2 * n + 1))
                    elif n >= 2:
                        dve.wait_ge(acc_done.sem, acc_done.after(b, 2 * (n - 1)))
                    xb = x[:, at(2 * b + t), :]
                    src = xb if n < 2 and k == 0 else acc[:, t, :]
                    dst = xb if n >= N_ATTN - 2 and k == 1 else acc[:, t, :]
                    nc.vector.scalar_tensor_tensor(dst, out_bank[n % 2][:, k, :], weights[u][:, t, e + k:e + k + 1], src,
                                                   ALU.mult, ALU.add).then_inc(acc_done.sem, 1)

            def front(b, u):
                moments(b)
                normalise(b)
                route(b)
                for n in range(N_ATTN // 2):
                    mask_inputs(b, u, n)
                route_weights(b, u)

            def batch(b, u, left=2):
                score_maxima(b)
                if left >= 2:
                    normalise(b + 2)
                probabilities(b)
                if left >= 2:
                    route(b + 2)
                for n in range(N_ATTN):
                    add_output(b, u, n)
                    if left >= 2 and n in (1, 3):
                        mask_inputs(b + 2, u, n - 1)
                        mask_inputs(b + 2, u, n)
                if left >= 2:
                    route_weights(b + 2, u)
                if left >= 3:
                    moments(b + 3)

            for done in (stats_done, moments_done, u_done):
                dve.sem_inc(done.sem, 2)
            dve.wait_ge(constants_done.sem, 2)
            dve.wait_ge(gate_done.sem, 1)
            nc.vector.tensor_scalar(gate[:, :], gate[:, :], 1.0, None, ALU.add).then_inc(gate_done.sem, 1)
            dve.wait_ge(sim_sq_in_psum.sem, 1)
            nc.vector.tensor_scalar(sim_norm[:, :], logits_bank[:, 0, 0:N_ATTN], NORM_EPS ** 2, None, ALU.max).then_inc(sim_norm_sq_done.sem, 1)
            dve.wait_ge(gate_done.sem, 2)
            nc.vector.reciprocal(gate[:, :], gate[:, :]).then_inc(gate_done.sem, 1)
            dve.wait_ge(gate_done.sem, 3)
            route(0)
            for n in range(N_ATTN // 2):
                mask_inputs(0, 0, n)
            route_weights(0, 0)
            front(1, 1)
            moments(2)
            with dve.Fori(0, (B - 4) // 2) as pair:
                for u in range(2):
                    batch(pair * 2 + u, u, 3)
            for b in range(B - 4, B):
                batch(b, b % 2, min(3, B - 1 - b))


LEAST = float(np.finfo(np.float32).min)


def decoder(nc, w, out, first=1, last=6):
    with ExitStack() as ctx:
        def sb(n, shape, dt=fp32):
            return ctx.enter_context(nc.sbuf_tensor(n, shape, dt))

        class Shared:
            pass

        shared = Shared()
        shared.x = sb("x_res", [P, T, C])
        shared.xn = sb("xn", [P, 2, C])
        stats = sb("stats", [P, 2, 6])
        mean_var = sb("mean_var", [P, 2, 2])
        var_eps = sb("var_eps", [P, 2])
        rstd = sb("rstd", [P, 2])
        shared.ident = sb("ident", [P, P])
        shared.ident_bf = sb("ident_bf", [P, P], bf16)
        shared.neg_half = sb("neg_half", [P, 64])
        shared.rms_eps = sb("rms_eps", [P, 1])
        shared.ln_eps = sb("ln_eps", [P, 1])
        shared.bias_row = sb("bias_row", [P, 1])
        x0 = dict(wq=sb("x0_wq", [P, 2, C]), wkv=sb("x0_wkv", [P, 2, 2 * C]), wo=sb("x0_wo", [P, 4, C]),
                  gain=sb("x0_gain", [P, 3, DH]), offset=sb("x0_offset", [P, 3, DH]))
        big = sb("big", [P, 2 * (N_ROUTED + 1) * C])
        f0_wr = big[:, 0:2 * N_ROUTED * C].rearrange("p (a e c) -> p a e c", a=2, e=N_ROUTED)
        f0_ws = big[:, 2 * N_ROUTED * C:].rearrange("p (a c) -> p a c", a=2)
        ws_pair = sb("f0_ws_pair", [P, 2, 2, C])
        f0 = dict(centroids=sb("f0_centroids", [P, 2, N_ROUTED]), bias=sb("f0_bias", [P, N_ROUTED]),
                  wr=f0_wr, ws=f0_ws, wb=sb("f0_wb", [N_ROUTED + 2, C]))
        size = 2 * N_ATTN * P
        f1_wq, f1_wk, f1_wv = (big[:, n * size:(n + 1) * size].rearrange("p (a e d) -> p a e d", a=2, e=N_ATTN) for n in range(3))
        f1_wo = big[:, 3 * size:3 * size + N_ATTN * C].rearrange("p (e c) -> p e c", e=N_ATTN)
        f1 = dict(sim=sb("f1_sim", [P, 2, N_ATTN]), gate=sb("f1_gate", [P, N_ATTN]), wq=f1_wq, wk=f1_wk, wv=f1_wv, wo=f1_wo,
                  causal=sb("f1_causal", [P, 3, P]))
        ones = shared.ones = sb("ones", [P, P])
        x1 = dict(wq=sb("x1_wq", [P, 2, C]), wkv=sb("x1_wkv", [P, 2, 2 * C]), wo=sb("x1_wo", [P, 4, C]),
                  bqkv=sb("x1_bqkv", [P, 3 * C]), mask=sb("x1_mask", [P, 2, SK]))
        a0 = dict(wqkv=sb("a0_wqkv", [P, 2, 3 * C]), bqkv=sb("a0_bqkv", [P, 3 * C]), wo=sb("a0_wo", [P, 4, C]))
        a1 = dict(wqkv=sb("a1_wqkv", [P, 2, 3 * C]), bqkv=sb("a1_bqkv", [P, 3 * C]), wo=sb("a1_wo", [P, 4, C]))
        gain = sb("a0_gain", [P, 2, DH])
        qk_gain = sb("a0_qk_gain", [P, DH])
        head_mask = sb("a1_head_mask", [P, 4])

        prepared = nc.alloc_semaphore("prepared")
        moments_done, var_done, rstd_done, xn_done = (
            nc.alloc_semaphore(n) for n in ("moments_done", "var_done", "rstd_done", "xn_done"))
        routed_ready = nc.alloc_semaphore("routed_ready")
        masks_done = nc.alloc_semaphore("masks_done")

        loads = {
            "first": [(shared.x[:, 0:4, :], w["x"][0:2].rearrange("b (t p) c -> p (b t) c", p=P))],
            "a0": [
                (a0["wqkv"][:, :, :], w["a0_wqkv"]),
                (a0["bqkv"][:, :], w["a0_bqkv"].partition_broadcast(P)),
                (gain[:, :, :], w["a0_gain"].partition_broadcast(P)),
                (shared.bias_row[:, :], w["bias_row"]),
            ],
            "a0_late": [
                (shared.x[:, 4:T, :], w["x"][2:B].rearrange("b (t p) c -> p (b t) c", p=P)),
                (a0["wo"][:, :, :], w["a0_wo"]),
            ],
            "x0": [
                (x0["wq"][:, :, :], w["x0_wq"]),
                (x0["wkv"][:, :, :], w["x0_wkv"]),
                (x0["wo"][:, :, :], w["x0_wo"]),
                (x0["gain"][:, :, :], w["x0_gain"].partition_broadcast(P)),
                (x0["offset"][:, :, :], w["x0_offset"].partition_broadcast(P)),
            ],
            "f0": [
                (f0_wr, w["f0_wr"]),
                (ws_pair[:, :, :, :], w["f0_ws"]),
                (f0["centroids"][:, :, :], w["f0_centroids"]),
                (f0["bias"][:, :], w["f0_bias"].partition_broadcast(P)),
                (f0["wb"][:, :], w["f0_wb"]),
            ],
            "rest": [
                (a1["wqkv"][:, :, :], w["a1_wqkv"]),
                (a1["bqkv"][:, :], w["a1_bqkv"].partition_broadcast(P)),
                (a1["wo"][:, :, :], w["a1_wo"]),
                (head_mask[:, :], w["a1_head_mask"]),
                (x1["wq"][:, :, :], w["x1_wq"]),
                (x1["wkv"][:, :, :], w["x1_wkv"]),
                (x1["wo"][:, :, :], w["x1_wo"]),
                (x1["bqkv"][:, :], w["x1_bqkv"].partition_broadcast(P)),
                (x1["mask"][:, :, :], w["x1_mask"].rearrange("(t p) s -> p t s", p=P)),
                (f1["sim"][:, :, :], w["f1_sim"]),
                (f1["gate"][:, :], w["f1_gates"].partition_broadcast(P)),
            ],
            "f1": [(dst, w[src]) for dst, src in zip((f1_wq, f1_wk, f1_wv, f1_wo), ("f1_wq", "f1_wk", "f1_wv", "f1_wo"))],
        }
        loaded = {layer: nc.alloc_semaphore(f"loaded_{layer}") for layer in loads}

        def start_loads(sp, *layers):
            for layer in layers:
                for dst, src in loads[layer]:
                    sp.dma_start(dst, src).then_inc(loaded[layer], 16)

        def wait_loaded(engine, layer):
            engine.wait_ge(loaded[layer], 16 * len(loads[layer]))

        with nc.Block() as block:
            @block.sync
            def _(sp):
                start_loads(sp, "first", "a0", "a0_late")
                wait_loaded(sp, "a0")

            @block.gpsimd
            def _(pool):
                nc.gpsimd.memset(shared.ln_eps[:, :], LN_EPS).then_inc(prepared, 1)
                nc.gpsimd.memset(shared.ident[:, :], 0.0).then_inc(prepared, 1)
                nc.gpsimd.memset(shared.neg_half[:, :], -0.5).then_inc(prepared, 1)
                nc.gpsimd.memset(shared.rms_eps[:, :], RMS_EPS).then_inc(prepared, 1)
                pool.wait_ge(prepared, 4)
                nc.gpsimd.affine_select(out=shared.ident[:, :], in_=shared.ident[:, :], compare_op=ALU.not_equal, fill=1.0,
                                        base=0, pattern=[[-1, P]], channel_multiplier=1).then_inc(prepared, 1)
                pool.wait_ge(prepared, 5)
                nc.gpsimd.tensor_copy(shared.ident_bf[:, :], shared.ident[:, :]).then_inc(prepared, 1)
                nc.gpsimd.memset(f1["causal"][:, :, :], 0.0).then_inc(prepared, 1)
                nc.gpsimd.memset(ones[:, :], 1.0).then_inc(prepared, 1)
                for n, tile in enumerate((0, 2)):
                    pool.wait_ge(prepared, 8 + n)
                    nc.gpsimd.affine_select(out=f1["causal"][:, tile, :], in_=f1["causal"][:, tile, :], compare_op=ALU.is_ge,
                                            fill=LEAST, base=0, pattern=[[-1, P]], channel_multiplier=1).then_inc(prepared, 1)
                pool.wait_ge(prepared, 10)
                pool.wait_ge(moments_done, 4)
                nc.gpsimd.tensor_scalar(var_eps[:, :], mean_var[:, :, 1], LN_EPS, None, ALU.add).then_inc(var_done, 1)
                pool.wait_ge(var_done, 1)
                nc.gpsimd.tensor_tensor(rstd[:, :], var_eps[:, :], shared.neg_half[:, 0:2], ALU.pow).then_inc(rstd_done, 1)
                pool.wait_ge(rstd_done, 1)
                wait_loaded(pool, "a0")
                nc.gpsimd.tensor_tensor(qk_gain[:, :], gain[:, 0], gain[:, 1], ALU.mult).then_inc(prepared, 1)
                pool.wait_ge(prepared, 11)

            @block.vector
            def _(dve):
                wait_loaded(dve, "first")
                for t in range(2):
                    nc.vector.bn_stats(stats[:, t], shared.x[:, t, :]).then_inc(moments_done, 1)
                for t in range(2):
                    dve.wait_ge(moments_done, t + 1)
                    nc.vector.bn_aggr(mean_var[:, t], stats[:, t]).then_inc(moments_done, 1)
                dve.wait_ge(moments_done, 4)
                dve.wait_ge(rstd_done, 1)
                for t in range(2):
                    nc.vector.tensor_scalar(shared.xn[:, t], shared.x[:, t, :], mean_var[:, t, 0:1], rstd[:, t:t + 1],
                                            ALU.subtract, ALU.mult).then_inc(xn_done, 1)
                dve.wait_ge(xn_done, 2)

            @block.scalar
            def _(act):
                nc.scalar.preload_act_table_set(LN_EXP_TABLES)

        def prepare_routed(pool):
            wait_loaded(pool, "f0")
            nc.gpsimd.tensor_tensor(f0_ws, ws_pair[:, :, 0, :], ws_pair[:, :, 1, :], ALU.add).then_inc(routed_ready, 1)
            pool.wait_ge(routed_ready, 1)
            nc.gpsimd.tensor_scalar(f0_ws, f0_ws, 0.5, None, ALU.mult).then_inc(routed_ready, 1)
            pool.wait_ge(routed_ready, 2)

        def prepare_masks(pool):
            wait_loaded(pool, "rest")
            nc.gpsimd.tensor_tensor(a1["wo"][:, :, :], a1["wo"][:, :, :], head_mask[:, :].unsqueeze(2).broadcast_to([P, 4, C]), ALU.mult)\
                .then_inc(masks_done, 1)
            nc.gpsimd.tensor_scalar(x1["mask"][:, :, :], x1["mask"][:, :, :], -1e9, None, ALU.mult).then_inc(masks_done, 1)
            pool.wait_ge(masks_done, 2)

        if first <= 1 <= last:
            self_attention(nc, shared, "a0", qk_gain=qk_gain, wait_late=lambda engine: wait_loaded(engine, "a0_late"),
                           start_others=lambda sp: start_loads(sp, "x0", "f0", "rest"), at_end=prepare_routed, **a0)
        if first <= 2 <= last:
            with nc.Block() as block:
                @block.sync
                def _(sp):
                    wait_loaded(sp, "x0")
            cross_attention(nc, shared, "x0", w["ctx"], at_end=prepare_masks, **x0)
        if first <= 3 <= last:
            with nc.Block() as block:
                @block.sync
                def _(sp):
                    wait_loaded(sp, "f0")

                @block.scalar
                def _(act):
                    nc.scalar.preload_act_table_set(LN_EXP_TABLES)
            shared_and_routed_experts(nc, shared, "f0", **f0)
        if first <= 4 <= last:
            self_attention(nc, shared, "a1", qk_gain=None, start_others=lambda sp: start_loads(sp, "f1"), **a1)
        if first <= 5 <= last:
            cross_attention(nc, shared, "x1", w["ctx"], **x1)
        with nc.Block() as block:
            @block.sync
            def _(sp):
                wait_loaded(sp, "f1")
        if first <= 6 <= last:
            attention_of_experts(nc, shared, "f1", **f1)
        stored = nc.alloc_semaphore("stored")
        with nc.Block() as block:
            @block.sync
            def _(sp):
                sp.dma_start(out.rearrange("b (t p) c -> p (b t) c", p=P), shared.x[:, :, :]).then_inc(stored, 16)
                sp.wait_ge(stored, 16)
                for layer in loads:
                    wait_loaded(sp, layer)


def laid_out(inputs):
    f = {k: np.asarray(v) for k, v in inputs.items()}

    def rows(w):
        return np.ascontiguousarray(w.reshape(-1, P, w.shape[1]).transpose(1, 0, 2))

    def per_head(w, bias):
        o = np.zeros((4, 2 * DH, 4, w.shape[0]), w.dtype)
        o[:, 0:DH] = w.T.reshape(4, 4, DH, w.shape[0]).transpose(1, 2, 0, 3)
        if bias is not None:
            o[0, DH, 0] = bias
        return o.reshape(P, 4, w.shape[0])

    mask = np.ones((4, 2 * DH, 4), f["L1_attn_head_mask"].dtype)
    mask[:, 0:DH] = f["L1_attn_head_mask"].reshape(4, 4).T[:, None, :]
    a = {
        "x": f["x"],
        "a0_wqkv": rows(f["L0_attn_w_qkv"].T),
        "a0_bqkv": f["L0_attn_b_qkv"],
        "a0_wo": per_head(f["L0_attn_w_proj"], f["L0_attn_b_proj"]),
        "a0_gain": np.stack([f["L0_attn_qn_w"], f["L0_attn_kn_w"]]),
        "a1_wqkv": rows(np.concatenate([f["L1_attn_Wq"], f["L1_attn_Wk"], f["L1_attn_Wv"]]).T),
        "a1_bqkv": np.concatenate([f["L1_attn_bq"], f["L1_attn_bk"], f["L1_attn_bv"]]),
        "a1_wo": per_head(f["L1_attn_Wo"], f["L1_attn_bo"]),
        "a1_head_mask": mask.reshape(P, 4),
        "bias_row": (np.arange(P) == DH).astype(np.float32).reshape(P, 1),
        "ctx": np.ascontiguousarray(f["ctx_1024"].reshape(B, SK, 2, P).transpose(3, 0, 2, 1)),
        "f0_wr": np.ascontiguousarray(f["L0_ffn_Wr"].reshape(N_ROUTED, C, 2, P).transpose(3, 2, 0, 1)),
        "f0_ws": np.ascontiguousarray(f["L0_ffn_Ws"].reshape(2, C, 2, P).transpose(3, 2, 0, 1)),
        "f0_centroids": rows(f["L0_ffn_centroids"].T),
        "f0_bias": f["L0_ffn_expert_biases"],
        "f0_wb": np.concatenate([f["L0_ffn_br"], f["L0_ffn_bs"]]),
        "f1_sim": rows(f["L1_ffn_sim_matrix"]),
        "f1_gates": f["L1_ffn_gates"],
        "f1_wo": np.ascontiguousarray(f["L1_ffn_o_proj"].transpose(1, 0, 2)),
        "x0_wq": rows(f["L0_xattn_Wq"].T),
        "x0_wkv": rows(np.concatenate([f["L0_xattn_Wk"], f["L0_xattn_Wv"]]).T),
        "x0_wo": per_head(f["L0_xattn_Wo"], f["L0_xattn_bo"]),
        "x0_gain": np.stack([f["L0_xattn_gq"], f["L0_xattn_gq"], f["L0_xattn_gk"]]),
        "x0_offset": np.stack([f["L0_xattn_bq"], f["L0_xattn_bq"], f["L0_xattn_bk"]]),
        "x1_wq": rows(f["L1_xattn_wq_w"].T),
        "x1_wkv": rows(np.concatenate([f["L1_xattn_wk_w"], f["L1_xattn_wv_w"]]).T),
        "x1_wo": per_head(f["L1_xattn_dense_w"], f["L1_xattn_dense_b"]),
        "x1_bqkv": np.concatenate([f["L1_xattn_wq_b"], f["L1_xattn_wk_b"], f["L1_xattn_wv_b"]]),
        "x1_mask": f["mask_1x1xSxS2_fk1"].reshape(S, SK),
    }
    for n in "qkv":
        a[f"f1_w{n}"] = np.ascontiguousarray(f[f"L1_ffn_{n}_proj"].reshape(N_ATTN, 2, P, P).transpose(2, 1, 0, 3))
    return a


def kernel(**inputs):
    import concourse.bacc as bacc
    from concourse.bass_utils import run_bass_kernel_spmd

    arrays = laid_out(inputs)
    nc = bacc.Bacc("TRN2", target_bir_lowering=False, num_devices=1)
    w = {n: nc.dram_tensor(f"in_{n}", a.shape, mybir.dt.from_np(a.dtype), kind="ExternalInput").ap() for n, a in arrays.items()}
    out = nc.dram_tensor("out_x", (B, S, C), fp32, kind="ExternalOutput").ap()
    decoder(nc, w, out)
    r = run_bass_kernel_spmd(nc, [{f"in_{n}": a for n, a in arrays.items()}], core_ids=[0])
    return r.results[0]["out_x"]
```
